# Optimizing a Trainium2 kernel written in Bass

```python
import numpy as np
import jax
import jax.numpy as jnp

def _softmax(x, axis=-1):
    return jax.nn.softmax(x, axis=axis)

def _gelu(x):
    return jax.nn.gelu(x, approximate=True)

def _silu(x):
    return jax.nn.silu(x)

def _sigmoid(x):
    return jax.nn.sigmoid(x)

def _layernorm(x, axis=-1, eps=1e-05):
    m = jnp.mean(x, axis=axis, keepdims=True)
    v = jnp.var(x, axis=axis, keepdims=True)
    return (x - m) / jnp.sqrt(v + eps)

def _scatter_add(tgt, idx, src, axis=0):
    return tgt.at[idx].add(src)

def _segment_sum(src, seg, n):
    return jax.ops.segment_sum(src, seg, n)
kernel_name = 'mk_xattn_seq_d2_seqx_r4_dbb4ce'

def setup_inputs(seed: int=0):
    np.random.seed(seed)
    _w = jnp.asarray

    def _rec_inputs():
        import jax
        import jax.numpy as jnp
        _rk = jax.random.key(seed)
        x = 7.22e-05 + 1 * jax.random.normal(jax.random.fold_in(_rk, 1), (16, 100, 512), jnp.float32)
        _lenS = 100 - jax.random.randint(jax.random.fold_in(_rk, 7), (16,), 0, max(1, 100 // 4) + 1, jnp.int32)
        _lenS2 = 361 - jax.random.randint(jax.random.fold_in(_rk, 8), (16,), 0, max(1, 361 // 4) + 1, jnp.int32)
        _ctx_1024P = jax.random.normal(jax.random.fold_in(_rk, 11), (16, 16, 256), jnp.float32)
        _ctx_1024c = jax.random.dirichlet(jax.random.fold_in(_rk, 511), 0.3 * jnp.ones((16,), jnp.float32), (16, 361))
        _ctx_1024t = jnp.einsum('bsk,bkd->bsd', _ctx_1024c, _ctx_1024P)
        _ctx_1024t = _ctx_1024t * jax.lax.rsqrt(jnp.mean(jnp.square(_ctx_1024t)) + 1e-12) * 0.953939
        ctx_1024 = -0.000514642 + 1.00011 * (_ctx_1024t + 0.3 * jax.random.normal(jax.random.fold_in(_rk, 611), (16, 361, 256), jnp.float32))
        pos_1xS = jnp.broadcast_to(jnp.arange(100, dtype=jnp.int32), (1, 100))
        _validS = jnp.arange(100)[None, :] < _lenS[:, None]
        _validS2 = jnp.arange(361)[None, :] < _lenS2[:, None]
        _causal = jnp.tril(jnp.ones((100, 100), dtype=bool))
        mask_BxS_ik0 = jnp.where(jnp.broadcast_to(_validS[:, :], (16, 100)), 0, 1).astype(jnp.int32)
        return (x, ctx_1024, pos_1xS, mask_BxS_ik0)
    x, ctx_1024, pos_1xS, mask_BxS_ik0 = _rec_inputs()

    def _L0_xattn_setup():
        import jax, jax.numpy as jnp
        import numpy as np
        H = 512
        NH = 16
        HD = H // NH
        CH = 256
        CC = 256
        CHD = CC // NH
        I = 1376
        B = 2
        L = 512
        LE = 256
        EPS = 1e-06

        def rms_norm(x, w):
            xf = x.astype(jnp.float32)
            var = jnp.mean(xf * xf, axis=-1, keepdims=True)
            return (w * (xf * jax.lax.rsqrt(var + EPS))).astype(x.dtype)

        def expert_mask(tt):
            vm = jnp.zeros(tt.shape, dtype=bool)
            vm = vm.at[:, :-1].set((tt[:, :-1] == 1) & (tt[:, 1:] == 1))
            return vm

        def rotate_half(x):
            d = x.shape[-1] // 2
            return jnp.concatenate([-x[..., d:], x[..., :d]], axis=-1)

        def apply_rotary(q, k, position_ids, seq_len):
            inv = 1.0 / 10000.0 ** (jnp.arange(0, HD, 2, dtype=jnp.float32) / HD)
            t = jnp.arange(seq_len, dtype=jnp.float32)
            freqs = jnp.outer(t, inv)
            emb = jnp.concatenate([freqs, freqs], axis=-1)
            cos = jnp.cos(emb)[position_ids][:, None].astype(q.dtype)
            sin = jnp.sin(emb)[position_ids][:, None].astype(q.dtype)
            return (q * cos + rotate_half(q) * sin, k * cos + rotate_half(k) * sin)

        def sdpa(q, k, v, causal):
            scale = 1.0 / np.sqrt(q.shape[-1])
            scores = jnp.einsum('bhqd,bhkd->bhqk', q * scale, k)
            if causal:
                mask = jnp.tril(jnp.ones((q.shape[-2], k.shape[-2]), dtype=bool))
                scores = jnp.where(mask, scores, jnp.finfo(jnp.float32).min)
            p = jax.nn.softmax(scores.astype(jnp.float32), axis=-1).astype(q.dtype)
            return jnp.einsum('bhqk,bhkd->bhqd', p, v)

        def heads(x, nh, hd):
            b, l, _ = x.shape
            return x.reshape(b, l, nh, hd).transpose(0, 2, 1, 3)
        key = jax.random.key(seed)
        ks = jax.random.split(key, 20)
        s = 0.02
        f32 = jnp.float32
        return {'hidden_states': jax.random.normal(ks[0], (B, L, H), f32), 'encoder_outputs': jax.random.normal(ks[1], (B, LE, CH), f32), 'token_type_ids': jax.random.randint(ks[2], (B, L), 0, 2, jnp.int32), 'position_ids': jnp.arange(L, dtype=jnp.int32)[None, :], 'ln_in_w': jnp.ones((H,), f32), 'ln_post_attn_w': jnp.ones((H,), f32), 'ln_post_cross_w': jnp.ones((H,), f32), 'v_qkv': jax.random.normal(ks[3], (H, 3 * H), f32) * s, 'l_qkv': jax.random.normal(ks[4], (H, 3 * H), f32) * s, 'v_dense': jax.random.normal(ks[5], (H, H), f32) * s, 'l_dense': jax.random.normal(ks[6], (H, H), f32) * s, 'cq_w': jax.random.normal(ks[7], (H, CC), f32) * s, 'ckv_w': jax.random.normal(ks[8], (CH, 2 * CC), f32) * s, 'cdense_w': jax.random.normal(ks[9], (CC, H), f32) * s, 'v_gate': jax.random.normal(ks[10], (H, I), f32) * s, 'v_up': jax.random.normal(ks[11], (H, I), f32) * s, 'v_down': jax.random.normal(ks[12], (I, H), f32) * s, 'l_gate': jax.random.normal(ks[13], (H, I), f32) * s, 'l_up': jax.random.normal(ks[14], (H, I), f32) * s, 'l_down': jax.random.normal(ks[15], (I, H), f32) * s}
    _L0_xattn_all = _L0_xattn_setup()
    _L0_xattn_in = {k: v for k, v in _L0_xattn_all.items() if k in ('ln_in_w', 'ln_post_attn_w', 'ln_post_cross_w', 'v_qkv', 'l_qkv', 'v_dense', 'l_dense', 'cq_w', 'ckv_w', 'cdense_w', 'v_gate', 'v_up', 'v_down', 'l_gate', 'l_up', 'l_down')}
    del _L0_xattn_all

    def _L1_xattn_setup():
        import jax, jax.numpy as jnp
        import numpy as np
        EPS = 1e-06

        def _rmsnorm(x, w):
            var = jnp.mean(jnp.square(x), axis=-1, keepdims=True)
            return x * jax.lax.rsqrt(var + EPS) * w
        key = jax.random.key(seed)
        ks = jax.random.split(key, 6)
        B, N, M = (4, 1024, 512)
        d_model, memory_dim = (512, 256)
        hidden_states = jax.random.normal(ks[0], (B, N, d_model), dtype=jnp.float32)
        memory = jax.random.normal(ks[1], (B, M, memory_dim), dtype=jnp.float32)
        W_mem = jax.random.normal(ks[2], (d_model, memory_dim), dtype=jnp.float32) / np.sqrt(memory_dim)
        W_gate = jax.random.normal(ks[3], (d_model, 2 * d_model), dtype=jnp.float32) / np.sqrt(2 * d_model)
        b_gate = jax.random.normal(ks[4], (d_model,), dtype=jnp.float32) * 0.01
        norm_w = jnp.ones((d_model,), dtype=jnp.float32)
        return {'hidden_states': hidden_states, 'memory': memory, 'W_mem': W_mem, 'W_gate': W_gate, 'b_gate': b_gate, 'norm_w': norm_w}
    _L1_xattn_all = _L1_xattn_setup()
    _L1_xattn_in = {k: v for k, v in _L1_xattn_all.items() if k in ('W_mem', 'W_gate', 'b_gate', 'norm_w')}
    del _L1_xattn_all
    return {'x': x, 'ctx_1024': ctx_1024, 'pos_1xS': pos_1xS, 'mask_BxS_ik0': mask_BxS_ik0, 'L0_xattn_ln_in_w': _L0_xattn_in['ln_in_w'], 'L0_xattn_ln_post_attn_w': _L0_xattn_in['ln_post_attn_w'], 'L0_xattn_ln_post_cross_w': _L0_xattn_in['ln_post_cross_w'], 'L0_xattn_v_qkv': _L0_xattn_in['v_qkv'], 'L0_xattn_l_qkv': _L0_xattn_in['l_qkv'], 'L0_xattn_v_dense': _L0_xattn_in['v_dense'], 'L0_xattn_l_dense': _L0_xattn_in['l_dense'], 'L0_xattn_cq_w': _L0_xattn_in['cq_w'], 'L0_xattn_ckv_w': _L0_xattn_in['ckv_w'], 'L0_xattn_cdense_w': _L0_xattn_in['cdense_w'], 'L0_xattn_v_gate': _L0_xattn_in['v_gate'], 'L0_xattn_v_up': _L0_xattn_in['v_up'], 'L0_xattn_v_down': _L0_xattn_in['v_down'], 'L0_xattn_l_gate': _L0_xattn_in['l_gate'], 'L0_xattn_l_up': _L0_xattn_in['l_up'], 'L0_xattn_l_down': _L0_xattn_in['l_down'], 'L1_xattn_W_mem': _L1_xattn_in['W_mem'], 'L1_xattn_W_gate': _L1_xattn_in['W_gate'], 'L1_xattn_b_gate': _L1_xattn_in['b_gate'], 'L1_xattn_norm_w': _L1_xattn_in['norm_w']}

def reference(x, ctx_1024, pos_1xS, mask_BxS_ik0, L0_xattn_ln_in_w, L0_xattn_ln_post_attn_w, L0_xattn_ln_post_cross_w, L0_xattn_v_qkv, L0_xattn_l_qkv, L0_xattn_v_dense, L0_xattn_l_dense, L0_xattn_cq_w, L0_xattn_ckv_w, L0_xattn_cdense_w, L0_xattn_v_gate, L0_xattn_v_up, L0_xattn_v_down, L0_xattn_l_gate, L0_xattn_l_up, L0_xattn_l_down, L1_xattn_W_mem, L1_xattn_W_gate, L1_xattn_b_gate, L1_xattn_norm_w):
    import jax
    import jax.numpy as jnp

    def _L0_xattn_ref(hidden_states, encoder_outputs, token_type_ids, position_ids, ln_in_w, ln_post_attn_w, ln_post_cross_w, v_qkv, l_qkv, v_dense, l_dense, cq_w, ckv_w, cdense_w, v_gate, v_up, v_down, l_gate, l_up, l_down):
        import jax, jax.numpy as jnp
        import numpy as np
        H = 512
        NH = 16
        HD = H // NH
        CH = 256
        CC = 256
        CHD = CC // NH
        I = 1376
        B = 2
        L = 512
        LE = 256
        EPS = 1e-06

        def rms_norm(x, w):
            xf = x.astype(jnp.float32)
            var = jnp.mean(xf * xf, axis=-1, keepdims=True)
            return (w * (xf * jax.lax.rsqrt(var + EPS))).astype(x.dtype)

        def expert_mask(tt):
            vm = jnp.zeros(tt.shape, dtype=bool)
            vm = vm.at[:, :-1].set((tt[:, :-1] == 1) & (tt[:, 1:] == 1))
            return vm

        def rotate_half(x):
            d = x.shape[-1] // 2
            return jnp.concatenate([-x[..., d:], x[..., :d]], axis=-1)

        def apply_rotary(q, k, position_ids, seq_len):
            inv = 1.0 / 10000.0 ** (jnp.arange(0, HD, 2, dtype=jnp.float32) / HD)
            t = jnp.arange(seq_len, dtype=jnp.float32)
            freqs = jnp.outer(t, inv)
            emb = jnp.concatenate([freqs, freqs], axis=-1)
            cos = jnp.cos(emb)[position_ids][:, None].astype(q.dtype)
            sin = jnp.sin(emb)[position_ids][:, None].astype(q.dtype)
            return (q * cos + rotate_half(q) * sin, k * cos + rotate_half(k) * sin)

        def sdpa(q, k, v, causal):
            scale = 1.0 / np.sqrt(q.shape[-1])
            scores = jnp.einsum('bhqd,bhkd->bhqk', q * scale, k)
            if causal:
                mask = jnp.tril(jnp.ones((q.shape[-2], k.shape[-2]), dtype=bool))
                scores = jnp.where(mask, scores, jnp.finfo(jnp.float32).min)
            p = jax.nn.softmax(scores.astype(jnp.float32), axis=-1).astype(q.dtype)
            return jnp.einsum('bhqk,bhkd->bhqd', p, v)

        def heads(x, nh, hd):
            b, l, _ = x.shape
            return x.reshape(b, l, nh, hd).transpose(0, 2, 1, 3)
        b, l, _ = hidden_states.shape
        vm = expert_mask(token_type_ids)[..., None]
        residual = hidden_states
        x = rms_norm(hidden_states, ln_in_w)
        mixed = jnp.where(vm, x @ v_qkv, x @ l_qkv)
        q, k, v = jnp.split(mixed, 3, axis=-1)
        q, k, v = (heads(q, NH, HD), heads(k, NH, HD), heads(v, NH, HD))
        q, k = apply_rotary(q, k, position_ids, l)
        ctx = sdpa(q, k, v, causal=True)
        ctx = ctx.transpose(0, 2, 1, 3).reshape(b, l, H)
        attn_out = jnp.where(vm, ctx @ v_dense, ctx @ l_dense)
        hidden_states = residual + attn_out
        ci = rms_norm(hidden_states, ln_post_cross_w)
        cq = heads(ci @ cq_w, NH, CHD)
        ckv = encoder_outputs @ ckv_w
        ck, cv = jnp.split(ckv, 2, axis=-1)
        ck, cv = (heads(ck, NH, CHD), heads(cv, NH, CHD))
        cctx = sdpa(cq, ck, cv, causal=False)
        cctx = cctx.transpose(0, 2, 1, 3).reshape(b, l, CC)
        hidden_states = hidden_states + cctx @ cdense_w
        mi = rms_norm(hidden_states, ln_post_attn_w)
        v_out = jax.nn.silu(mi @ v_gate) * (mi @ v_up) @ v_down
        l_out = jax.nn.silu(mi @ l_gate) * (mi @ l_up) @ l_down
        hidden_states = hidden_states + jnp.where(vm, v_out, l_out)
        return hidden_states

    def _L1_xattn_ref(hidden_states, memory, W_mem, W_gate, b_gate, norm_w):
        import jax, jax.numpy as jnp
        import numpy as np
        EPS = 1e-06

        def _rmsnorm(x, w):
            var = jnp.mean(jnp.square(x), axis=-1, keepdims=True)
            return x * jax.lax.rsqrt(var + EPS) * w
        D = hidden_states.shape[-1]
        memory_proj = jnp.einsum('bme,de->bmd', memory, W_mem)
        scores = jnp.einsum('bnd,bmd->bnm', hidden_states, memory_proj) / jnp.sqrt(jnp.float32(D))
        attn = jax.nn.softmax(scores, axis=-1)
        memory_context = jnp.einsum('bnm,bmd->bnd', attn, memory_proj)
        gate_input = jnp.concatenate([hidden_states, memory_context], axis=-1)
        gate = jax.nn.sigmoid(jnp.einsum('bnf,df->bnd', gate_input, W_gate) + b_gate)
        fused = hidden_states + gate * memory_context
        return _rmsnorm(fused, norm_w)
    x = _L0_xattn_ref(x, ctx_1024, mask_BxS_ik0, pos_1xS, L0_xattn_ln_in_w, L0_xattn_ln_post_attn_w, L0_xattn_ln_post_cross_w, L0_xattn_v_qkv, L0_xattn_l_qkv, L0_xattn_v_dense, L0_xattn_l_dense, L0_xattn_cq_w, L0_xattn_ckv_w, L0_xattn_cdense_w, L0_xattn_v_gate, L0_xattn_v_up, L0_xattn_v_down, L0_xattn_l_gate, L0_xattn_l_up, L0_xattn_l_down)
    x = _L1_xattn_ref(x, ctx_1024, L1_xattn_W_mem, L1_xattn_W_gate, L1_xattn_b_gate, L1_xattn_norm_w)
    return x

_drawn_inputs = setup_inputs


def setup_inputs(seed=0):
    import zlib

    import numpy as np

    out = dict(_drawn_inputs(seed))
    spreads = {'L0_xattn_ln_in_w': (1.0, 0.6),
     'L0_xattn_ln_post_attn_w': (1.0, 0.6),
     'L0_xattn_ln_post_cross_w': (1.0, 0.6),
     'L1_xattn_norm_w': (1.0, 0.2)}
    factors = {'L0_xattn_v_qkv': 8.0,
     'L0_xattn_v_dense': 7.352,
     'L0_xattn_cq_w': 8.0,
     'L1_xattn_b_gate': 55.704,
     'L0_xattn_v_gate': 8.0,
     'L0_xattn_v_up': 8.0,
     'L0_xattn_v_down': 8.0}
    for name, (base, spread) in spreads.items():
        noise = np.random.default_rng([zlib.crc32(name.encode()), seed]).standard_normal(out[name].shape)
        drawn = base * np.exp(spread * noise) if base else spread * noise
        out[name] = jnp.asarray(drawn.astype(out[name].dtype))
    for name, factor in factors.items():
        out[name] = (out[name] * factor).astype(out[name].dtype)
    return out
```

```python
from contextlib import ExitStack

import numpy as np

import concourse.bass as bass
from concourse import mybir

F32 = mybir.dt.float32
F32R = mybir.dt.float32r
BF16 = mybir.dt.bfloat16
I32 = mybir.dt.int32
ALU = mybir.AluOpType
ACT = mybir.ActivationFunctionType
AX_X = mybir.AxisListType.X

B, S, H = 16, 100, 512
N = B * S
P = 128
KT = H // P
NH, HD = 16, 32
CC, CHD = 256, 16
M = 361
MK, MT = 121, 3
IT = 11
G = 400
NG = N // G
GP = G // B
EPS = 1e-6
FREE = 1

C_ID, C_ONE, C_M4, C_M8, C_COS, C_SIN, C_IDX, C_ROW, C_EPS, C_ZERO, C_SCALE, C_END = 0, 128, 256, 260, 268, 396, 524, 525, 528, 529, 657, 658
W_IN, W_CROSS, W_ATTN, W_OUT, W_BIAS = 0, 4, 8, 12, 16


def shape_constants():
    c = np.zeros((P, C_END), np.float32)
    c[:, C_ID:C_ID + P] = np.eye(P)
    c[:, C_ONE:C_ONE + P] = 1.0
    p = np.arange(P)
    for j in range(4):
        c[:, C_M4 + j] = (p // HD == j) * np.float32(1.0 / np.sqrt(HD))
    for j in range(8):
        c[:, C_M8 + j] = (p // CHD == j) * np.float32(1.0 / np.sqrt(CHD))
    inv = (1.0 / np.power(np.float32(10000.0), np.arange(0, HD, 2, dtype=np.float32) / np.float32(HD))).astype(np.float32)
    angle = np.outer(np.arange(S, dtype=np.float32), inv).astype(np.float32)
    d = p % HD
    c[:S, C_COS:C_COS + P] = np.cos(angle)[:, d % (HD // 2)]
    c[:S, C_SIN:C_SIN + P] = np.sin(angle)[:, d % (HD // 2)] * np.where(d < HD // 2, -1.0, 1.0)[None, :]
    c[:, C_IDX] = p
    c[:, C_ROW:C_ROW + MT] = 1.0
    c[0, C_ROW + 1:C_ROW + MT] = 0.0
    c[:, C_EPS] = EPS
    c[:, C_SCALE] = 1.0 / np.sqrt(H)
    causal = np.zeros((S, 4, S), np.float32)
    causal[:] = np.where(np.tril(np.ones((S, S), bool)), 0.0, -3.0e38)[:, None, :]
    return c, causal.reshape(S, 4 * S)


def build(nc, d, out):
    ctx = ExitStack()
    n_sem = [0]

    stage_sems = []

    def sem(name):
        n_sem[0] += 1
        stage_sems.append(nc.alloc_semaphore(name=f"{name}_{n_sem[0]}"))
        return stage_sems[-1]

    def end_stage():
        nc.clear_and_free_semaphores(stage_sems)
        nc.all_engine_barrier()
        stage_sems.clear()

    def sbuf(stack, name, shape, dt=F32):
        n_sem[0] += 1
        return stack.enter_context(nc.sbuf_tensor(f"{name}_{n_sem[0]}", shape, dt))

    with ctx:
        bank = [ctx.enter_context(nc.psum_tensor(f"bank{i}", [P, 512], F32)) for i in range(8)]
        hT = sbuf(ctx, "hT", [P, KT, N])
        is_v = sbuf(ctx, "is_v", [P, N])
        is_l = sbuf(ctx, "is_l", [P, N])
        con = sbuf(ctx, "con", [P, C_END])
        wcol = sbuf(ctx, "wcol", [P, 20])
        cosT = sbuf(ctx, "cosT", [P, S])
        sinT = sbuf(ctx, "sinT", [P, S])
        flag = sbuf(ctx, "flag", [P, NG], I32)
        ident = con[:, C_ID:C_ID + P]
        ones = con[:, C_ONE:C_ONE + P]

        with ExitStack() as st:
            tok = sbuf(st, "tok", [P, N], I32)
            tokf = sbuf(st, "tokf", [P, N])
            posi = sbuf(st, "posi", [S, S], I32)
            posf = sbuf(st, "posf", [S, S])
            wrap = sbuf(st, "wrap", [S, S])
            hot = sbuf(st, "hot", [S, S])
            flagf = sbuf(st, "flagf", [P, NG])
            loaded, step, hot_ready, table, copied = (sem(x) for x in ("loaded", "step", "hot_ready", "table", "copied"))
            with nc.Block() as block:
                @block.sync
                def _(sp):
                    sp.dma_start(con[:, :], d["con"]).then_inc(loaded, 16)
                    sp.dma_start(wcol[:, :], d["wcol"]).then_inc(loaded, 16)
                    sp.dma_start(tok[:, :], d["tok"].partition_broadcast(P)).then_inc(loaded, 16)
                    sp.dma_start(posi[:, :], d["pos"].partition_broadcast(S)).then_inc(loaded, 16)
                    sp.dma_start(hT[:, :, :], d["x"]).then_inc(loaded, 16)

                @block.vector
                def _(dve):
                    n = [0]

                    def after(ins):
                        n[0] += 1
                        ins.then_inc(step, 1)
                        dve.wait_ge(step, n[0])

                    dve.wait_ge(loaded, 80)
                    after(dve.tensor_copy(posf[:, :], posi[:, :]))
                    after(dve.tensor_scalar(wrap[:, :], posf[:, :], 0.0, float(S), ALU.is_lt, ALU.mult))
                    after(dve.tensor_tensor(posf[:, :], posf[:, :], wrap[:, :], ALU.add))
                    after(dve.tensor_scalar(posf[:, :], posf[:, :], 0.0, float(S - 1), ALU.max, ALU.min))
                    dve.tensor_scalar(hot[:, :], posf[:, :], con[0:S, C_IDX:C_IDX + 1], None, ALU.is_equal).then_inc(hot_ready, 1)
                    after(dve.tensor_scalar(tokf[:, :], tok[:, :], 1.0, None, ALU.is_equal))
                    after(dve.tensor_tensor(is_v[:, 0:N - B], tokf[:, 0:N - B], tokf[:, B:N], ALU.mult))
                    after(dve.memset(is_v[:, N - B:N], 0.0))
                    dve.tensor_scalar(is_l[:, :], is_v[:, :], -1.0, 1.0, ALU.mult, ALU.add)
                    after(dve.tensor_reduce(flagf[:, :], is_v[:, :].rearrange("p (g c) -> p g c", g=NG), AX_X, ALU.max))
                    after(dve.tensor_copy(flag[:, :], flagf[:, :]))
                    dve.wait_ge(table, 1)
                    dve.tensor_copy(cosT[:, :], bank[0][:, 0:S]).then_inc(copied, 1)
                    dve.tensor_copy(sinT[:, :], bank[0][:, S:2 * S]).then_inc(copied, 1)
                    dve.wait_ge(copied, 2)

                @block.tensor
                def _(pe):
                    pe.wait_ge(hot_ready, 1)
                    pe.matmul(bank[0][:, 0:S], con[0:S, C_COS:C_COS + P], hot[:, :], start=True, stop=True)
                    pe.matmul(bank[0][:, S:2 * S], con[0:S, C_SIN:C_SIN + P], hot[:, :], start=True, stop=True).then_inc(table, 1)

        end_stage()

        def linear(name, w, pairs, nk, ne, operand, epilogue, prepare=None, first_flag=0, vision_slot=False):
            R = ne * nk * P
            with ExitStack() as st:
                raw = [sbuf(st, f"raw{s}", [P, R]) for s in range(2)]
                whi = [sbuf(st, f"whi{s}", [P, R], F32R) for s in range(2)]
                wlo = [sbuf(st, f"wlo{s}", [P, R], F32R) for s in range(2)]
                w_loaded = [sem("w_loaded") for _ in range(2)]
                w_hi = [sem("w_hi") for _ in range(2)]
                w_lo = [sem("w_lo") for _ in range(2)]
                ready = [sem("out_ready") for _ in range(4)]
                taken = [sem("out_taken") for _ in range(4)]
                operands_ready = sem("operands_ready")
                env = dict(st=st, ready=ready, taken=taken, operands_ready=operands_ready, n_operands=0)
                prep = prepare(env) if prepare else {}
                epi = epilogue(env)

                with nc.Block() as block:
                    @block.sync
                    def _(sp):
                        with sp.Fori(0, pairs) as p:
                            for s in range(2):
                                sp.wait_ge(w_lo[s], FREE + p)
                                sp.dma_start(raw[s][:, :], w[2 * p + s]).then_inc(w_loaded[s], 16)
                        for s in range(2):
                            sp.wait_ge(w_loaded[s], 16 * pairs)

                    @block.gpsimd
                    def _(pool):
                        def split_low(s, p):
                            pool.wait_ge(w_hi[s], p + 1)
                            pool.tensor_tensor(wlo[s][:, :], raw[s][:, :], whi[s][:, :].bitcast(F32), ALU.subtract).then_inc(w_lo[s], 1)

                        for s in range(2):
                            split_low(s, 0)
                        if "pool" in prep:
                            prep["pool"](pool)
                        if pairs > 1:
                            with pool.Fori(1, pairs) as p:
                                for s in range(2):
                                    split_low(s, p)
                        if "pool" in epi:
                            epi["pool"](pool)

                    @block.scalar
                    def _(act):
                        def split_high(s, p):
                            act.wait_ge(w_loaded[s], 16 * (p + 1))
                            act.activation(whi[s][:, :], raw[s][:, :], ACT.Copy).then_inc(w_hi[s], 1)

                        for s in range(2):
                            split_high(s, 0)
                        if "act" in prep:
                            prep["act"](act)

                        def body(p, last):
                            for s in range(2):
                                act.wait_ge(ready[2 * s + 1], p + 1)
                                if not last:
                                    split_high(s, p + 1)
                                for g in range(2):
                                    epi["act"](act, p, s, g)

                        if pairs > 1:
                            with act.Fori(0, pairs - 1) as p:
                                body(p, False)
                        body(pairs - 1, True)

                    @block.vector
                    def _(dve):
                        for free in (*w_lo, *taken, *env.get("open", ())):
                            dve.sem_inc(free, FREE)
                        if "dve" in prep:
                            prep["dve"](dve)
                        with dve.Fori(0, pairs) as p:
                            for s in range(2):
                                for g in range(2):
                                    epi["dve"](dve, p, s, g)

                    @block.tensor
                    def _(pe):
                        has_v = []
                        if ne == 2 or vision_slot:
                            for g in range(2):
                                has_v.append(pe.value_load(flag[0:1, first_flag + g:first_flag + g + 1], min_val=0, max_val=1))
                        if "pe" in prep:
                            prep["pe"](pe)
                        if env["n_operands"]:
                            pe.wait_ge(operands_ready, env["n_operands"])

                        def products(acc, s, e, g, kts, start, stop):
                            last = None
                            for kt in kts:
                                c = (e * nk + kt) * P
                                cols = slice(g * G, g * G + G)
                                hi, lo = operand[e]
                                terms = ((whi, hi), (wlo, hi), (whi, lo))
                                for n, (wt, x) in enumerate(terms):
                                    last = pe.matmul(acc, wt[s][:, c:c + P], x[:, kt, cols], start=start and kt == kts[0] and n == 0,
                                                     stop=stop and kt == kts[-1] and n == 2, skip_group_check=True)
                            return last

                        with pe.Fori(0, pairs) as p:
                            for s in range(2):
                                pe.wait_ge(w_lo[s], FREE + p + 1)
                                for g in range(2):
                                    i = 2 * s + g
                                    pe.wait_ge(taken[i], FREE + p)
                                    acc = bank[i][:, 0:G]
                                    if vision_slot and s == 1:
                                        with pe.If(has_v[g] != 0):
                                            products(acc, s, 0, g, range(nk), True, True).then_inc(ready[i], 1)
                                        with pe.Else():
                                            pe.matmul(acc, con[:, C_ZERO:C_ZERO + P], con[:, 0:G], start=True, stop=True,
                                                      skip_group_check=True).then_inc(ready[i], 1)
                                        continue
                                    products(acc, s, 0, g, range(0, 1), True, False)
                                    if ne == 2:
                                        with pe.If(has_v[g] != 0):
                                            products(acc, s, 1, g, range(nk), False, False)
                                    products(acc, s, 0, g, range(1, nk), False, True).then_inc(ready[i], 1)

            end_stage()

        def splitter(source, operand, nk, first, norm=None, batch_major=False, masked=True, more=None):
            ne = 2 if masked else 1

            def columns(kt, g):
                c0 = first + g * G
                if batch_major:
                    return source[:, kt, :, c0 // B:c0 // B + GP].rearrange("p b s -> p s b")
                if kt >= KT:
                    return more[:, kt - KT, c0:c0 + G]
                return source[:, kt, c0:c0 + G]

            def shaped(ap):
                return ap.rearrange("p (s b) -> p s b", b=B) if batch_major else ap

            def prepare(env):
                st = env["st"]
                tmp = [sbuf(st, f"tmp{i}", [P, G]) for i in range(2)]
                steps = [(g, kt, e) for g in range(2) for kt in range(nk) for e in range(ne)]
                env["n_operands"] = len(steps)
                made, high = sem("made"), sem("high")
                low = env["operands_ready"]
                if norm is not None:
                    sq = [sbuf(st, f"sq{i}", [P, G]) for i in range(2)]
                    rms = sbuf(st, "rms", [P, G])
                    rs = [sbuf(st, f"rs{i}", [P, G]) for i in range(2)]
                    squared, summed, root, inverse, scaled = (sem(x) for x in ("squared", "summed", "root", "inverse", "scaled"))

                def pe(eng):
                    if norm is None:
                        return
                    for g in range(2):
                        for kt in range(nk):
                            eng.wait_ge(squared, g * nk + kt + 1)
                            eng.matmul(bank[4 + g][:, 0:G], ones, sq[kt % 2][:, :], start=kt == 0, stop=kt == nk - 1).then_inc(summed, 1)

                def act(eng):
                    if norm is not None:
                        for g in range(2):
                            for kt in range(nk):
                                n = g * nk + kt
                                if n >= 2:
                                    eng.wait_ge(summed, n - 1)
                                eng.activation(sq[kt % 2][:, :], columns(kt, g), ACT.Square).then_inc(squared, 1)
                        for g in range(2):
                            eng.wait_ge(summed, (g + 1) * nk)
                            if g:
                                eng.wait_ge(inverse, g)
                            eng.activation(rms[:, :], bank[4 + g][:, 0:G], ACT.Sqrt, bias=con[:, C_EPS:C_EPS + 1],
                                           scale=1.0 / H).then_inc(root, 1)
                            for n in range(g * nk * ne, (g + 1) * nk * ne):
                                _, kt, e = steps[n]
                                eng.wait_ge(made, n + 1)
                                eng.activation(operand[e][0][:, kt, g * G:g * G + G], tmp[n % 2][:, :], ACT.Copy).then_inc(high, 1)
                        return
                    for n, (g, kt, e) in enumerate(steps):
                        eng.wait_ge(made, n + 1)
                        eng.activation(operand[e][0][:, kt, g * G:g * G + G], tmp[n % 2][:, :], ACT.Copy).then_inc(high, 1)

                def dve(eng):
                    for n, (g, kt, e) in enumerate(steps):
                        if norm is not None and kt == 0 and e == 0:
                            eng.wait_ge(root, g + 1)
                            if g:
                                eng.wait_ge(made, n)
                            target = rms if masked else rs[0]
                            eng.reciprocal(target[:, :], rms[:, :]).then_inc(inverse, 1)
                            eng.wait_ge(inverse, g + 1)
                            if masked:
                                cols = slice(first + g * G, first + g * G + G)
                                eng.tensor_tensor(rs[0][:, :], rms[:, :], is_l[:, cols], ALU.mult).then_inc(scaled, 1)
                                eng.tensor_tensor(rs[1][:, :], rms[:, :], is_v[:, cols], ALU.mult).then_inc(scaled, 1)
                                eng.wait_ge(scaled, 2 * (g + 1))
                        if n >= 2:
                            eng.wait_ge(low, n - 1)
                        if norm is not None:
                            ins = eng.scalar_tensor_tensor(out=tmp[n % 2][:, :], in0=columns(kt, g), scalar=wcol[:, norm + kt:norm + kt + 1],
                                                           in1=rs[e][:, :], op0=ALU.mult, op1=ALU.mult)
                        elif masked:
                            mask = (is_l, is_v)[e][:, first + g * G:first + g * G + G]
                            ins = eng.tensor_tensor(shaped(tmp[n % 2][:, :]), columns(kt, g), shaped(mask), ALU.mult)
                        else:
                            ins = eng.tensor_copy(shaped(tmp[n % 2][:, :]), columns(kt, g))
                        ins.then_inc(made, 1)

                def pool(eng):
                    for n, (g, kt, e) in enumerate(steps):
                        eng.wait_ge(high, n + 1)
                        hi, lo = operand[e]
                        cols = slice(g * G, g * G + G)
                        eng.tensor_tensor(lo[:, kt, cols], tmp[n % 2][:, :], hi[:, kt, cols].bitcast(F32), ALU.subtract).then_inc(low, 1)

                return dict(pe=pe, act=act, dve=dve, pool=pool)

            return prepare

        def store_batch_major(target, first):
            def epilogue(env):
                def emit(eng, mine, copy):
                    def f(eng, p, s, g):
                        if s != mine:
                            return
                        i = 2 * s + g
                        p0 = (first + g * G) // B
                        eng.wait_ge(env["ready"][i], p + 1)
                        copy(eng, target[:, 2 * p + s, :, p0:p0 + GP], bank[i][:, 0:G].rearrange("p (s b) -> p b s", b=B)).then_inc(env["taken"][i], 1)
                    return f
                return dict(act=emit(None, 0, lambda e, o, i: e.activation(o, i, ACT.Copy)),
                            dve=emit(None, 1, lambda e, o, i: e.tensor_copy(o, i)))
            return epilogue

        def add_to_residual(first):
            def epilogue(env):
                def dve(eng, p, s, g):
                    i = 2 * s + g
                    c0 = first + g * G
                    eng.wait_ge(env["ready"][i], p + 1)
                    h = hT[:, 2 * p + s, c0:c0 + G]
                    eng.tensor_tensor(h, h, bank[i][:, 0:G], ALU.add).then_inc(env["taken"][i], 1)
                return dict(act=lambda *a: None, dve=dve)
            return epilogue

        def add_masked(first):
            def epilogue(env):
                part = [sbuf(env["st"], f"part{g}", [P, G]) for g in range(2)]
                added = sem("added")

                def dve(eng, p, s, g):
                    i = 2 * s + g
                    cols = slice(first + g * G, first + g * G + G)
                    eng.wait_ge(env["ready"][i], p + 1)
                    eng.tensor_tensor(part[g][:, :], bank[i][:, 0:G], (is_l, is_v)[s][:, cols], ALU.mult).then_inc(env["taken"][i], 1)
                    eng.wait_ge(env["taken"][i], FREE + p + 1)
                    h = hT[:, p, cols]
                    eng.tensor_tensor(h, h, part[g][:, :], ALU.add).then_inc(added, 1)
                    eng.wait_ge(added, 4 * p + 2 * s + g + 1)
                return dict(act=lambda *a: None, dve=dve)
            return epilogue

        def pair_of_splits(st, name, nk):
            return tuple(sbuf(st, f"{name}_{part}", [P, nk, 2 * G], F32R) for part in ("hi", "lo"))

        with ExitStack() as st:
            qkv = sbuf(st, "qkv", [P, 12, B, S])
            for half in range(2):
                with ExitStack() as s2:
                    xl, xv = pair_of_splits(s2, "xl", KT), pair_of_splits(s2, "xv", KT)
                    linear("qkv", d["w_qkv"], 6, KT, 2, (xl, xv), store_batch_major(qkv, half * 2 * G),
                           splitter(hT, (xl, xv), KT, half * 2 * G, norm=W_IN), first_flag=2 * half)
            rotate(nc, sem, sbuf, qkv, cosT, sinT)
            end_stage()
            self_attention(nc, sem, sbuf, d, qkv, bank, con, ident, ones)
            end_stage()
            for half in range(2):
                with ExitStack() as s2:
                    al, av = pair_of_splits(s2, "al", KT), pair_of_splits(s2, "av", KT)
                    linear("dense", d["w_dense"], 2, KT, 2, (al, av), add_to_residual(half * 2 * G),
                           splitter(qkv, (al, av), KT, half * 2 * G, batch_major=True), first_flag=2 * half)

        with ExitStack() as st:
            cctx = sbuf(st, "cctx", [P, 4, B, S])
            with ExitStack() as s1:
                cq = sbuf(s1, "cq", [P, 2, B, S])
                for half in range(2):
                    with ExitStack() as s2:
                        x = pair_of_splits(s2, "x", KT)
                        linear("cq", d["w_cq"], 1, KT, 1, (x,), store_batch_major(cq, half * 2 * G),
                               splitter(hT, (x,), KT, half * 2 * G, norm=W_CROSS, masked=False))
                cross_attention(nc, sem, sbuf, d, cq, cctx, bank, con, ident)
                end_stage()
            for half in range(2):
                with ExitStack() as s2:
                    x = pair_of_splits(s2, "x", KT)
                    linear("cdense", d["w_cd"], 2, KT, 1, (x,), add_to_residual(half * 2 * G),
                           splitter(cctx, (x,), KT, half * 2 * G, batch_major=True, masked=False))

        for half in range(2):
            with ExitStack() as st:
                act_hi = sbuf(st, "act_hi", [P, IT, 2 * G], F32R)
                act_lo = sbuf(st, "act_lo", [P, IT, 2 * G], F32R)

                def gate_times_up(env):
                    silu = [sbuf(env["st"], f"silu{g}", [P, G]) for g in range(2)]
                    prod = [sbuf(env["st"], f"prod{g}", [P, G]) for g in range(2)]
                    prod_ready = [sem("prod_ready") for _ in range(2)]
                    prod_high = [sem("prod_high") for _ in range(2)]
                    prod_low = [sem("prod_low") for _ in range(2)]
                    ready, taken = env["ready"], env["taken"]
                    env["open"] = prod_ready

                    def act(eng, p, s, g):
                        if s == 0:
                            eng.wait_ge(ready[g], p + 1)
                            eng.wait_ge(prod_ready[g], FREE + p)
                            eng.activation(silu[g][:, :], bank[g][:, 0:G], ACT.Silu).then_inc(taken[g], 1)
                        else:
                            eng.wait_ge(prod_ready[g], FREE + p + 1)
                            eng.activation(act_hi[:, p, g * G:g * G + G], prod[g][:, :], ACT.Copy).then_inc(prod_high[g], 1)

                    def dve(eng, p, s, g):
                        if s == 0:
                            return
                        eng.wait_ge(ready[2 + g], p + 1)
                        eng.wait_ge(taken[g], FREE + p + 1)
                        eng.tensor_tensor(prod[g][:, :], silu[g][:, :], bank[2 + g][:, 0:G], ALU.mult).then_inc(prod_ready[g], 1)
                        eng.wait_ge(prod_high[g], p + 1)
                        cols = slice(g * G, g * G + G)
                        eng.tensor_tensor(act_lo[:, p, cols], prod[g][:, :], act_hi[:, p, cols].bitcast(F32), ALU.subtract).then_inc(taken[2 + g], 1)

                    return dict(act=act, dve=dve)

                with ExitStack() as s2:
                    xl, xv = pair_of_splits(s2, "xl", KT), pair_of_splits(s2, "xv", KT)
                    linear("gate_up", d["w_gu"], IT, KT, 2, (xl, xv), gate_times_up,
                           splitter(hT, (xl, xv), KT, half * 2 * G, norm=W_ATTN), first_flag=2 * half)
                linear("down", d["w_down"], 4, IT, 1, ((act_hi, act_lo),), add_masked(half * 2 * G), first_flag=2 * half,
                       vision_slot=True)

        fusion(nc, sem, end_stage, sbuf, d, linear, splitter, store_batch_major, pair_of_splits, bank, hT, con, wcol, ident, ones, out)


def wait_apart(eng, passed, sem, value):
    eng.wait_ge(sem, value)
    eng.sem_inc(passed, 1)


def rotate(nc, sem, sbuf, qkv, cosT, sinT):
    with ExitStack() as st:
        swap = [sbuf(st, f"swap{i}", [P, B, S]) for i in range(2)]
        part = [sbuf(st, f"part{i}", [P, B, S]) for i in range(2)]
        swapped, sined, cosed, done = (sem(x) for x in ("swapped", "sined", "cosed", "done"))
        mask = [(i + HD // 2) % HD for i in range(HD)]
        cos = cosT[:, :].unsqueeze(1).to_broadcast([P, B, S])
        sin = sinT[:, :].unsqueeze(1).to_broadcast([P, B, S])
        with nc.Block() as block:
            @block.vector
            def _(dve):
                for t in range(8):
                    if t >= 2:
                        dve.wait_ge(done, t - 1)
                    dve.stream_shuffle(swap[t % 2][:, :, :], qkv[:, t], mask).then_inc(swapped, 1)
                    dve.tensor_tensor(part[t % 2][:, :, :], qkv[:, t], cos, ALU.mult).then_inc(cosed, 1)
                    if t >= 1:
                        dve.wait_ge(sined, t)
                        dve.wait_ge(cosed, t)
                        dve.tensor_tensor(qkv[:, t - 1], swap[(t - 1) % 2][:, :, :], part[(t - 1) % 2][:, :, :], ALU.add).then_inc(done, 1)
                dve.wait_ge(sined, 8)
                dve.wait_ge(cosed, 8)
                dve.tensor_tensor(qkv[:, 7], swap[1][:, :, :], part[1][:, :, :], ALU.add).then_inc(done, 1)

            @block.gpsimd
            def _(pool):
                for t in range(8):
                    pool.wait_ge(swapped, t + 1)
                    pool.tensor_tensor(swap[t % 2][:, :, :], swap[t % 2][:, :, :], sin, ALU.mult).then_inc(sined, 1)



def self_attention(nc, sem, sbuf, d, qkv, bank, con, ident, ones):
    with ExitStack() as st:
        causal_f = sbuf(st, "causal_f", [S, 4 * S])
        causal = sbuf(st, "causal", [S, 4 * S], BF16)
        ident_b = sbuf(st, "ident_b", [S, S], BF16)
        q_masked = [sbuf(st, f"q_masked{i}", [P, 4, S]) for i in range(2)]
        v_in = sbuf(st, "v_in", [P, 4, S])
        v = sbuf(st, "v", [S, H])
        neg_max = [sbuf(st, f"neg_max{i}", [S, 4]) for i in range(2)]
        probs = [sbuf(st, f"probs{i}", [S, 4, S]) for i in range(2)]
        probs_t = [sbuf(st, f"probs_t{i}", [S, 4 * S]) for i in range(2)]
        rden = sbuf(st, "rden", [P, 4 * S])
        passed = sem("passed")
        sc, pt, ob, lb, vb = bank[0:2], bank[2:4], bank[4], bank[5], bank[6]
        c_loaded, c_ready, v_in_ready, v_turned, v_ready, inverted, normed = (
            sem(x) for x in ("c_loaded", "c_ready", "v_in_ready", "v_turned", "v_ready", "inverted", "normed"))
        q_ready, scored, maxed, exped, turned, copied, weighted = (
            [sem(x), sem(x)] for x in ("q_ready", "scored", "maxed", "exped", "turned", "copied", "weighted"))

        def use(b, t):
            return 2 * b + t // 2

        with nc.Block() as block:
            @block.sync
            def _(sp):
                sp.dma_start(causal_f[:, :], d["causal"]).then_inc(c_loaded, 16)

            @block.gpsimd
            def _(pool):
                with pool.Fori(0, B) as b:
                    wait_apart(pool, passed, v_turned, FREE + b)
                    pool.tensor_copy(v_in[:, :, :], qkv[:, 8:12, b, :]).then_inc(v_in_ready, 1)
                    for t in range(4):
                        wait_apart(pool, passed, scored[t % 2], FREE + use(b, t))
                        pool.tensor_tensor(q_masked[t % 2][:, :, :], qkv[:, t, b, :].unsqueeze(1).to_broadcast([P, 4, S]),
                                           con[:, C_M4:C_M4 + 4].unsqueeze(2).to_broadcast([P, 4, S]), ALU.mult).then_inc(q_ready[t % 2], 1)

            @block.tensor
            def _(pe):
                def turn_v(b):
                    pe.wait_ge(v_in_ready, b + 1)
                    pe.wait_ge(v_ready, FREE + b)
                    for t in range(4):
                        ins = pe.transpose(vb[0:S, t * P:t * P + P], v_in[:, t, :], ident)
                    ins.then_inc(v_turned, 1)

                def score(b, t):
                    par, n = t % 2, use(b, t)
                    pe.wait_ge(q_ready[par], n + 1)
                    pe.wait_ge(exped[par], FREE + n)
                    pe.matmul(sc[par][0:S, 0:4 * S], ident_b[:, :], causal[:, :], start=True, stop=False, skip_group_check=True)
                    for j in range(4):
                        ins = pe.matmul(sc[par][0:S, j * S:j * S + S], q_masked[par][:, j, :], qkv[:, 4 + t, b, :],
                                        start=False, stop=j == 3, skip_group_check=True)
                    ins.then_inc(scored[par], 1)

                def turn(b, t):
                    par, n = t % 2, use(b, t)
                    pe.wait_ge(exped[par], FREE + n + 1)
                    pe.wait_ge(copied[par], FREE + n)
                    for j in range(4):
                        ins = pe.transpose(pt[par][0:S, j * S:j * S + S], probs[par][:, j, :], ident[0:S, 0:S])
                    ins.then_inc(turned[par], 1)

                def weigh(b, t):
                    par, n = t % 2, use(b, t)
                    pe.wait_ge(copied[par], FREE + n + 1)
                    if t == 0:
                        pe.wait_ge(v_ready, FREE + b + 1)
                        pe.wait_ge(normed, FREE + b)
                    for j in range(4):
                        h = 4 * t + j
                        pe.matmul(ob[j * HD:j * HD + HD, t * S:t * S + S], v[:, h * HD:h * HD + HD], probs_t[par][:, j * S:j * S + S],
                                  start=True, stop=True)
                        ins = pe.matmul(lb[j * HD:j * HD + HD, t * S:t * S + S], ones[0:S, 0:HD], probs_t[par][:, j * S:j * S + S],
                                        start=True, stop=True)
                    ins.then_inc(weighted[par], 1)

                def body(b, first):
                    for t in range(4):
                        if t == 0:
                            turn_v(b)
                        score(b, t)
                        if not first or t >= 1:
                            turn(*((b, t - 1) if t >= 1 else (b - 1, 3)))
                        if not first or t >= 2:
                            weigh(*((b, t - 2) if t >= 2 else (b - 1, t + 2)))

                pe.wait_ge(c_ready, 2)
                body(0, True)
                with pe.Fori(1, B) as b:
                    body(b, False)
                turn(B - 1, 3)
                weigh(B - 1, 2)
                weigh(B - 1, 3)

            @block.scalar
            def _(act):
                with act.Fori(0, B) as b:
                    for t in range(4):
                        par, n = t % 2, use(b, t)
                        if t == 2:
                            act.wait_ge(v_turned, FREE + b + 1)
                            act.wait_ge(weighted[1], FREE + 2 * b)
                            act.wait_ge(weighted[0], FREE + 2 * b)
                            act.activation(v[:, :], vb[0:S, 0:H], ACT.Copy).then_inc(v_ready, 1)
                        act.wait_ge(maxed[par], n + 1)
                        act.wait_ge(turned[par], FREE + n)
                        for j in range(4):
                            ins = act.activation(probs[par][:, j, :], sc[par][0:S, j * S:j * S + S], ACT.Exp, bias=neg_max[par][:, j:j + 1])
                        ins.then_inc(exped[par], 1)

            @block.vector
            def _(dve):
                def row_max(b, t):
                    par, n = t % 2, use(b, t)
                    dve.wait_ge(scored[par], FREE + n + 1)
                    dve.wait_ge(exped[par], FREE + n)
                    dve.tensor_reduce(neg_max[par][:, :], sc[par][0:S, 0:4 * S].rearrange("p (j k) -> p j k", j=4), AX_X, ALU.max,
                                      negate=True).then_inc(maxed[par], 1)

                def copy_turned(b, t):
                    par, n = t % 2, use(b, t)
                    dve.wait_ge(turned[par], FREE + n + 1)
                    dve.wait_ge(weighted[par], FREE + n)
                    dve.tensor_copy(probs_t[par][:, :], pt[par][0:S, 0:4 * S]).then_inc(copied[par], 1)

                def normalise(b):
                    for par in range(2):
                        dve.wait_ge(weighted[par], FREE + 2 * b + 2)
                    dve.reciprocal(rden[:, :], lb[:, 0:4 * S]).then_inc(inverted, 1)
                    dve.wait_ge(inverted, b + 1)
                    dve.tensor_tensor(qkv[:, 0:4, b, :], ob[:, 0:4 * S].rearrange("p (t s) -> p t s", t=4),
                                      rden[:, :].rearrange("p (t s) -> p t s", t=4), ALU.mult).then_inc(normed, 1)

                def body(b, first):
                    for t in range(4):
                        row_max(b, t)
                        if t == 2 and not first:
                            normalise(b - 1)
                        if not first or t >= 1:
                            copy_turned(*((b, t - 1) if t >= 1 else (b - 1, 3)))

                for free in (v_turned, v_ready, normed, *scored, *exped, *turned, *copied, *weighted):
                    dve.sem_inc(free, FREE)
                dve.wait_ge(c_loaded, 16)
                dve.tensor_copy(causal[:, :], causal_f[:, :]).then_inc(c_ready, 1)
                dve.tensor_copy(ident_b[:, :], ident[0:S, 0:S]).then_inc(c_ready, 1)
                body(0, True)
                with dve.Fori(1, B) as b:
                    body(b, False)
                copy_turned(B - 1, 3)
                normalise(B - 1)


def cross_attention(nc, sem, sbuf, d, cq, cctx, bank, con, ident):
    MP = M + 1
    with ExitStack() as st:
        w_kv = sbuf(st, "w_kv", [P, 2, 2 * CC])
        w_hi = sbuf(st, "w_hi", [P, 2, 2 * CC], F32R)
        w_lo = sbuf(st, "w_lo", [P, 2, 2 * CC], F32R)
        ctx_raw = sbuf(st, "ctx_raw", [P, 2, MP])
        ctx_hi = sbuf(st, "ctx_hi", [P, 2, MP], F32R)
        ctx_lo = sbuf(st, "ctx_lo", [P, 2, MP], F32R)
        ck_hi = [sbuf(st, f"ck_hi{i}", [P, 2, MP], F32R) for i in range(2)]
        ck_lo = [sbuf(st, f"ck_lo{i}", [P, 2, MP], F32R) for i in range(2)]
        cv = [sbuf(st, f"cv{i}", [MK, MT, NH, 32]) for i in range(2)]
        q_tmp = [sbuf(st, f"q_tmp{i}", [P, 2, S]) for i in range(2)]
        q_hi = [sbuf(st, f"q_hi{i}", [P, 2, S], F32R) for i in range(2)]
        q_lo = [sbuf(st, f"q_lo{i}", [P, 2, S], F32R) for i in range(2)]
        neg_max = [sbuf(st, f"neg_max{i}", [S, 2]) for i in range(2)]
        probs = [sbuf(st, f"probs{i}", [S, 2, M]) for i in range(2)]
        probs_t = [sbuf(st, f"probs_t{i}", [MK, 2, MT * S]) for i in range(2)]
        den = sbuf(st, "den", [P, 4 * S])
        rden = sbuf(st, "rden", [P, 4 * S])
        passed = sem("passed")
        pt, ob, xb = bank[4:6], bank[6], bank[7]
        w_loaded, w_high, w_ready, ctx_loaded, ctx_high, ctx_ready, x_ready, ck_high, x_taken, ones_ready, shuffled, inverted, normed, q_step = (
            sem(x) for x in ("w_loaded", "w_high", "w_ready", "ctx_loaded", "ctx_high", "ctx_ready", "x_ready", "ck_high", "x_taken",
                             "ones_ready", "shuffled", "inverted", "normed", "q_step"))
        q_ready, scored, maxed, exped, turned, copied, weighted = (
            [sem(x), sem(x)] for x in ("q_ready", "scored", "maxed", "exped", "turned", "copied", "weighted"))

        def use(b, u):
            return 4 * b + u // 2

        def scores_bank(par, j):
            return bank[2 * par + j]

        with nc.Block() as block:
            @block.sync
            def _(sp):
                sp.dma_start(w_kv[:, :, :], d["w_ckv"]).then_inc(w_loaded, 16)
                with sp.Fori(0, B + 2) as b:
                    sp.wait_ge(ctx_ready, FREE + b)
                    sp.dma_start(ctx_raw[:, :, :], d["ctx_t"][b]).then_inc(ctx_loaded, 16)
                sp.wait_ge(ctx_loaded, 16 * (B + 2))

            @block.gpsimd
            def _(pool):
                def split_context(b):
                    wait_apart(pool, passed, ctx_high, b + 1)
                    pool.tensor_tensor(ctx_lo[:, :, :], ctx_raw[:, :, :], ctx_hi[:, :, :].bitcast(F32), ALU.subtract).then_inc(ctx_ready, 1)

                def mask_q(b, u):
                    par, n = u % 2, use(b, u)
                    wait_apart(pool, passed, scored[par], FREE + n)
                    k = 16 * b + 2 * u
                    pool.tensor_tensor(q_tmp[par][:, :, :], cq[:, u // 4, b, :].unsqueeze(1).to_broadcast([P, 2, S]),
                                       con[:, C_M8 + 2 * (u % 4):C_M8 + 2 * (u % 4) + 2].unsqueeze(2).to_broadcast([P, 2, S]),
                                       ALU.mult).then_inc(q_step, 1)
                    wait_apart(pool, passed, q_step, k + 1)
                    pool.tensor_copy(q_hi[par][:, :, :], q_tmp[par][:, :, :]).then_inc(q_step, 1)
                    wait_apart(pool, passed, q_step, k + 2)
                    pool.tensor_tensor(q_lo[par][:, :, :], q_tmp[par][:, :, :], q_hi[par][:, :, :].bitcast(F32), ALU.subtract)\
                        .then_inc(q_ready[par], 1)

                pool.wait_ge(w_high, 1)
                pool.tensor_tensor(w_lo[:, :, :], w_kv[:, :, :], w_hi[:, :, :].bitcast(F32), ALU.subtract).then_inc(w_ready, 1)
                split_context(0)
                split_context(1)
                with pool.Fori(0, B) as b:
                    for u in range(8):
                        mask_q(b, u)
                    split_context(b + 2)

            @block.tensor
            def _(pe):
                def make_kv(b, r):
                    if r == 0:
                        pe.wait_ge(ctx_ready, FREE + b + 1)
                    pe.wait_ge(x_taken, FREE + 5 * b + r)
                    terms = ((w_hi, ctx_hi), (w_lo, ctx_hi), (w_hi, ctx_lo))
                    for kt in range(2):
                        for n, (w, c) in enumerate(terms):
                            start, stop = kt == 0 and n == 0, kt == 1 and n == 2
                            if r < 2:
                                ins = pe.matmul(xb[:, 0:MP], w[:, kt, r * P:r * P + P], c[:, kt, :], start=start, stop=stop)
                            else:
                                m0 = (r - 2) * (MK - 1)
                                ins = pe.matmul(xb[0:MK, 0:CC], c[:, kt, m0:m0 + MK], w[:, kt, CC:2 * CC], start=start, stop=stop)
                    ins.then_inc(x_ready, 1)

                def score(b, par_b, u):
                    par, n = u % 2, use(b, u)
                    if u == 0:
                        pe.wait_ge(x_taken, FREE + 5 * b + 2)
                    pe.wait_ge(q_ready[par], n + 1)
                    pe.wait_ge(exped[par], FREE + n)
                    for j in range(2):
                        for k, (q, c) in enumerate(((q_hi, ck_hi), (q_lo, ck_hi), (q_hi, ck_lo))):
                            ins = pe.matmul(scores_bank(par, j)[0:S, 0:MP], q[par][:, j, :], c[par_b][:, u // 4, :], start=k == 0, stop=k == 2)
                    ins.then_inc(scored[par], 1)

                def turn(b, u):
                    par, n = u % 2, use(b, u)
                    pe.wait_ge(exped[par], FREE + n + 1)
                    pe.wait_ge(copied[1 - par], FREE + (4 * b + (u + 1) // 2 if par else 4 * b + u // 2))
                    for j in range(2):
                        for kt in range(MT):
                            m0 = kt * (MK - 1)
                            ins = pe.transpose(pt[j][0:MK, kt * S:kt * S + S], probs[par][:, j, m0:m0 + MK], ident[0:S, 0:S])
                    ins.then_inc(turned[par], 1)

                def weigh(b, par_b, u):
                    par, n = u % 2, use(b, u)
                    pe.wait_ge(copied[par], FREE + n + 1)
                    if u == 0:
                        pe.wait_ge(x_taken, FREE + 5 * b + 5)
                        pe.wait_ge(normed, FREE + b)
                    for j in range(2):
                        h = 2 * u + j
                        q0, c0 = 32 * (h % 4), (h // 4) * S
                        for kt in range(MT):
                            ins = pe.matmul(ob[q0:q0 + 32, c0:c0 + S], cv[par_b][:, kt, h, :], probs_t[par][:, j, kt * S:kt * S + S],
                                            start=kt == 0, stop=kt == MT - 1)
                    ins.then_inc(weighted[par], 1)

                def batch(b, par_b, first):
                    for u in range(8):
                        score(b, par_b, u)
                        if not first or u >= 1:
                            turn(*((b, u - 1) if u >= 1 else (b - 1, 7)))
                        if not first or u >= 2:
                            weigh(*((b, par_b, u - 2) if u >= 2 else (b - 1, 1 - par_b, u + 6)))
                        if 2 <= u < 7:
                            make_kv(b + 1, u - 2)

                pe.wait_ge(w_ready, 1)
                for r in range(5):
                    make_kv(0, r)
                pe.wait_ge(ones_ready, 2)
                batch(0, 0, True)
                batch(1, 1, False)
                with pe.Fori(1, B // 2) as c:
                    for par_b in range(2):
                        batch(2 * c + par_b, par_b, False)
                turn(B - 1, 7)
                weigh(B - 1, 1, 6)
                weigh(B - 1, 1, 7)

            @block.scalar
            def _(act):
                def split_context(b):
                    act.wait_ge(ctx_loaded, 16 * (b + 1))
                    if not isinstance(b, int) or b > 0:
                        act.wait_ge(x_ready, 5 * b)
                        act.wait_ge(ctx_ready, FREE + b)
                    act.activation(ctx_hi[:, :, :], ctx_raw[:, :, :], ACT.Copy).then_inc(ctx_high, 1)

                def take_keys(b, par_b, r):
                    act.wait_ge(x_ready, 5 * b + r + 1)
                    act.activation(ck_hi[par_b][:, r, :], xb[:, 0:MP], ACT.Copy).then_inc(ck_high, 1)

                def exps(b, u):
                    par, n = u % 2, use(b, u)
                    act.wait_ge(maxed[par], n + 1)
                    act.wait_ge(turned[par], FREE + n)
                    for j in range(2):
                        ins = act.activation(probs[par][:, j, :], scores_bank(par, j)[0:S, 0:M], ACT.Exp, bias=neg_max[par][:, j:j + 1])
                    ins.then_inc(exped[par], 1)

                act.wait_ge(w_loaded, 16)
                act.activation(w_hi[:, :, :], w_kv[:, :, :], ACT.Copy).then_inc(w_high, 1)
                split_context(0)
                for r in range(2):
                    take_keys(0, 0, r)
                split_context(1)
                with act.Fori(0, B // 2) as c:
                    for par_b in range(2):
                        b = 2 * c + par_b
                        for u in range(8):
                            exps(b, u)
                            if 2 <= u < 4:
                                take_keys(b + 1, 1 - par_b, u - 2)
                        split_context(b + 2)

            @block.vector
            def _(dve):
                def take_kv(b, par_b, r):
                    dve.wait_ge(x_ready, 5 * b + r + 1)
                    if r < 2:
                        dve.wait_ge(ck_high, 2 * b + r + 1)
                        ins = dve.tensor_tensor(ck_lo[par_b][:, r, :], xb[:, 0:MP], ck_hi[par_b][:, r, :].bitcast(F32), ALU.subtract)
                    else:
                        ins = dve.tensor_scalar(cv[par_b][:, r - 2, :, 0:CHD], xb[0:MK, 0:CC].rearrange("p (h e) -> p h e", h=NH),
                                                con[0:MK, C_ROW + r - 2:C_ROW + r - 1], None, ALU.mult)
                    ins.then_inc(x_taken, 1)

                def row_max(b, u):
                    par, n = u % 2, use(b, u)
                    dve.wait_ge(scored[par], FREE + n + 1)
                    dve.wait_ge(exped[par], FREE + n)
                    for j in range(2):
                        ins = dve.tensor_reduce(neg_max[par][:, j:j + 1], scores_bank(par, j)[0:S, 0:M], AX_X, ALU.max, negate=True)
                    ins.then_inc(maxed[par], 1)

                def copy_turned(b, u):
                    par, n = u % 2, use(b, u)
                    dve.wait_ge(turned[par], FREE + n + 1)
                    dve.wait_ge(weighted[par], FREE + n)
                    for j in range(2):
                        ins = dve.tensor_copy(probs_t[par][:, j, :], pt[j][0:MK, 0:MT * S])
                    ins.then_inc(copied[par], 1)

                def normalise(b):
                    for par in range(2):
                        dve.wait_ge(weighted[par], FREE + 4 * b + 4)
                    dve.reciprocal(den[:, :], ob[:, 0:4 * S]).then_inc(inverted, 1)
                    wait_apart(dve, passed, inverted, b + 1)
                    dve.stream_shuffle(rden[:, :], den[:, :], [16 + i % 16 for i in range(32)]).then_inc(shuffled, 1)
                    dve.wait_ge(shuffled, b + 1)
                    dve.tensor_tensor(cctx[:, :, b, :], ob[:, 0:4 * S].rearrange("p (t s) -> p t s", t=4),
                                      rden[:, :].rearrange("p (t s) -> p t s", t=4), ALU.mult).then_inc(normed, 1)

                def batch(b, par_b, first):
                    for u in range(8):
                        row_max(b, u)
                        if u == 2 and not first:
                            normalise(b - 1)
                        if not first or u >= 1:
                            copy_turned(*((b, u - 1) if u >= 1 else (b - 1, 7)))
                        if 2 <= u < 7:
                            take_kv(b + 1, 1 - par_b, u - 2)

                for free in (ctx_ready, x_taken, normed, *scored, *exped, *turned, *copied, *weighted):
                    dve.sem_inc(free, FREE)
                for i in range(2):
                    for kt in range(MT):
                        ins = dve.tensor_copy(cv[i][:, kt, :, CHD:32], con[0:MK, C_ROW + kt:C_ROW + kt + 1].unsqueeze(2).to_broadcast([MK, NH, 32 - CHD]))
                    ins.then_inc(ones_ready, 1)
                for r in range(5):
                    take_kv(0, 0, r)
                batch(0, 0, True)
                batch(1, 1, False)
                with dve.Fori(1, B // 2) as c:
                    for par_b in range(2):
                        batch(2 * c + par_b, par_b, False)
                copy_turned(B - 1, 7)
                normalise(B - 1)


def memory_attention(nc, sem, sbuf, d, gT, am, bank, con, ident):
    MP = M + 1
    with ExitStack() as st:
        def two(name, shape, dt=F32):
            return [sbuf(st, f"{name}{i}", shape, dt) for i in range(2)]

        raw, hi, lo = two("raw", [P, 2, MP]), two("hi", [P, 2, MP], F32R), two("lo", [P, 2, MP], F32R)
        rows = two("rows", [MK, MT, CC])
        g_tmp, g_hi, g_lo = two("g_tmp", [P, 2, S]), two("g_hi", [P, 2, S], F32R), two("g_lo", [P, 2, S], F32R)
        neg_max, probs, probs_t = two("neg_max", [S, 1]), two("probs", [S, M]), two("probs_t", [MK, MT * S])
        rden = two("rden", [P, S])
        row_ones = sbuf(st, "row_ones", [MK, MT, P])
        sc, pt, ob = bank[0:2], bank[2:4], bank[4:6]
        loaded, rows_loaded, high, low, g_made, g_high, g_low, scored, maxed, exped, turned, copied, weighted, inverted, normed = (
            [sem(x), sem(x)] for x in ("loaded", "rows_loaded", "high", "low", "g_made", "g_high", "g_low", "scored", "maxed", "exped",
                                       "turned", "copied", "weighted", "inverted", "normed"))
        ones_ready, passed = sem("ones_ready"), sem("passed")
        with nc.Block() as block:
            @block.sync
            def _(sp):
                with sp.Fori(0, B // 2) as c:
                    for r in range(2):
                        sp.wait_ge(low[r], FREE + c)
                        sp.dma_start(raw[r][:, :, :], d["ctx_t"][2 * c + r]).then_inc(loaded[r], 16)
                        sp.wait_ge(weighted[r], FREE + c)
                        sp.dma_start(rows[r][:, :, :], d["ctx_rows"][2 * c + r]).then_inc(rows_loaded[r], 16)

            @block.gpsimd
            def _(pool):
                with pool.Fori(0, B // 2) as c:
                    for r in range(2):
                        wait_apart(pool, passed, g_low[r], FREE + c)
                        pool.tensor_tensor(g_tmp[r][:, :, :], gT[:, :, 2 * c + r, :],
                                           con[:, C_SCALE:C_SCALE + 1].unsqueeze(2).to_broadcast([P, 2, S]), ALU.mult).then_inc(g_made[r], 1)
                        wait_apart(pool, passed, high[r], c + 1)
                        pool.tensor_tensor(lo[r][:, :, :], raw[r][:, :, :], hi[r][:, :, :].bitcast(F32), ALU.subtract).then_inc(low[r], 1)
                        wait_apart(pool, passed, g_high[r], c + 1)
                        pool.tensor_tensor(g_lo[r][:, :, :], g_tmp[r][:, :, :], g_hi[r][:, :, :].bitcast(F32), ALU.subtract).then_inc(g_low[r], 1)

            @block.scalar
            def _(act):
                def split(c, r):
                    act.wait_ge(loaded[r], 16 * (c + 1))
                    act.wait_ge(scored[r], FREE + c)
                    act.activation(hi[r][:, :, :], raw[r][:, :, :], ACT.Copy).then_inc(high[r], 1)
                    act.wait_ge(g_made[r], c + 1)
                    act.activation(g_hi[r][:, :, :], g_tmp[r][:, :, :], ACT.Copy).then_inc(g_high[r], 1)

                def exps(c, r):
                    act.wait_ge(maxed[r], c + 1)
                    act.wait_ge(turned[r], FREE + c)
                    act.activation(probs[r][:, :], sc[r][0:S, 0:M], ACT.Exp, bias=neg_max[r][:, :]).then_inc(exped[r], 1)

                split(0, 0)
                with act.Fori(0, B // 2 - 1) as c:
                    split(c, 1)
                    exps(c, 0)
                    split(c + 1, 0)
                    exps(c, 1)
                split(B // 2 - 1, 1)
                exps(B // 2 - 1, 0)
                exps(B // 2 - 1, 1)

            @block.tensor
            def _(pe):
                def score(c, r):
                    pe.wait_ge(low[r], FREE + c + 1)
                    pe.wait_ge(g_low[r], FREE + c + 1)
                    pe.wait_ge(exped[r], FREE + c)
                    for kt in range(2):
                        for n, (g, m) in enumerate(((g_hi, hi), (g_lo, hi), (g_hi, lo))):
                            ins = pe.matmul(sc[r][0:S, 0:MP], g[r][:, kt, :], m[r][:, kt, :], start=kt == 0 and n == 0, stop=kt == 1 and n == 2)
                    ins.then_inc(scored[r], 1)

                def turn(c, r):
                    pe.wait_ge(exped[r], FREE + c + 1)
                    pe.wait_ge(copied[r], FREE + c)
                    for kt in range(MT):
                        ins = pe.transpose(pt[r][0:MK, kt * S:kt * S + S], probs[r][:, kt * (MK - 1):kt * (MK - 1) + MK], ident[0:S, 0:S])
                    ins.then_inc(turned[r], 1)

                def weigh(c, r):
                    pe.wait_ge(copied[r], FREE + c + 1)
                    pe.wait_ge(rows_loaded[r], 16 * (c + 1))
                    pe.wait_ge(normed[r], FREE + c)
                    for m in range(3):
                        for kt in range(MT):
                            w = rows[r][:, kt, m * P:m * P + P] if m < 2 else row_ones[:, kt, :]
                            ins = pe.matmul(ob[r][:, m * S:m * S + S], w, probs_t[r][:, kt * S:kt * S + S], start=kt == 0, stop=kt == MT - 1)
                    ins.then_inc(weighted[r], 1)

                pe.wait_ge(ones_ready, MT)
                score(0, 0)
                score(0, 1)
                turn(0, 0)
                with pe.Fori(1, B // 2) as c:
                    score(c, 0)
                    turn(c - 1, 1)
                    weigh(c - 1, 0)
                    score(c, 1)
                    turn(c, 0)
                    weigh(c - 1, 1)
                last = B // 2 - 1
                turn(last, 1)
                weigh(last, 0)
                weigh(last, 1)

            @block.vector
            def _(dve):
                def row_max(c, r):
                    dve.wait_ge(scored[r], FREE + c + 1)
                    dve.wait_ge(exped[r], FREE + c)
                    dve.tensor_reduce(neg_max[r][:, :], sc[r][0:S, 0:M], AX_X, ALU.max, negate=True).then_inc(maxed[r], 1)

                def copy_turned(c, r):
                    dve.wait_ge(turned[r], FREE + c + 1)
                    dve.wait_ge(weighted[r], FREE + c)
                    dve.tensor_copy(probs_t[r][:, :], pt[r][0:MK, 0:MT * S]).then_inc(copied[r], 1)

                def normalise(c, r):
                    dve.wait_ge(weighted[r], FREE + c + 1)
                    dve.reciprocal(rden[r][:, :], ob[r][:, 2 * S:3 * S]).then_inc(inverted[r], 1)
                    dve.wait_ge(inverted[r], c + 1)
                    dve.tensor_tensor(am[:, :, 2 * c + r, :], ob[r][:, 0:2 * S].rearrange("p (m s) -> p m s", m=2),
                                      rden[r][:, :].unsqueeze(1).to_broadcast([P, 2, S]), ALU.mult).then_inc(normed[r], 1)

                for free in (*low, *g_low, *scored, *exped, *turned, *copied, *weighted, *normed):
                    dve.sem_inc(free, FREE)
                for kt in range(MT):
                    dve.tensor_scalar(row_ones[:, kt, :], con[0:MK, C_ONE:C_ONE + P], con[0:MK, C_ROW + kt:C_ROW + kt + 1], None,
                                      ALU.mult).then_inc(ones_ready, 1)
                row_max(0, 0)
                row_max(0, 1)
                copy_turned(0, 0)
                with dve.Fori(1, B // 2) as c:
                    row_max(c, 0)
                    copy_turned(c - 1, 1)
                    normalise(c - 1, 0)
                    row_max(c, 1)
                    copy_turned(c, 0)
                    normalise(c - 1, 1)
                last = B // 2 - 1
                copy_turned(last, 1)
                normalise(last, 0)
                normalise(last, 1)


def fusion(nc, sem, end_stage, sbuf, d, linear, splitter, store_batch_major, pair_of_splits, bank, hT, con, wcol, ident, ones, out):
    with ExitStack() as st:
        mc = sbuf(st, "mc", [P, KT, N])
        with ExitStack() as s1:
            gT = sbuf(s1, "gT", [P, 2, B, S])
            am = sbuf(s1, "am", [P, 2, B, S])
            for half in range(2):
                with ExitStack() as s2:
                    x = pair_of_splits(s2, "x", KT)
                    linear("mem_query", d["w_mem"], 1, KT, 1, (x,), store_batch_major(gT, half * 2 * G),
                           splitter(hT, (x,), KT, half * 2 * G, masked=False))
            memory_attention(nc, sem, sbuf, d, gT, am, bank, con, ident)
            end_stage()

            def store_context(first):
                def epilogue(env):
                    def emit(mine, copy):
                        def f(eng, p, s, g):
                            if s != mine:
                                return
                            i = 2 * s + g
                            eng.wait_ge(env["ready"][i], p + 1)
                            copy(eng, mc[:, 2 * p + s, first + g * G:first + g * G + G], bank[i][:, 0:G]).then_inc(env["taken"][i], 1)
                        return f
                    return dict(act=emit(0, lambda e, o, i: e.activation(o, i, ACT.Copy)), dve=emit(1, lambda e, o, i: e.tensor_copy(o, i)))
                return epilogue

            for half in range(2):
                with ExitStack() as s2:
                    x = pair_of_splits(s2, "x", 2)
                    linear("mem_out", d["w_mem_t"], 2, 2, 1, (x,), store_context(half * 2 * G),
                           splitter(am, (x,), 2, half * 2 * G, batch_major=True, masked=False))

        def gate_and_fuse(first):
            def epilogue(env):
                gate = [sbuf(env["st"], f"gate{i}", [P, G]) for i in range(4)]
                gated, fused = [sem("gated") for _ in range(4)], [sem("fused") for _ in range(4)]
                env["open"] = fused

                def act(eng, p, s, g):
                    i = 2 * s + g
                    eng.wait_ge(env["ready"][i], p + 1)
                    eng.wait_ge(fused[i], FREE + p)
                    eng.activation(gate[i][:, :], bank[i][:, 0:G], ACT.Sigmoid, bias=bias[:, 2 * p + s]).then_inc(env["taken"][i], 1)

                def dve(eng, p, s, g):
                    i = 2 * s + g
                    cols = slice(first + g * G, first + g * G + G)
                    eng.wait_ge(env["taken"][i], FREE + p + 1)
                    eng.tensor_tensor(gate[i][:, :], gate[i][:, :], mc[:, 2 * p + s, cols], ALU.mult).then_inc(gated[i], 1)
                    eng.wait_ge(gated[i], p + 1)
                    h = hT[:, 2 * p + s, cols]
                    eng.tensor_tensor(h, h, gate[i][:, :], ALU.add).then_inc(fused[i], 1)

                bias = wcol[:, W_BIAS:W_BIAS + KT].rearrange("p (k o) -> p k o", o=1)
                return dict(act=act, dve=dve)
            return epilogue

        for half in range(2):
            with ExitStack() as s2:
                x = pair_of_splits(s2, "x", 2 * KT)
                linear("gate", d["w_gate"], 2, 2 * KT, 1, (x,), gate_and_fuse(half * 2 * G),
                       splitter(hT, (x,), 2 * KT, half * 2 * G, masked=False, more=mc))

    with ExitStack() as st:
        sq = [sbuf(st, f"sq{i}", [P, G]) for i in range(2)]
        rms = [sbuf(st, f"rms{i}", [P, G]) for i in range(2)]
        y = sbuf(st, "y", [P, KT, N])
        squared, summed, root, inverse, scaled, stored = (sem(x) for x in ("squared", "summed", "root", "inverse", "scaled", "stored"))
        with nc.Block() as block:
            @block.scalar
            def _(act):
                for g in range(NG):
                    for kt in range(KT):
                        n = g * KT + kt
                        if n >= 2:
                            act.wait_ge(summed, n - 1)
                        act.activation(sq[kt % 2][:, :], hT[:, kt, g * G:g * G + G], ACT.Square).then_inc(squared, 1)
                    act.wait_ge(summed, (g + 1) * KT)
                    if g >= 2:
                        act.wait_ge(scaled, (g - 1) * KT)
                    act.activation(rms[g % 2][:, :], bank[g % 2][:, 0:G], ACT.Sqrt, bias=con[:, C_EPS:C_EPS + 1], scale=1.0 / H).then_inc(root, 1)

            @block.tensor
            def _(pe):
                for g in range(NG):
                    if g >= 2:
                        pe.wait_ge(root, g - 1)
                    for kt in range(KT):
                        pe.wait_ge(squared, g * KT + kt + 1)
                        pe.matmul(bank[g % 2][:, 0:G], ones, sq[kt % 2][:, :], start=kt == 0, stop=kt == KT - 1).then_inc(summed, 1)

            @block.vector
            def _(dve):
                for g in range(NG):
                    dve.wait_ge(root, g + 1)
                    dve.reciprocal(rms[g % 2][:, :], rms[g % 2][:, :]).then_inc(inverse, 1)
                    dve.wait_ge(inverse, g + 1)
                    for kt in range(KT):
                        dve.scalar_tensor_tensor(out=y[:, kt, g * G:g * G + G], in0=hT[:, kt, g * G:g * G + G],
                                                 scalar=wcol[:, W_OUT + kt:W_OUT + kt + 1], in1=rms[g % 2][:, :],
                                                 op0=ALU.mult, op1=ALU.mult).then_inc(scaled, 1)

            @block.sync
            def _(sp):
                for g in range(NG):
                    sp.wait_ge(scaled, (g + 1) * KT)
                    sp.dma_start(out[:, :, g * G:g * G + G], y[:, :, g * G:g * G + G]).then_inc(stored, 16)
                sp.wait_ge(stored, 16 * NG)


def kernel(**inputs):
    import concourse.bacc as _bacc
    from concourse.bass_utils import run_bass_kernel_spmd as _run

    a = {k: np.ascontiguousarray(v) for k, v in inputs.items()}

    def tiles(w):
        k, m = w.shape
        return w.reshape(k // P, P, m // P, P).transpose(2, 1, 0, 3)

    def experts(v, l):
        return np.stack([tiles(l), tiles(v)], axis=2)

    def padded(w, axis):
        pad = [(0, 0), (0, 0)]
        pad[axis] = (0, IT * P - w.shape[axis])
        return np.pad(w, pad)

    L0, L1 = "L0_xattn_", "L1_xattn_"
    ctx = a["ctx_1024"]
    ctx_t = np.pad(ctx.reshape(B, M, 2, P).transpose(0, 3, 2, 1), ((0, 2), (0, 0), (0, 0), (0, 1)))
    rows = np.zeros((B, MK, MT, CC), ctx.dtype)
    for kt in range(MT):
        lo = 0 if kt == 0 else 1
        rows[:, lo:, kt] = ctx[:, kt * (MK - 1) + lo:kt * (MK - 1) + MK]
    w_cd = np.zeros((NH, 32, H), np.float32)
    w_cd[:, :CHD] = a[L0 + "cdense_w"].reshape(NH, CHD, H)
    gu = np.stack([experts(padded(a[L0 + "v_" + n], 1), padded(a[L0 + "l_" + n], 1)) for n in ("gate", "up")], axis=1)
    down = np.stack([tiles(padded(a[L0 + n + "_down"], 0)) for n in ("l", "v")], axis=1)
    ckv = a[L0 + "ckv_w"]
    con, causal = shape_constants()
    vec = [a[L0 + "ln_in_w"], a[L0 + "ln_post_cross_w"], a[L0 + "ln_post_attn_w"], a[L1 + "norm_w"], a[L1 + "b_gate"]]
    arrays = {
        "x": a["x"].transpose(2, 1, 0).reshape(KT, P, N).transpose(1, 0, 2),
        "tok": a["mask_BxS_ik0"].T.reshape(N),
        "pos": a["pos_1xS"].reshape(S),
        "con": con,
        "causal": causal,
        "wcol": np.concatenate([v.reshape(KT, P).T for v in vec], axis=1),
        "w_qkv": experts(a[L0 + "v_qkv"], a[L0 + "l_qkv"]).reshape(12, P, -1),
        "w_dense": experts(a[L0 + "v_dense"], a[L0 + "l_dense"]).reshape(4, P, -1),
        "w_cq": tiles(a[L0 + "cq_w"]).reshape(2, P, -1),
        "w_ckv": ckv.reshape(2, P, 2 * CC).transpose(1, 0, 2),
        "w_cd": tiles(w_cd.reshape(NH * 32, H)).reshape(4, P, -1),
        "w_gu": gu.reshape(2 * IT, P, -1),
        "w_down": down.reshape(8, P, -1),
        "w_mem": tiles(a[L1 + "W_mem"]).reshape(2, P, -1),
        "w_mem_t": tiles(np.ascontiguousarray(a[L1 + "W_mem"].T)).reshape(4, P, -1),
        "w_gate": tiles(np.ascontiguousarray(a[L1 + "W_gate"].T)).reshape(4, P, -1),
        "ctx_t": ctx_t,
        "ctx_rows": rows,
    }
    arrays = {f"in_{k}": np.ascontiguousarray(v) for k, v in arrays.items()}
    nc = _bacc.Bacc("TRN2", target_bir_lowering=False, num_devices=1)
    d = {k[3:]: nc.dram_tensor(k, v.shape, mybir.dt.from_np(v.dtype), kind="ExternalInput").ap() for k, v in arrays.items()}
    out = nc.dram_tensor("out_0", (P, KT, N), F32, kind="ExternalOutput").ap()
    build(nc, d, out)
    got = _run(nc, [arrays], core_ids=[0]).results[0]["out_0"]
    return np.ascontiguousarray(got.transpose(1, 0, 2).reshape(H, S, B).transpose(2, 1, 0))
```

```python
from contextlib import ExitStack

import numpy as np

import concourse.bass as bass
from concourse import mybir

F32 = mybir.dt.float32
F32R = mybir.dt.float32r
BF16 = mybir.dt.bfloat16
I32 = mybir.dt.int32
ALU = mybir.AluOpType
ACT = mybir.ActivationFunctionType
AX_X = mybir.AxisListType.X

B, S, H = 16, 100, 512
N = B * S
P = 128
KT = H // P
NH, HD = 16, 32
CC, CHD = 256, 16
M = 361
MK, MT = 121, 3
IT = 11
G = 400
NG = N // G
GP = G // B
EPS = 1e-6
FREE, TWO = 1, 2

C_ID, C_ONE, C_M4, C_M8, C_COS, C_SIN, C_IDX, C_ROW, C_EPS, C_ZERO, C_SCALE, C_END = 0, 128, 256, 260, 268, 396, 524, 525, 528, 529, 657, 658
W_IN, W_CROSS, W_ATTN, W_OUT, W_BIAS = 0, 4, 8, 12, 16


def shape_constants():
    c = np.zeros((P, C_END), np.float32)
    c[:, C_ID:C_ID + P] = np.eye(P)
    c[:, C_ONE:C_ONE + P] = 1.0
    p = np.arange(P)
    for j in range(4):
        c[:, C_M4 + j] = (p // HD == j) * np.float32(1.0 / np.sqrt(HD))
    for j in range(8):
        c[:, C_M8 + j] = (p // CHD == j) * np.float32(1.0 / np.sqrt(CHD))
    inv = (1.0 / np.power(np.float32(10000.0), np.arange(0, HD, 2, dtype=np.float32) / np.float32(HD))).astype(np.float32)
    angle = np.outer(np.arange(S, dtype=np.float32), inv).astype(np.float32)
    d = p % HD
    c[:S, C_COS:C_COS + P] = np.cos(angle)[:, d % (HD // 2)]
    c[:S, C_SIN:C_SIN + P] = np.sin(angle)[:, d % (HD // 2)] * np.where(d < HD // 2, -1.0, 1.0)[None, :]
    c[:, C_IDX] = p
    c[:, C_ROW:C_ROW + MT] = 1.0
    c[0, C_ROW + 1:C_ROW + MT] = 0.0
    c[:, C_EPS] = EPS
    c[:, C_SCALE] = 1.0 / np.sqrt(H)
    causal = np.zeros((S, 4, S), np.float32)
    causal[:] = np.where(np.tril(np.ones((S, S), bool)), 0.0, -3.0e38)[:, None, :]
    return c, causal.reshape(S, 4 * S)


def build(nc, d, out):
    ctx = ExitStack()
    n_sem = [0]

    stage_sems = []

    def sem(name):
        n_sem[0] += 1
        stage_sems.append(nc.alloc_semaphore(name=f"{name}_{n_sem[0]}"))
        return stage_sems[-1]

    def end_stage():
        nc.clear_and_free_semaphores(stage_sems)
        nc.all_engine_barrier()
        stage_sems.clear()

    def sbuf(stack, name, shape, dt=F32):
        n_sem[0] += 1
        return stack.enter_context(nc.sbuf_tensor(f"{name}_{n_sem[0]}", shape, dt))

    with ctx:
        bank = [ctx.enter_context(nc.psum_tensor(f"bank{i}", [P, 512], F32)) for i in range(8)]
        hT = sbuf(ctx, "hT", [P, KT, N])
        is_v = sbuf(ctx, "is_v", [P, N])
        is_l = sbuf(ctx, "is_l", [P, N])
        con = sbuf(ctx, "con", [P, C_END])
        wcol = sbuf(ctx, "wcol", [P, 20])
        cosT = sbuf(ctx, "cosT", [P, S])
        sinT = sbuf(ctx, "sinT", [P, S])
        flag = sbuf(ctx, "flag", [P, NG], I32)
        ident = con[:, C_ID:C_ID + P]
        ones = con[:, C_ONE:C_ONE + P]

        with ExitStack() as st:
            tok = sbuf(st, "tok", [P, N], I32)
            tokf = sbuf(st, "tokf", [P, N])
            posi = sbuf(st, "posi", [S, S], I32)
            posf = sbuf(st, "posf", [S, S])
            wrap = sbuf(st, "wrap", [S, S])
            hot = sbuf(st, "hot", [S, S])
            flagf = sbuf(st, "flagf", [P, NG])
            loaded, step, hot_ready, table, copied = (sem(x) for x in ("loaded", "step", "hot_ready", "table", "copied"))
            with nc.Block() as block:
                @block.sync
                def _(sp):
                    sp.dma_start(con[:, :], d["con"]).then_inc(loaded, 16)
                    sp.dma_start(wcol[:, :], d["wcol"]).then_inc(loaded, 16)
                    sp.dma_start(tok[:, :], d["tok"].partition_broadcast(P)).then_inc(loaded, 16)
                    sp.dma_start(posi[:, :], d["pos"].partition_broadcast(S)).then_inc(loaded, 16)
                    sp.dma_start(hT[:, :, :], d["x"]).then_inc(loaded, 16)

                @block.vector
                def _(dve):
                    n = [0]

                    def after(ins):
                        n[0] += 1
                        ins.then_inc(step, 1)
                        dve.wait_ge(step, n[0])

                    dve.wait_ge(loaded, 80)
                    after(dve.tensor_copy(posf[:, :], posi[:, :]))
                    after(dve.tensor_scalar(wrap[:, :], posf[:, :], 0.0, float(S), ALU.is_lt, ALU.mult))
                    after(dve.tensor_tensor(posf[:, :], posf[:, :], wrap[:, :], ALU.add))
                    after(dve.tensor_scalar(posf[:, :], posf[:, :], 0.0, float(S - 1), ALU.max, ALU.min))
                    dve.tensor_scalar(hot[:, :], posf[:, :], con[0:S, C_IDX:C_IDX + 1], None, ALU.is_equal).then_inc(hot_ready, 1)
                    after(dve.tensor_scalar(tokf[:, :], tok[:, :], 1.0, None, ALU.is_equal))
                    after(dve.tensor_tensor(is_v[:, 0:N - B], tokf[:, 0:N - B], tokf[:, B:N], ALU.mult))
                    after(dve.memset(is_v[:, N - B:N], 0.0))
                    dve.tensor_scalar(is_l[:, :], is_v[:, :], -1.0, 1.0, ALU.mult, ALU.add)
                    after(dve.tensor_reduce(flagf[:, :], is_v[:, :].rearrange("p (g c) -> p g c", g=NG), AX_X, ALU.max))
                    after(dve.tensor_copy(flag[:, :], flagf[:, :]))
                    dve.wait_ge(table, 1)
                    dve.tensor_copy(cosT[:, :], bank[0][:, 0:S]).then_inc(copied, 1)
                    dve.tensor_copy(sinT[:, :], bank[0][:, S:2 * S]).then_inc(copied, 1)
                    dve.wait_ge(copied, 2)

                @block.tensor
                def _(pe):
                    pe.wait_ge(hot_ready, 1)
                    pe.matmul(bank[0][:, 0:S], con[0:S, C_COS:C_COS + P], hot[:, :], start=True, stop=True)
                    pe.matmul(bank[0][:, S:2 * S], con[0:S, C_SIN:C_SIN + P], hot[:, :], start=True, stop=True).then_inc(table, 1)

        end_stage()

        def linear(name, w, pairs, nk, ne, operand, epilogue, prepare=None, first_flag=0, vision_slot=False):
            R = ne * nk * P
            with ExitStack() as st:
                raw = [sbuf(st, f"raw{s}", [P, R]) for s in range(2)]
                whi = [sbuf(st, f"whi{s}", [P, R], F32R) for s in range(2)]
                wlo = [sbuf(st, f"wlo{s}", [P, R], F32R) for s in range(2)]
                w_loaded = [sem("w_loaded") for _ in range(2)]
                w_hi = [sem("w_hi") for _ in range(2)]
                w_lo = [sem("w_lo") for _ in range(2)]
                ready = [sem("out_ready") for _ in range(4)]
                taken = [sem("out_taken") for _ in range(4)]
                operands_ready = sem("operands_ready")
                env = dict(st=st, ready=ready, taken=taken, operands_ready=operands_ready, n_operands=0)
                prep = prepare(env) if prepare else {}
                epi = epilogue(env)

                with nc.Block() as block:
                    @block.sync
                    def _(sp):
                        with sp.Fori(0, pairs) as p:
                            for s in range(2):
                                sp.wait_ge(w_lo[s], FREE + p)
                                sp.dma_start(raw[s][:, :], w[2 * p + s]).then_inc(w_loaded[s], 16)
                        for s in range(2):
                            sp.wait_ge(w_loaded[s], 16 * pairs)

                    @block.gpsimd
                    def _(pool):
                        def split_low(s, p):
                            pool.wait_ge(w_hi[s], p + 1)
                            pool.tensor_tensor(wlo[s][:, :], raw[s][:, :], whi[s][:, :].bitcast(F32), ALU.subtract).then_inc(w_lo[s], 1)

                        for s in range(2):
                            split_low(s, 0)
                        if "pool" in prep:
                            prep["pool"](pool)
                        if pairs > 1:
                            with pool.Fori(1, pairs) as p:
                                for s in range(2):
                                    split_low(s, p)
                        if "pool" in epi:
                            epi["pool"](pool)

                    @block.scalar
                    def _(act):
                        def split_high(s, p):
                            act.wait_ge(w_loaded[s], 16 * (p + 1))
                            act.activation(whi[s][:, :], raw[s][:, :], ACT.Copy).then_inc(w_hi[s], 1)

                        for s in range(2):
                            split_high(s, 0)
                        if "act" in prep:
                            prep["act"](act)

                        def body(p, last):
                            for s in range(2):
                                act.wait_ge(ready[2 * s + 1], p + 1)
                                if not last:
                                    split_high(s, p + 1)
                                for g in range(2):
                                    epi["act"](act, p, s, g)

                        if pairs > 1:
                            with act.Fori(0, pairs - 1) as p:
                                body(p, False)
                        body(pairs - 1, True)

                    @block.vector
                    def _(dve):
                        for free in (*w_lo, *taken, *env.get("open", ())):
                            dve.sem_inc(free, FREE)
                        if "dve" in prep:
                            prep["dve"](dve)
                        with dve.Fori(0, pairs) as p:
                            for s in range(2):
                                for g in range(2):
                                    epi["dve"](dve, p, s, g)

                    @block.tensor
                    def _(pe):
                        has_v = []
                        if ne == 2 or vision_slot:
                            for g in range(2):
                                has_v.append(pe.value_load(flag[0:1, first_flag + g:first_flag + g + 1], min_val=0, max_val=1))
                        if "pe" in prep:
                            prep["pe"](pe)
                        if env["n_operands"]:
                            pe.wait_ge(operands_ready, env["n_operands"])

                        def products(acc, s, e, g, kts, start, stop):
                            last = None
                            for kt in kts:
                                c = (e * nk + kt) * P
                                cols = slice(g * G, g * G + G)
                                hi, lo = operand[e]
                                terms = ((whi, hi), (wlo, hi), (whi, lo))
                                for n, (wt, x) in enumerate(terms):
                                    last = pe.matmul(acc, wt[s][:, c:c + P], x[:, kt, cols], start=start and kt == kts[0] and n == 0,
                                                     stop=stop and kt == kts[-1] and n == 2, skip_group_check=True)
                            return last

                        with pe.Fori(0, pairs) as p:
                            for s in range(2):
                                pe.wait_ge(w_lo[s], FREE + p + 1)
                                for g in range(2):
                                    i = 2 * s + g
                                    pe.wait_ge(taken[i], FREE + p)
                                    acc = bank[i][:, 0:G]
                                    if vision_slot and s == 1:
                                        with pe.If(has_v[g] != 0):
                                            products(acc, s, 0, g, range(nk), True, True).then_inc(ready[i], 1)
                                        with pe.Else():
                                            pe.matmul(acc, con[:, C_ZERO:C_ZERO + P], con[:, 0:G], start=True, stop=True,
                                                      skip_group_check=True).then_inc(ready[i], 1)
                                        continue
                                    products(acc, s, 0, g, range(0, 1), True, False)
                                    if ne == 2:
                                        with pe.If(has_v[g] != 0):
                                            products(acc, s, 1, g, range(nk), False, False)
                                    products(acc, s, 0, g, range(1, nk), False, True).then_inc(ready[i], 1)

            end_stage()

        def splitter(source, operand, nk, first, norm=None, batch_major=False, masked=True, more=None):
            ne = 2 if masked else 1

            def columns(kt, g):
                c0 = first + g * G
                if batch_major:
                    return source[:, kt, :, c0 // B:c0 // B + GP].rearrange("p b s -> p s b")
                if kt >= KT:
                    return more[:, kt - KT, c0:c0 + G]
                return source[:, kt, c0:c0 + G]

            def shaped(ap):
                return ap.rearrange("p (s b) -> p s b", b=B) if batch_major else ap

            def prepare(env):
                st = env["st"]
                tmp = [sbuf(st, f"tmp{i}", [P, G]) for i in range(2)]
                steps = [(g, kt, e) for g in range(2) for kt in range(nk) for e in range(ne)]
                env["n_operands"] = len(steps)
                made, high = sem("made"), sem("high")
                low = env["operands_ready"]
                if norm is not None:
                    sq = [sbuf(st, f"sq{i}", [P, G]) for i in range(2)]
                    rms = sbuf(st, "rms", [P, G])
                    rs = [sbuf(st, f"rs{i}", [P, G]) for i in range(2)]
                    squared, summed, root, inverse, scaled = (sem(x) for x in ("squared", "summed", "root", "inverse", "scaled"))

                def pe(eng):
                    if norm is None:
                        return
                    for g in range(2):
                        for kt in range(nk):
                            eng.wait_ge(squared, g * nk + kt + 1)
                            eng.matmul(bank[4 + g][:, 0:G], ones, sq[kt % 2][:, :], start=kt == 0, stop=kt == nk - 1).then_inc(summed, 1)

                def act(eng):
                    if norm is not None:
                        for g in range(2):
                            for kt in range(nk):
                                n = g * nk + kt
                                if n >= 2:
                                    eng.wait_ge(summed, n - 1)
                                eng.activation(sq[kt % 2][:, :], columns(kt, g), ACT.Square).then_inc(squared, 1)
                        for g in range(2):
                            eng.wait_ge(summed, (g + 1) * nk)
                            if g:
                                eng.wait_ge(inverse, g)
                            eng.activation(rms[:, :], bank[4 + g][:, 0:G], ACT.Sqrt, bias=con[:, C_EPS:C_EPS + 1],
                                           scale=1.0 / H).then_inc(root, 1)
                            for n in range(g * nk * ne, (g + 1) * nk * ne):
                                _, kt, e = steps[n]
                                eng.wait_ge(made, n + 1)
                                eng.activation(operand[e][0][:, kt, g * G:g * G + G], tmp[n % 2][:, :], ACT.Copy).then_inc(high, 1)
                        return
                    for n, (g, kt, e) in enumerate(steps):
                        eng.wait_ge(made, n + 1)
                        eng.activation(operand[e][0][:, kt, g * G:g * G + G], tmp[n % 2][:, :], ACT.Copy).then_inc(high, 1)

                def dve(eng):
                    for n, (g, kt, e) in enumerate(steps):
                        if norm is not None and kt == 0 and e == 0:
                            eng.wait_ge(root, g + 1)
                            if g:
                                eng.wait_ge(made, n)
                            target = rms if masked else rs[0]
                            eng.reciprocal(target[:, :], rms[:, :]).then_inc(inverse, 1)
                            eng.wait_ge(inverse, g + 1)
                            if masked:
                                cols = slice(first + g * G, first + g * G + G)
                                eng.tensor_tensor(rs[0][:, :], rms[:, :], is_l[:, cols], ALU.mult).then_inc(scaled, 1)
                                eng.tensor_tensor(rs[1][:, :], rms[:, :], is_v[:, cols], ALU.mult).then_inc(scaled, 1)
                                eng.wait_ge(scaled, 2 * (g + 1))
                        if n >= 2:
                            eng.wait_ge(low, n - 1)
                        if norm is not None:
                            ins = eng.scalar_tensor_tensor(out=tmp[n % 2][:, :], in0=columns(kt, g), scalar=wcol[:, norm + kt:norm + kt + 1],
                                                           in1=rs[e][:, :], op0=ALU.mult, op1=ALU.mult)
                        elif masked:
                            mask = (is_l, is_v)[e][:, first + g * G:first + g * G + G]
                            ins = eng.tensor_tensor(shaped(tmp[n % 2][:, :]), columns(kt, g), shaped(mask), ALU.mult)
                        else:
                            ins = eng.tensor_copy(shaped(tmp[n % 2][:, :]), columns(kt, g))
                        ins.then_inc(made, 1)

                def pool(eng):
                    for n, (g, kt, e) in enumerate(steps):
                        eng.wait_ge(high, n + 1)
                        hi, lo = operand[e]
                        cols = slice(g * G, g * G + G)
                        eng.tensor_tensor(lo[:, kt, cols], tmp[n % 2][:, :], hi[:, kt, cols].bitcast(F32), ALU.subtract).then_inc(low, 1)

                return dict(pe=pe, act=act, dve=dve, pool=pool)

            return prepare

        def store_batch_major(target, first):
            def epilogue(env):
                def emit(eng, mine, copy):
                    def f(eng, p, s, g):
                        if s != mine:
                            return
                        i = 2 * s + g
                        p0 = (first + g * G) // B
                        eng.wait_ge(env["ready"][i], p + 1)
                        copy(eng, target[:, 2 * p + s, :, p0:p0 + GP], bank[i][:, 0:G].rearrange("p (s b) -> p b s", b=B)).then_inc(env["taken"][i], 1)
                    return f
                return dict(act=emit(None, 0, lambda e, o, i: e.activation(o, i, ACT.Copy)),
                            dve=emit(None, 1, lambda e, o, i: e.tensor_copy(o, i)))
            return epilogue

        def add_to_residual(first):
            def epilogue(env):
                def dve(eng, p, s, g):
                    i = 2 * s + g
                    c0 = first + g * G
                    eng.wait_ge(env["ready"][i], p + 1)
                    h = hT[:, 2 * p + s, c0:c0 + G]
                    eng.tensor_tensor(h, h, bank[i][:, 0:G], ALU.add).then_inc(env["taken"][i], 1)
                return dict(act=lambda *a: None, dve=dve)
            return epilogue

        def add_masked(first):
            def epilogue(env):
                part = [sbuf(env["st"], f"part{g}", [P, G]) for g in range(2)]
                added = sem("added")

                def dve(eng, p, s, g):
                    i = 2 * s + g
                    cols = slice(first + g * G, first + g * G + G)
                    eng.wait_ge(env["ready"][i], p + 1)
                    eng.tensor_tensor(part[g][:, :], bank[i][:, 0:G], (is_l, is_v)[s][:, cols], ALU.mult).then_inc(env["taken"][i], 1)
                    eng.wait_ge(env["taken"][i], FREE + p + 1)
                    h = hT[:, p, cols]
                    eng.tensor_tensor(h, h, part[g][:, :], ALU.add).then_inc(added, 1)
                    eng.wait_ge(added, 4 * p + 2 * s + g + 1)
                return dict(act=lambda *a: None, dve=dve)
            return epilogue

        def pair_of_splits(st, name, nk):
            return tuple(sbuf(st, f"{name}_{part}", [P, nk, 2 * G], F32R) for part in ("hi", "lo"))

        with ExitStack() as st:
            qkv = sbuf(st, "qkv", [P, 12, B, S])
            for half in range(2):
                with ExitStack() as s2:
                    xl, xv = pair_of_splits(s2, "xl", KT), pair_of_splits(s2, "xv", KT)
                    linear("qkv", d["w_qkv"], 6, KT, 2, (xl, xv), store_batch_major(qkv, half * 2 * G),
                           splitter(hT, (xl, xv), KT, half * 2 * G, norm=W_IN), first_flag=2 * half)
            rotate(nc, sem, sbuf, qkv, cosT, sinT)
            end_stage()
            self_attention(nc, sem, sbuf, d, qkv, bank, con, ident)
            end_stage()
            for half in range(2):
                with ExitStack() as s2:
                    al, av = pair_of_splits(s2, "al", KT), pair_of_splits(s2, "av", KT)
                    linear("dense", d["w_dense"], 2, KT, 2, (al, av), add_to_residual(half * 2 * G),
                           splitter(qkv, (al, av), KT, half * 2 * G, batch_major=True), first_flag=2 * half)

        with ExitStack() as st:
            cctx = sbuf(st, "cctx", [P, 2, B, S])
            with ExitStack() as s1:
                cq = sbuf(s1, "cq", [P, 2, B, S])
                for half in range(2):
                    with ExitStack() as s2:
                        x = pair_of_splits(s2, "x", KT)
                        linear("cq", d["w_cq"], 1, KT, 1, (x,), store_batch_major(cq, half * 2 * G),
                               splitter(hT, (x,), KT, half * 2 * G, norm=W_CROSS, masked=False))
                cross_attention(nc, sem, sbuf, d, cq, cctx, bank, con, ident)
                end_stage()
            for half in range(2):
                with ExitStack() as s2:
                    x = pair_of_splits(s2, "x", 2)
                    linear("cdense", d["w_cd"], 2, 2, 1, (x,), add_to_residual(half * 2 * G),
                           splitter(cctx, (x,), 2, half * 2 * G, batch_major=True, masked=False))

        for half in range(2):
            with ExitStack() as st:
                act_hi = sbuf(st, "act_hi", [P, IT, 2 * G], F32R)
                act_lo = sbuf(st, "act_lo", [P, IT, 2 * G], F32R)

                def gate_times_up(env):
                    silu = [sbuf(env["st"], f"silu{g}", [P, G]) for g in range(2)]
                    prod = [sbuf(env["st"], f"prod{g}", [P, G]) for g in range(2)]
                    prod_ready = [sem("prod_ready") for _ in range(2)]
                    prod_high = [sem("prod_high") for _ in range(2)]
                    prod_low = [sem("prod_low") for _ in range(2)]
                    ready, taken = env["ready"], env["taken"]
                    env["open"] = prod_ready

                    def act(eng, p, s, g):
                        if s == 0:
                            eng.wait_ge(ready[g], p + 1)
                            eng.wait_ge(prod_ready[g], FREE + p)
                            eng.activation(silu[g][:, :], bank[g][:, 0:G], ACT.Silu).then_inc(taken[g], 1)
                        else:
                            eng.wait_ge(prod_ready[g], FREE + p + 1)
                            eng.activation(act_hi[:, p, g * G:g * G + G], prod[g][:, :], ACT.Copy).then_inc(prod_high[g], 1)

                    def dve(eng, p, s, g):
                        if s == 0:
                            return
                        eng.wait_ge(ready[2 + g], p + 1)
                        eng.wait_ge(taken[g], FREE + p + 1)
                        eng.tensor_tensor(prod[g][:, :], silu[g][:, :], bank[2 + g][:, 0:G], ALU.mult).then_inc(prod_ready[g], 1)
                        eng.wait_ge(prod_high[g], p + 1)
                        cols = slice(g * G, g * G + G)
                        eng.tensor_tensor(act_lo[:, p, cols], prod[g][:, :], act_hi[:, p, cols].bitcast(F32), ALU.subtract).then_inc(taken[2 + g], 1)

                    return dict(act=act, dve=dve)

                with ExitStack() as s2:
                    xl, xv = pair_of_splits(s2, "xl", KT), pair_of_splits(s2, "xv", KT)
                    linear("gate_up", d["w_gu"], IT, KT, 2, (xl, xv), gate_times_up,
                           splitter(hT, (xl, xv), KT, half * 2 * G, norm=W_ATTN), first_flag=2 * half)
                linear("down", d["w_down"], 4, IT, 1, ((act_hi, act_lo),), add_masked(half * 2 * G), first_flag=2 * half,
                       vision_slot=True)

        fusion(nc, sem, end_stage, sbuf, d, linear, splitter, store_batch_major, pair_of_splits, bank, hT, con, wcol, ident, ones, out)


def wait_apart(eng, passed, sem, value):
    eng.wait_ge(sem, value)
    eng.sem_inc(passed, 1)


def rotate(nc, sem, sbuf, qkv, cosT, sinT):
    with ExitStack() as st:
        swap = [sbuf(st, f"swap{i}", [P, B, S]) for i in range(2)]
        part = [sbuf(st, f"part{i}", [P, B, S]) for i in range(2)]
        swapped, sined, cosed, done = (sem(x) for x in ("swapped", "sined", "cosed", "done"))
        mask = [(i + HD // 2) % HD for i in range(HD)]
        cos = cosT[:, :].unsqueeze(1).to_broadcast([P, B, S])
        sin = sinT[:, :].unsqueeze(1).to_broadcast([P, B, S])
        with nc.Block() as block:
            @block.vector
            def _(dve):
                for t in range(8):
                    if t >= 2:
                        dve.wait_ge(done, t - 1)
                    dve.stream_shuffle(swap[t % 2][:, :, :], qkv[:, t], mask).then_inc(swapped, 1)
                    dve.tensor_tensor(part[t % 2][:, :, :], qkv[:, t], cos, ALU.mult).then_inc(cosed, 1)
                    if t >= 1:
                        dve.wait_ge(sined, t)
                        dve.wait_ge(cosed, t)
                        dve.tensor_tensor(qkv[:, t - 1], swap[(t - 1) % 2][:, :, :], part[(t - 1) % 2][:, :, :], ALU.add).then_inc(done, 1)
                dve.wait_ge(sined, 8)
                dve.wait_ge(cosed, 8)
                dve.tensor_tensor(qkv[:, 7], swap[1][:, :, :], part[1][:, :, :], ALU.add).then_inc(done, 1)

            @block.gpsimd
            def _(pool):
                for t in range(8):
                    pool.wait_ge(swapped, t + 1)
                    pool.tensor_tensor(swap[t % 2][:, :, :], swap[t % 2][:, :, :], sin, ALU.mult).then_inc(sined, 1)



def self_attention(nc, sem, sbuf, d, qkv, bank, con, ident):
    T = NH // 4
    with ExitStack() as st:
        def two(name, shape, dt=F32):
            return [sbuf(st, f"{name}{i}", shape, dt) for i in range(2)]

        causal_f = sbuf(st, "causal_f", [S, 4 * S])
        causal = sbuf(st, "causal", [S, 4 * S], BF16)
        ident_b = sbuf(st, "ident_b", [S, S], BF16)
        q_masked = two("q_masked", [P, 4, S])
        v_in = sbuf(st, "v_in", [P, T, S])
        v = two("v", [S, H])
        neg_max, probs, probs_t = two("neg_max", [S, 4]), two("probs", [S, 4, S]), two("probs_t", [S, 4 * S])
        den, rden = two("den", [S, NH]), two("rden", [S, NH])
        rows = sbuf(st, "rows", [S, NH, HD])
        sc, pt, ob, vb, xb = bank[0:2], bank[2:4], bank[4:6], bank[6], bank[7]
        (c_loaded, c_ready, v_in_ready, v_turned, v_ready, q_ready, scored, maxed, exped, turned, copied, weighted, inverted, normed,
         rows_turned, stored, passed) = (
            sem(x) for x in ("c_loaded", "c_ready", "v_in_ready", "v_turned", "v_ready", "q_ready", "scored", "maxed", "exped", "turned",
                             "copied", "weighted", "inverted", "normed", "rows_turned", "stored", "passed"))

        def before(b, t, lag):
            return (b, 0, t - lag) if t >= lag else (b - 1, 1, t - lag + T)

        with nc.Block() as block:
            @block.sync
            def _(sp):
                sp.dma_start(causal_f[:, :], d["causal"]).then_inc(c_loaded, 16)

            @block.gpsimd
            def _(pool):
                with pool.Fori(0, B) as b:
                    wait_apart(pool, passed, v_turned, FREE + b)
                    pool.tensor_copy(v_in[:, :, :], qkv[:, 8:12, b, :]).then_inc(v_in_ready, 1)
                    for t in range(T):
                        wait_apart(pool, passed, scored, 1 + T * b + t)
                        pool.tensor_tensor(q_masked[t % 2][:, :, :], qkv[:, t, b, :].unsqueeze(1).to_broadcast([P, 4, S]),
                                           con[:, C_M4:C_M4 + 4].unsqueeze(2).to_broadcast([P, 4, S]), ALU.mult).then_inc(q_ready, 1)

            @block.tensor
            def _(pe):
                def turn_v(b):
                    pe.wait_ge(v_in_ready, b + 1)
                    pe.wait_ge(v_ready, FREE + b)
                    for t in range(T):
                        ins = pe.transpose(vb[0:S, t * P:t * P + P], v_in[:, t, :], ident)
                    ins.then_inc(v_turned, 1)

                def score(b, t):
                    pe.wait_ge(q_ready, T * b + t + 1)
                    pe.wait_ge(exped, 1 + T * b + t)
                    pe.matmul(sc[t % 2][0:S, 0:4 * S], ident_b[:, :], causal[:, :], start=True, stop=False, skip_group_check=True)
                    for j in range(4):
                        ins = pe.matmul(sc[t % 2][0:S, j * S:j * S + S], q_masked[t % 2][:, j, :], qkv[:, 4 + t, b, :],
                                        start=False, stop=j == 3, skip_group_check=True)
                    ins.then_inc(scored, 1)

                def turn(b, t):
                    pe.wait_ge(exped, TWO + T * b + t + 1)
                    pe.wait_ge(copied, 1 + T * b + t)
                    for j in range(4):
                        ins = pe.transpose(pt[t % 2][0:S, j * S:j * S + S], probs[t % 2][:, j, :], ident[0:S, 0:S])
                    ins.then_inc(turned, 1)

                def weigh(b, r, t):
                    pe.wait_ge(copied, TWO + T * b + t + 1)
                    if t == 0:
                        pe.wait_ge(v_ready, FREE + b + 1)
                        pe.wait_ge(normed, 1 + b)
                    for j in range(4):
                        h = 4 * t + j
                        ins = pe.matmul(ob[r][0:S, h * HD:h * HD + HD], probs_t[t % 2][:, j * S:j * S + S], v[r][:, h * HD:h * HD + HD],
                                        start=True, stop=True)
                    ins.then_inc(weighted, 1)

                def turn_rows(b):
                    pe.wait_ge(normed, TWO + b + 1)
                    pe.wait_ge(stored, FREE + b)
                    for t in range(T):
                        ins = pe.transpose(xb[:, t * S:t * S + S], rows[:, 4 * t:4 * t + 4, :].rearrange("p h e -> p (h e)"), ident[0:S, 0:S])
                    ins.then_inc(rows_turned, 1)

                def batch(b, r, first):
                    for t in range(T):
                        if t == 0:
                            turn_v(b)
                        score(b, t)
                        for lag, step in ((2, "turn"), (3, "weigh")):
                            bb, back, tt = before(b, t, lag)
                            if first and back:
                                continue
                            if step == "turn":
                                turn(bb, tt)
                            else:
                                weigh(bb, r ^ back, tt)
                        if t == 3 and not first:
                            turn_rows(b - 1)

                pe.wait_ge(c_ready, 2)
                batch(0, 0, True)
                batch(1, 1, False)
                with pe.Fori(1, B // 2) as c:
                    for r in range(2):
                        batch(2 * c + r, r, False)
                turn(B - 1, 2)
                weigh(B - 1, 1, 1)
                turn(B - 1, 3)
                weigh(B - 1, 1, 2)
                weigh(B - 1, 1, 3)
                turn_rows(B - 1)

            @block.scalar
            def _(act):
                with act.Fori(0, B // 2) as c:
                    for r in range(2):
                        b = 2 * c + r
                        for t in range(T):
                            act.wait_ge(maxed, T * b + t + 1)
                            act.wait_ge(turned, 1 + T * b + t)
                            if t == 0:
                                act.wait_ge(normed, 1 + b)
                            for j in range(4):
                                ins = act.activation(probs[t % 2][:, j, :], sc[t % 2][0:S, j * S:j * S + S], ACT.Exp,
                                                     bias=neg_max[t % 2][:, j:j + 1], accum_out=den[r][:, 4 * t + j:4 * t + j + 1])
                            ins.then_inc(exped, 1)
                            if t == 1:
                                act.wait_ge(v_turned, FREE + b + 1)
                                act.activation(v[r][:, :], vb[0:S, 0:H], ACT.Copy).then_inc(v_ready, 1)

            @block.vector
            def _(dve):
                def row_max(b, t):
                    dve.wait_ge(scored, TWO + T * b + t + 1)
                    dve.wait_ge(exped, 1 + T * b + t)
                    dve.tensor_reduce(neg_max[t % 2][:, :], sc[t % 2][0:S, 0:4 * S].rearrange("p (j k) -> p j k", j=4), AX_X, ALU.max,
                                      negate=True).then_inc(maxed, 1)

                def copy_turned(b, t):
                    dve.wait_ge(turned, TWO + T * b + t + 1)
                    dve.wait_ge(weighted, 1 + T * b + t)
                    dve.tensor_copy(probs_t[t % 2][:, :], pt[t % 2][0:S, 0:4 * S]).then_inc(copied, 1)

                def normalise(b, r):
                    dve.wait_ge(weighted, TWO + T * (b + 1))
                    dve.wait_ge(rows_turned, FREE + b)
                    dve.reciprocal(rden[r][:, :], den[r][:, :]).then_inc(inverted, 1)
                    dve.wait_ge(inverted, b + 1)
                    dve.tensor_tensor(rows[:, :, :], ob[r][0:S, 0:H].rearrange("p (h e) -> p h e", h=NH),
                                      rden[r][:, :].unsqueeze(2).to_broadcast([S, NH, HD]), ALU.mult).then_inc(normed, 1)

                def store(b):
                    dve.wait_ge(rows_turned, FREE + b + 1)
                    dve.tensor_copy(qkv[:, 0:T, b, :], xb[:, 0:4 * S].rearrange("p (t s) -> p t s", t=T)).then_inc(stored, 1)

                def batch(b, r, first):
                    for t in range(T):
                        row_max(b, t)
                        bb, back, tt = before(b, t, 2)
                        if not first or not back:
                            copy_turned(bb, tt)
                        if t == 2 and not first:
                            normalise(b - 1, 1 - r)
                        if t == 3 and not first:
                            store(b - 1)

                for free in (v_turned, v_ready, stored, rows_turned):
                    dve.sem_inc(free, FREE)
                for free in (scored, exped, turned, copied, weighted, normed):
                    dve.sem_inc(free, TWO)
                dve.wait_ge(c_loaded, 16)
                dve.tensor_copy(causal[:, :], causal_f[:, :]).then_inc(c_ready, 1)
                dve.tensor_copy(ident_b[:, :], ident[0:S, 0:S]).then_inc(c_ready, 1)
                batch(0, 0, True)
                batch(1, 1, False)
                with dve.Fori(1, B // 2) as c:
                    for r in range(2):
                        batch(2 * c + r, r, False)
                copy_turned(B - 1, 2)
                copy_turned(B - 1, 3)
                normalise(B - 1, 1)
                store(B - 1)


def cross_attention(nc, sem, sbuf, d, cq, cctx, bank, con, ident):
    MP = M + 1
    TURN, WEIGH = 3, 4
    with ExitStack() as st:
        def many(n, name, shape, dt=F32):
            return [sbuf(st, f"{name}{i}", shape, dt) for i in range(n)]

        w_kv = sbuf(st, "w_kv", [P, 2, 2 * CC])
        w_hi = sbuf(st, "w_hi", [P, 2, 2 * CC], F32R)
        w_lo = sbuf(st, "w_lo", [P, 2, 2 * CC], F32R)
        ctx_raw = sbuf(st, "ctx_raw", [P, 2, MP])
        ctx_hi = sbuf(st, "ctx_hi", [P, 2, MP], F32R)
        ctx_lo = sbuf(st, "ctx_lo", [P, 2, MP], F32R)
        ck_hi, ck_lo = many(2, "ck_hi", [P, 2, MP], F32R), many(2, "ck_lo", [P, 2, MP], F32R)
        cv = many(2, "cv", [MK, MT, CC])
        q_parts = sbuf(st, "q_parts", [P, 2, 2, B, S], F32R)
        q = many(4, "q", [P, 2, S], F32R)
        neg_max, probs = many(4, "neg_max", [S, 1]), many(4, "probs", [S, M])
        probs_t = many(2, "probs_t", [MK, MT * S])
        den, rden = many(2, "den", [S, NH]), many(2, "rden", [S, NH])
        rows = sbuf(st, "rows", [S, NH, CHD])
        sc, pt, ob, xb = bank[0:4], bank[4:6], bank[6], bank[7]
        XT = MT * S
        (w_loaded, w_high, w_ready, q_high, q_split, ctx_loaded, ctx_high, ctx_ready, x_ready, ck_high, x_taken, inverted, normed, rows_turned,
         stored, q_ready, scored, maxed, exped, turned, weighted, passed) = (
            sem(x) for x in ("w_loaded", "w_high", "w_ready", "q_high", "q_split", "ctx_loaded", "ctx_high", "ctx_ready", "x_ready", "ck_high",
                             "x_taken", "inverted", "normed", "rows_turned", "stored", "q_ready", "scored", "maxed", "exped", "turned",
                             "weighted", "passed"))
        copied = [sem("copied_even"), sem("copied_odd")]

        def before(h, lag):
            return (h - lag) % NH, int(h < lag)

        with nc.Block() as block:
            @block.sync
            def _(sp):
                sp.dma_start(w_kv[:, :, :], d["w_ckv"]).then_inc(w_loaded, 16)
                with sp.Fori(0, B + 2) as b:
                    sp.wait_ge(ctx_ready, FREE + b)
                    sp.dma_start(ctx_raw[:, :, :], d["ctx_t"][b]).then_inc(ctx_loaded, 16)
                sp.wait_ge(ctx_loaded, 16 * (B + 2))

            @block.gpsimd
            def _(pool):
                def split_context(b):
                    wait_apart(pool, passed, ctx_high, b + 1)
                    pool.tensor_tensor(ctx_lo[:, :, :], ctx_raw[:, :, :], ctx_hi[:, :, :].bitcast(F32), ALU.subtract).then_inc(ctx_ready, 1)

                pool.wait_ge(w_high, 1)
                pool.tensor_tensor(w_lo[:, :, :], w_kv[:, :, :], w_hi[:, :, :].bitcast(F32), ALU.subtract).then_inc(w_ready, 1)
                split_context(0)
                split_context(1)
                pool.wait_ge(q_split, 2)
                with pool.Fori(0, B) as b:
                    for h in range(NH):
                        wait_apart(pool, passed, scored, 1 + NH * b + h)
                        pool.tensor_tensor(q[h % 4][:, :, :], q_parts[:, h // 8, :, b, :].bitcast(F32),
                                           con[:, C_M8 + h % 8:C_M8 + h % 8 + 1].unsqueeze(2).to_broadcast([P, 2, S]),
                                           ALU.mult).then_inc(q_ready, 1)
                    split_context(b + 2)

            @block.tensor
            def _(pe):
                def make_kv(b, r, halves=range(2)):
                    terms = ((w_hi, ctx_hi), (w_lo, ctx_hi), (w_hi, ctx_lo))
                    for kt in halves:
                        if kt == 0:
                            if r == 0:
                                pe.wait_ge(ctx_ready, FREE + b + 1)
                            pe.wait_ge(x_taken, FREE + 5 * b + r)
                        for n, (w, c) in enumerate(terms):
                            start, stop = kt == 0 and n == 0, kt == 1 and n == 2
                            if r < 2:
                                ins = pe.matmul(xb[:, 0:MP], w[:, kt, r * P:r * P + P], c[:, kt, :], start=start, stop=stop)
                            else:
                                m0 = (r - 2) * (MK - 1)
                                ins = pe.matmul(xb[0:MK, 0:CC], c[:, kt, m0:m0 + MK], w[:, kt, CC:2 * CC], start=start, stop=stop)
                        if kt == 1:
                            ins.then_inc(x_ready, 1)

                def score(b, par_b, h):
                    if h == 0:
                        pe.wait_ge(x_taken, FREE + 5 * b + 2)
                    pe.wait_ge(q_ready, NH * b + h + 1)
                    pe.wait_ge(exped, 1 + NH * b + h)
                    for k, (part, c) in enumerate(((0, ck_hi), (1, ck_hi), (0, ck_lo))):
                        ins = pe.matmul(sc[h % 4][0:S, 0:MP], q[h % 4][:, part, :], c[par_b][:, h // 8, :], start=k == 0, stop=k == 2)
                    ins.then_inc(scored, 1)

                def turn(b, h):
                    pe.wait_ge(exped, 4 + NH * b + h + 1)
                    pe.wait_ge(copied[h % 2], FREE + 8 * b + h // 2)
                    if h == 12:
                        pe.wait_ge(stored, FREE + b)
                    for kt in range(MT):
                        m0 = kt * (MK - 1)
                        ins = pe.transpose(pt[h % 2][0:MK, kt * S:kt * S + S], probs[h % 4][:, m0:m0 + MK], ident[0:S, 0:S])
                    ins.then_inc(turned, 1)

                def weigh(b, par_b, h):
                    pe.wait_ge(copied[h % 2], FREE + 8 * b + h // 2 + 1)
                    if h == 0:
                        pe.wait_ge(x_taken, FREE + 5 * b + 5)
                        pe.wait_ge(normed, 1 + b + 1)
                    for kt in range(MT):
                        c0 = h * CHD
                        ins = pe.matmul(ob[0:S, c0:c0 + CHD], probs_t[h % 2][:, kt * S:kt * S + S], cv[par_b][:, kt, h * CHD:h * CHD + CHD],
                                        start=kt == 0, stop=kt == MT - 1)
                    ins.then_inc(weighted, 1)

                def turn_rows(b, rows_after=0):
                    pe.wait_ge(normed, TWO + b + 1)
                    pe.wait_ge(copied[0], FREE + 8 * b + 8 + rows_after)
                    for t in range(2):
                        ins = pe.transpose(pt[0][:, XT + t * S:XT + t * S + S], rows[:, 8 * t:8 * t + 8, :].rearrange("p h e -> p (h e)"),
                                           ident[0:S, 0:S])
                    ins.then_inc(rows_turned, 1)

                def batch(b, par_b, first):
                    for h in range(NH):
                        score(b, par_b, h)
                        if h == 13 and not first:
                            turn_rows(b - 1, 5)
                        hh, back = before(h, TURN)
                        if not (first and back):
                            turn(b - back, hh)
                        hh, back = before(h, WEIGH)
                        if not (first and back):
                            weigh(b - back, par_b ^ back, hh)
                        if 2 <= h < 12:
                            make_kv(b + 1, (h - 2) // 2, (h % 2,))

                pe.wait_ge(w_ready, 1)
                for r in range(5):
                    make_kv(0, r)
                batch(0, 0, True)
                batch(1, 1, False)
                with pe.Fori(1, B // 2) as c:
                    for par_b in range(2):
                        batch(2 * c + par_b, par_b, False)
                for h in range(NH, NH + WEIGH):
                    if h - TURN < NH:
                        turn(B - 1, h - TURN)
                    weigh(B - 1, 1, h - WEIGH)
                turn_rows(B - 1)

            @block.scalar
            def _(act):
                def split_context(b):
                    act.wait_ge(ctx_loaded, 16 * (b + 1))
                    if not isinstance(b, int) or b > 0:
                        act.wait_ge(x_ready, 5 * b)
                        act.wait_ge(ctx_ready, FREE + b)
                    act.activation(ctx_hi[:, :, :], ctx_raw[:, :, :], ACT.Copy).then_inc(ctx_high, 1)

                def take_keys(b, par_b, r):
                    act.wait_ge(x_ready, 5 * b + r + 1)
                    act.activation(ck_hi[par_b][:, r, :], xb[:, 0:MP], ACT.Copy).then_inc(ck_high, 1)

                def copy_turned(b, h):
                    act.wait_ge(turned, 4 + NH * b + h + 1)
                    act.wait_ge(weighted, 1 + NH * b + h)
                    act.activation(probs_t[1][:, :], pt[1][0:MK, 0:MT * S], ACT.Copy).then_inc(copied[1], 1)

                def exp(b, par_b, h):
                    act.wait_ge(maxed, NH * b + h + 1)
                    act.wait_ge(turned, 1 + NH * b + h)
                    if h == 0:
                        act.wait_ge(normed, 1 + b)
                    act.activation(probs[h % 4][:, :], sc[h % 4][0:S, 0:M], ACT.Exp, bias=neg_max[h % 4][:, :],
                                   accum_out=den[par_b][:, h:h + 1]).then_inc(exped, 1)

                def batch(b, par_b, first):
                    for h in range(NH):
                        hh, back = before(h, TURN)
                        if hh % 2 and not (first and back):
                            copy_turned(b - back, hh)
                        exp(b, par_b, h)
                        if h in (3, 5):
                            take_keys(b + 1, 1 - par_b, (h - 3) // 2)
                        if h == 12:
                            split_context(b + 2)

                act.wait_ge(w_loaded, 16)
                act.activation(w_hi[:, :, :], w_kv[:, :, :], ACT.Copy).then_inc(w_high, 1)
                split_context(0)
                for t in range(2):
                    act.activation(q_parts[:, t, 0], cq[:, t], ACT.Copy).then_inc(q_high, 1)
                for r in range(2):
                    take_keys(0, 0, r)
                split_context(1)
                batch(0, 0, True)
                batch(1, 1, False)
                with act.Fori(1, B // 2) as c:
                    for par_b in range(2):
                        batch(2 * c + par_b, par_b, False)
                for h in range(NH - TURN, NH):
                    if h % 2:
                        copy_turned(B - 1, h)

            @block.vector
            def _(dve):
                def take_kv(b, par_b, r):
                    dve.wait_ge(x_ready, 5 * b + r + 1)
                    if r < 2:
                        dve.wait_ge(ck_high, 2 * b + r + 1)
                        ins = dve.tensor_tensor(ck_lo[par_b][:, r, :], xb[:, 0:MP], ck_hi[par_b][:, r, :].bitcast(F32), ALU.subtract)
                    else:
                        ins = dve.tensor_scalar(cv[par_b][:, r - 2, :], xb[0:MK, 0:CC], con[0:MK, C_ROW + r - 2:C_ROW + r - 1], None, ALU.mult)
                    ins.then_inc(x_taken, 1)

                def row_max(b, h):
                    dve.wait_ge(scored, 4 + NH * b + h + 1)
                    dve.wait_ge(exped, 1 + NH * b + h)
                    dve.tensor_reduce(neg_max[h % 4][:, :], sc[h % 4][0:S, 0:M], AX_X, ALU.max, negate=True).then_inc(maxed, 1)

                def copy_turned(b, h):
                    dve.wait_ge(turned, 4 + NH * b + h + 1)
                    dve.wait_ge(weighted, 1 + NH * b + h)
                    dve.tensor_copy(probs_t[0][:, :], pt[0][0:MK, 0:MT * S]).then_inc(copied[0], 1)

                def normalise(b, par_b):
                    dve.wait_ge(weighted, 2 + NH * (b + 1))
                    dve.wait_ge(rows_turned, FREE + b)
                    dve.reciprocal(rden[par_b][:, :], den[par_b][:, :]).then_inc(inverted, 1)
                    dve.wait_ge(inverted, b + 1)
                    dve.tensor_tensor(rows[:, :, :], ob[0:S, 0:CC].rearrange("p (h e) -> p h e", h=NH),
                                      rden[par_b][:, :].unsqueeze(2).to_broadcast([S, NH, CHD]), ALU.mult).then_inc(normed, 1)

                def store(b):
                    dve.wait_ge(rows_turned, FREE + b + 1)
                    dve.tensor_copy(cctx[:, :, b, :], pt[0][:, XT:XT + 2 * S].rearrange("p (t s) -> p t s", t=2)).then_inc(stored, 1)

                def batch(b, par_b, first):
                    for h in range(NH):
                        row_max(b, h)
                        hh, back = before(h, TURN)
                        if hh % 2 == 0 and not (first and back):
                            copy_turned(b - back, hh)
                        if h == 3 and not first:
                            normalise(b - 1, 1 - par_b)
                        if h in (3, 5, 7, 9, 11):
                            take_kv(b + 1, 1 - par_b, (h - 3) // 2)
                        if h == 13 and not first:
                            store(b - 1)

                for free in (ctx_ready, x_taken, stored, rows_turned, *copied):
                    dve.sem_inc(free, FREE)
                for free in (normed, weighted):
                    dve.sem_inc(free, TWO)
                for free in (scored, exped, turned):
                    dve.sem_inc(free, 4)
                for t in range(2):
                    dve.wait_ge(q_high, t + 1)
                    dve.tensor_tensor(q_parts[:, t, 1], cq[:, t], q_parts[:, t, 0].bitcast(F32), ALU.subtract).then_inc(q_split, 1)
                for r in range(5):
                    take_kv(0, 0, r)
                batch(0, 0, True)
                batch(1, 1, False)
                with dve.Fori(1, B // 2) as c:
                    for par_b in range(2):
                        batch(2 * c + par_b, par_b, False)
                for h in range(NH - TURN, NH):
                    if h % 2 == 0:
                        copy_turned(B - 1, h)
                normalise(B - 1, 1)
                store(B - 1)


def memory_attention(nc, sem, sbuf, d, gT, am, bank, con, ident):
    MP = M + 1
    with ExitStack() as st:
        def two(name, shape, dt=F32):
            return [sbuf(st, f"{name}{i}", shape, dt) for i in range(2)]

        raw, hi, lo = two("raw", [P, 2, MP]), two("hi", [P, 2, MP], F32R), two("lo", [P, 2, MP], F32R)
        rows = two("rows", [MK, MT, CC])
        g_tmp, g_hi, g_lo = two("g_tmp", [P, 2, S]), two("g_hi", [P, 2, S], F32R), two("g_lo", [P, 2, S], F32R)
        neg_max, probs, probs_t = two("neg_max", [S, 1]), two("probs", [S, M]), two("probs_t", [MK, MT * S])
        rden = two("rden", [P, S])
        row_ones = sbuf(st, "row_ones", [MK, MT, P])
        sc, pt, ob = bank[0:2], bank[2:4], bank[4:6]
        loaded, rows_loaded, high, low, g_made, g_high, g_low, scored, maxed, exped, turned, copied, weighted, inverted, normed = (
            [sem(x), sem(x)] for x in ("loaded", "rows_loaded", "high", "low", "g_made", "g_high", "g_low", "scored", "maxed", "exped",
                                       "turned", "copied", "weighted", "inverted", "normed"))
        ones_ready, passed = sem("ones_ready"), sem("passed")
        with nc.Block() as block:
            @block.sync
            def _(sp):
                with sp.Fori(0, B // 2) as c:
                    for r in range(2):
                        sp.wait_ge(low[r], FREE + c)
                        sp.dma_start(raw[r][:, :, :], d["ctx_t"][2 * c + r]).then_inc(loaded[r], 16)
                        sp.wait_ge(weighted[r], FREE + c)
                        sp.dma_start(rows[r][:, :, :], d["ctx_rows"][2 * c + r]).then_inc(rows_loaded[r], 16)

            @block.gpsimd
            def _(pool):
                with pool.Fori(0, B // 2) as c:
                    for r in range(2):
                        wait_apart(pool, passed, g_low[r], FREE + c)
                        pool.tensor_tensor(g_tmp[r][:, :, :], gT[:, :, 2 * c + r, :],
                                           con[:, C_SCALE:C_SCALE + 1].unsqueeze(2).to_broadcast([P, 2, S]), ALU.mult).then_inc(g_made[r], 1)
                        wait_apart(pool, passed, high[r], c + 1)
                        pool.tensor_tensor(lo[r][:, :, :], raw[r][:, :, :], hi[r][:, :, :].bitcast(F32), ALU.subtract).then_inc(low[r], 1)
                        wait_apart(pool, passed, g_high[r], c + 1)
                        pool.tensor_tensor(g_lo[r][:, :, :], g_tmp[r][:, :, :], g_hi[r][:, :, :].bitcast(F32), ALU.subtract).then_inc(g_low[r], 1)

            @block.scalar
            def _(act):
                def split(c, r):
                    act.wait_ge(loaded[r], 16 * (c + 1))
                    act.wait_ge(scored[r], FREE + c)
                    act.activation(hi[r][:, :, :], raw[r][:, :, :], ACT.Copy).then_inc(high[r], 1)
                    act.wait_ge(g_made[r], c + 1)
                    act.activation(g_hi[r][:, :, :], g_tmp[r][:, :, :], ACT.Copy).then_inc(g_high[r], 1)

                def exps(c, r):
                    act.wait_ge(maxed[r], c + 1)
                    act.wait_ge(turned[r], FREE + c)
                    act.activation(probs[r][:, :], sc[r][0:S, 0:M], ACT.Exp, bias=neg_max[r][:, :]).then_inc(exped[r], 1)

                split(0, 0)
                with act.Fori(0, B // 2 - 1) as c:
                    split(c, 1)
                    exps(c, 0)
                    split(c + 1, 0)
                    exps(c, 1)
                split(B // 2 - 1, 1)
                exps(B // 2 - 1, 0)
                exps(B // 2 - 1, 1)

            @block.tensor
            def _(pe):
                def score(c, r):
                    pe.wait_ge(low[r], FREE + c + 1)
                    pe.wait_ge(g_low[r], FREE + c + 1)
                    pe.wait_ge(exped[r], FREE + c)
                    for kt in range(2):
                        for n, (g, m) in enumerate(((g_hi, hi), (g_lo, hi), (g_hi, lo))):
                            ins = pe.matmul(sc[r][0:S, 0:MP], g[r][:, kt, :], m[r][:, kt, :], start=kt == 0 and n == 0, stop=kt == 1 and n == 2)
                    ins.then_inc(scored[r], 1)

                def turn(c, r):
                    pe.wait_ge(exped[r], FREE + c + 1)
                    pe.wait_ge(copied[r], FREE + c)
                    for kt in range(MT):
                        ins = pe.transpose(pt[r][0:MK, kt * S:kt * S + S], probs[r][:, kt * (MK - 1):kt * (MK - 1) + MK], ident[0:S, 0:S])
                    ins.then_inc(turned[r], 1)

                def weigh(c, r):
                    pe.wait_ge(copied[r], FREE + c + 1)
                    pe.wait_ge(rows_loaded[r], 16 * (c + 1))
                    pe.wait_ge(normed[r], FREE + c)
                    for m in range(3):
                        for kt in range(MT):
                            w = rows[r][:, kt, m * P:m * P + P] if m < 2 else row_ones[:, kt, :]
                            ins = pe.matmul(ob[r][:, m * S:m * S + S], w, probs_t[r][:, kt * S:kt * S + S], start=kt == 0, stop=kt == MT - 1)
                    ins.then_inc(weighted[r], 1)

                pe.wait_ge(ones_ready, MT)
                score(0, 0)
                score(0, 1)
                turn(0, 0)
                with pe.Fori(1, B // 2) as c:
                    score(c, 0)
                    turn(c - 1, 1)
                    weigh(c - 1, 0)
                    score(c, 1)
                    turn(c, 0)
                    weigh(c - 1, 1)
                last = B // 2 - 1
                turn(last, 1)
                weigh(last, 0)
                weigh(last, 1)

            @block.vector
            def _(dve):
                def row_max(c, r):
                    dve.wait_ge(scored[r], FREE + c + 1)
                    dve.wait_ge(exped[r], FREE + c)
                    dve.tensor_reduce(neg_max[r][:, :], sc[r][0:S, 0:M], AX_X, ALU.max, negate=True).then_inc(maxed[r], 1)

                def copy_turned(c, r):
                    dve.wait_ge(turned[r], FREE + c + 1)
                    dve.wait_ge(weighted[r], FREE + c)
                    dve.tensor_copy(probs_t[r][:, :], pt[r][0:MK, 0:MT * S]).then_inc(copied[r], 1)

                def normalise(c, r):
                    dve.wait_ge(weighted[r], FREE + c + 1)
                    dve.reciprocal(rden[r][:, :], ob[r][:, 2 * S:3 * S]).then_inc(inverted[r], 1)
                    dve.wait_ge(inverted[r], c + 1)
                    dve.tensor_tensor(am[:, :, 2 * c + r, :], ob[r][:, 0:2 * S].rearrange("p (m s) -> p m s", m=2),
                                      rden[r][:, :].unsqueeze(1).to_broadcast([P, 2, S]), ALU.mult).then_inc(normed[r], 1)

                for free in (*low, *g_low, *scored, *exped, *turned, *copied, *weighted, *normed):
                    dve.sem_inc(free, FREE)
                for kt in range(MT):
                    dve.tensor_scalar(row_ones[:, kt, :], con[0:MK, C_ONE:C_ONE + P], con[0:MK, C_ROW + kt:C_ROW + kt + 1], None,
                                      ALU.mult).then_inc(ones_ready, 1)
                row_max(0, 0)
                row_max(0, 1)
                copy_turned(0, 0)
                with dve.Fori(1, B // 2) as c:
                    row_max(c, 0)
                    copy_turned(c - 1, 1)
                    normalise(c - 1, 0)
                    row_max(c, 1)
                    copy_turned(c, 0)
                    normalise(c - 1, 1)
                last = B // 2 - 1
                copy_turned(last, 1)
                normalise(last, 0)
                normalise(last, 1)


def fusion(nc, sem, end_stage, sbuf, d, linear, splitter, store_batch_major, pair_of_splits, bank, hT, con, wcol, ident, ones, out):
    with ExitStack() as st:
        mc = sbuf(st, "mc", [P, KT, N])
        with ExitStack() as s1:
            gT = sbuf(s1, "gT", [P, 2, B, S])
            am = sbuf(s1, "am", [P, 2, B, S])
            for half in range(2):
                with ExitStack() as s2:
                    x = pair_of_splits(s2, "x", KT)
                    linear("mem_query", d["w_mem"], 1, KT, 1, (x,), store_batch_major(gT, half * 2 * G),
                           splitter(hT, (x,), KT, half * 2 * G, masked=False))
            memory_attention(nc, sem, sbuf, d, gT, am, bank, con, ident)
            end_stage()

            def store_context(first):
                def epilogue(env):
                    def emit(mine, copy):
                        def f(eng, p, s, g):
                            if s != mine:
                                return
                            i = 2 * s + g
                            eng.wait_ge(env["ready"][i], p + 1)
                            copy(eng, mc[:, 2 * p + s, first + g * G:first + g * G + G], bank[i][:, 0:G]).then_inc(env["taken"][i], 1)
                        return f
                    return dict(act=emit(0, lambda e, o, i: e.activation(o, i, ACT.Copy)), dve=emit(1, lambda e, o, i: e.tensor_copy(o, i)))
                return epilogue

            for half in range(2):
                with ExitStack() as s2:
                    x = pair_of_splits(s2, "x", 2)
                    linear("mem_out", d["w_mem_t"], 2, 2, 1, (x,), store_context(half * 2 * G),
                           splitter(am, (x,), 2, half * 2 * G, batch_major=True, masked=False))

        def gate_and_fuse(first):
            def epilogue(env):
                gate = [sbuf(env["st"], f"gate{i}", [P, G]) for i in range(4)]
                gated, fused = [sem("gated") for _ in range(4)], [sem("fused") for _ in range(4)]
                env["open"] = fused

                def act(eng, p, s, g):
                    i = 2 * s + g
                    eng.wait_ge(env["ready"][i], p + 1)
                    eng.wait_ge(fused[i], FREE + p)
                    eng.activation(gate[i][:, :], bank[i][:, 0:G], ACT.Sigmoid, bias=bias[:, 2 * p + s]).then_inc(env["taken"][i], 1)

                def dve(eng, p, s, g):
                    i = 2 * s + g
                    cols = slice(first + g * G, first + g * G + G)
                    eng.wait_ge(env["taken"][i], FREE + p + 1)
                    eng.tensor_tensor(gate[i][:, :], gate[i][:, :], mc[:, 2 * p + s, cols], ALU.mult).then_inc(gated[i], 1)
                    eng.wait_ge(gated[i], p + 1)
                    h = hT[:, 2 * p + s, cols]
                    eng.tensor_tensor(h, h, gate[i][:, :], ALU.add).then_inc(fused[i], 1)

                bias = wcol[:, W_BIAS:W_BIAS + KT].rearrange("p (k o) -> p k o", o=1)
                return dict(act=act, dve=dve)
            return epilogue

        for half in range(2):
            with ExitStack() as s2:
                x = pair_of_splits(s2, "x", 2 * KT)
                linear("gate", d["w_gate"], 2, 2 * KT, 1, (x,), gate_and_fuse(half * 2 * G),
                       splitter(hT, (x,), 2 * KT, half * 2 * G, masked=False, more=mc))

    with ExitStack() as st:
        sq = [sbuf(st, f"sq{i}", [P, G]) for i in range(2)]
        rms = [sbuf(st, f"rms{i}", [P, G]) for i in range(2)]
        y = sbuf(st, "y", [P, KT, N])
        squared, summed, root, inverse, scaled, stored = (sem(x) for x in ("squared", "summed", "root", "inverse", "scaled", "stored"))
        with nc.Block() as block:
            @block.scalar
            def _(act):
                for g in range(NG):
                    for kt in range(KT):
                        n = g * KT + kt
                        if n >= 2:
                            act.wait_ge(summed, n - 1)
                        act.activation(sq[kt % 2][:, :], hT[:, kt, g * G:g * G + G], ACT.Square).then_inc(squared, 1)
                    act.wait_ge(summed, (g + 1) * KT)
                    if g >= 2:
                        act.wait_ge(scaled, (g - 1) * KT)
                    act.activation(rms[g % 2][:, :], bank[g % 2][:, 0:G], ACT.Sqrt, bias=con[:, C_EPS:C_EPS + 1], scale=1.0 / H).then_inc(root, 1)

            @block.tensor
            def _(pe):
                for g in range(NG):
                    if g >= 2:
                        pe.wait_ge(root, g - 1)
                    for kt in range(KT):
                        pe.wait_ge(squared, g * KT + kt + 1)
                        pe.matmul(bank[g % 2][:, 0:G], ones, sq[kt % 2][:, :], start=kt == 0, stop=kt == KT - 1).then_inc(summed, 1)

            @block.vector
            def _(dve):
                for g in range(NG):
                    dve.wait_ge(root, g + 1)
                    dve.reciprocal(rms[g % 2][:, :], rms[g % 2][:, :]).then_inc(inverse, 1)
                    dve.wait_ge(inverse, g + 1)
                    for kt in range(KT):
                        dve.scalar_tensor_tensor(out=y[:, kt, g * G:g * G + G], in0=hT[:, kt, g * G:g * G + G],
                                                 scalar=wcol[:, W_OUT + kt:W_OUT + kt + 1], in1=rms[g % 2][:, :],
                                                 op0=ALU.mult, op1=ALU.mult).then_inc(scaled, 1)

            @block.sync
            def _(sp):
                for g in range(NG):
                    sp.wait_ge(scaled, (g + 1) * KT)
                    sp.dma_start(out[:, :, g * G:g * G + G], y[:, :, g * G:g * G + G]).then_inc(stored, 16)
                sp.wait_ge(stored, 16 * NG)


def kernel(**inputs):
    import concourse.bacc as _bacc
    from concourse.bass_utils import run_bass_kernel_spmd as _run

    a = {k: np.ascontiguousarray(v) for k, v in inputs.items()}

    def tiles(w):
        k, m = w.shape
        return w.reshape(k // P, P, m // P, P).transpose(2, 1, 0, 3)

    def experts(v, l):
        return np.stack([tiles(l), tiles(v)], axis=2)

    def padded(w, axis):
        pad = [(0, 0), (0, 0)]
        pad[axis] = (0, IT * P - w.shape[axis])
        return np.pad(w, pad)

    L0, L1 = "L0_xattn_", "L1_xattn_"
    ctx = a["ctx_1024"]
    ctx_t = np.pad(ctx.reshape(B, M, 2, P).transpose(0, 3, 2, 1), ((0, 2), (0, 0), (0, 0), (0, 1)))
    rows = np.zeros((B, MK, MT, CC), ctx.dtype)
    for kt in range(MT):
        lo = 0 if kt == 0 else 1
        rows[:, lo:, kt] = ctx[:, kt * (MK - 1) + lo:kt * (MK - 1) + MK]
    gu = np.stack([experts(padded(a[L0 + "v_" + n], 1), padded(a[L0 + "l_" + n], 1)) for n in ("gate", "up")], axis=1)
    down = np.stack([tiles(padded(a[L0 + n + "_down"], 0)) for n in ("l", "v")], axis=1)
    ckv = a[L0 + "ckv_w"]
    con, causal = shape_constants()
    vec = [a[L0 + "ln_in_w"], a[L0 + "ln_post_cross_w"], a[L0 + "ln_post_attn_w"], a[L1 + "norm_w"], a[L1 + "b_gate"]]
    arrays = {
        "x": a["x"].transpose(2, 1, 0).reshape(KT, P, N).transpose(1, 0, 2),
        "tok": a["mask_BxS_ik0"].T.reshape(N),
        "pos": a["pos_1xS"].reshape(S),
        "con": con,
        "causal": causal,
        "wcol": np.concatenate([v.reshape(KT, P).T for v in vec], axis=1),
        "w_qkv": experts(a[L0 + "v_qkv"], a[L0 + "l_qkv"]).reshape(12, P, -1),
        "w_dense": experts(a[L0 + "v_dense"], a[L0 + "l_dense"]).reshape(4, P, -1),
        "w_cq": tiles(a[L0 + "cq_w"]).reshape(2, P, -1),
        "w_ckv": ckv.reshape(2, P, 2 * CC).transpose(1, 0, 2),
        "w_cd": tiles(a[L0 + "cdense_w"]).reshape(4, P, -1),
        "w_gu": gu.reshape(2 * IT, P, -1),
        "w_down": down.reshape(8, P, -1),
        "w_mem": tiles(a[L1 + "W_mem"]).reshape(2, P, -1),
        "w_mem_t": tiles(np.ascontiguousarray(a[L1 + "W_mem"].T)).reshape(4, P, -1),
        "w_gate": tiles(np.ascontiguousarray(a[L1 + "W_gate"].T)).reshape(4, P, -1),
        "ctx_t": ctx_t,
        "ctx_rows": rows,
    }
    arrays = {f"in_{k}": np.ascontiguousarray(v) for k, v in arrays.items()}
    nc = _bacc.Bacc("TRN2", target_bir_lowering=False, num_devices=1)
    d = {k[3:]: nc.dram_tensor(k, v.shape, mybir.dt.from_np(v.dtype), kind="ExternalInput").ap() for k, v in arrays.items()}
    out = nc.dram_tensor("out_0", (P, KT, N), F32, kind="ExternalOutput").ap()
    build(nc, d, out)
    got = _run(nc, [arrays], core_ids=[0]).results[0]["out_0"]
    return np.ascontiguousarray(got.transpose(1, 0, 2).reshape(H, S, B).transpose(2, 1, 0))
```

```python
from contextlib import ExitStack

import numpy as np

import concourse.bass as bass
from concourse import mybir

F32 = mybir.dt.float32
F32R = mybir.dt.float32r
BF16 = mybir.dt.bfloat16
I32 = mybir.dt.int32
ALU = mybir.AluOpType
ACT = mybir.ActivationFunctionType
AX_X = mybir.AxisListType.X

B, S, H = 16, 100, 512
N = B * S
P = 128
KT = H // P
NH, HD = 16, 32
CC, CHD = 256, 16
M = 361
MK, MT = 121, 3
IT = 11
G = 400
NG = N // G
GP = G // B
EPS = 1e-6
FREE, TWO = 1, 2

C_ID, C_ONE, C_M4, C_M8, C_COS, C_SIN, C_IDX, C_ROW, C_EPS, C_ZERO, C_END = 0, 128, 256, 260, 268, 396, 524, 525, 528, 529, 657
W_IN, W_CROSS, W_ATTN, W_OUT, W_BIAS = 0, 4, 8, 12, 16


def shape_constants():
    c = np.zeros((P, C_END), np.float32)
    c[:, C_ID:C_ID + P] = np.eye(P)
    c[:, C_ONE:C_ONE + P] = 1.0
    p = np.arange(P)
    for j in range(4):
        c[:, C_M4 + j] = (p // HD == j) * np.float32(1.0 / np.sqrt(HD))
    for j in range(8):
        c[:, C_M8 + j] = (p // CHD == j) * np.float32(1.0 / np.sqrt(CHD))
    inv = (1.0 / np.power(np.float32(10000.0), np.arange(0, HD, 2, dtype=np.float32) / np.float32(HD))).astype(np.float32)
    angle = np.outer(np.arange(S, dtype=np.float32), inv).astype(np.float32)
    d = p % HD
    c[:S, C_COS:C_COS + P] = np.cos(angle)[:, d % (HD // 2)]
    c[:S, C_SIN:C_SIN + P] = np.sin(angle)[:, d % (HD // 2)] * np.where(d < HD // 2, -1.0, 1.0)[None, :]
    c[:, C_IDX] = p
    c[:, C_ROW:C_ROW + MT] = 1.0
    c[0, C_ROW + 1:C_ROW + MT] = 0.0
    c[:, C_EPS] = EPS
    causal = np.zeros((S, 4, S), np.float32)
    causal[:] = np.where(np.tril(np.ones((S, S), bool)), 0.0, -3.0e38)[:, None, :]
    return c, causal.reshape(S, 4 * S)


def build(nc, d, out):
    ctx = ExitStack()
    n_sem = [0]

    stage_sems = []

    def sem(name):
        n_sem[0] += 1
        stage_sems.append(nc.alloc_semaphore(name=f"{name}_{n_sem[0]}"))
        return stage_sems[-1]

    def end_stage():
        nc.clear_and_free_semaphores(stage_sems)
        nc.all_engine_barrier()
        stage_sems.clear()

    def sbuf(stack, name, shape, dt=F32):
        n_sem[0] += 1
        return stack.enter_context(nc.sbuf_tensor(f"{name}_{n_sem[0]}", shape, dt))

    with ctx:
        bank = [ctx.enter_context(nc.psum_tensor(f"bank{i}", [P, 512], F32)) for i in range(8)]
        hT = sbuf(ctx, "hT", [P, KT, N])
        is_v = sbuf(ctx, "is_v", [P, N])
        is_l = sbuf(ctx, "is_l", [P, N])
        con = sbuf(ctx, "con", [P, C_END])
        wcol = sbuf(ctx, "wcol", [P, 20])
        cosT = sbuf(ctx, "cosT", [P, S])
        sinT = sbuf(ctx, "sinT", [P, S])
        flag = sbuf(ctx, "flag", [P, NG], I32)
        ident = con[:, C_ID:C_ID + P]
        ones = con[:, C_ONE:C_ONE + P]

        with ExitStack() as st:
            tok = sbuf(st, "tok", [P, N], I32)
            tokf = sbuf(st, "tokf", [P, N])
            posi = sbuf(st, "posi", [S, S], I32)
            posf = sbuf(st, "posf", [S, S])
            wrap = sbuf(st, "wrap", [S, S])
            hot = sbuf(st, "hot", [S, S])
            flagf = sbuf(st, "flagf", [P, NG])
            loaded, x_loaded, step, hot_ready, table, copied = (
                sem(x) for x in ("loaded", "x_loaded", "step", "hot_ready", "table", "copied"))
            with nc.Block() as block:
                @block.sync
                def _(sp):
                    sp.dma_start(con[:, :], d["con"]).then_inc(loaded, 16)
                    sp.dma_start(wcol[:, :], d["wcol"]).then_inc(loaded, 16)
                    sp.dma_start(tok[:, :], d["tok"].partition_broadcast(P)).then_inc(loaded, 16)
                    sp.dma_start(posi[:, :], d["pos"].partition_broadcast(S)).then_inc(loaded, 16)
                    sp.dma_start(hT[:, :, :], d["x"]).then_inc(x_loaded, 16)
                    sp.wait_ge(x_loaded, 16)

                @block.vector
                def _(dve):
                    n = [0]

                    def after(ins):
                        n[0] += 1
                        ins.then_inc(step, 1)
                        dve.wait_ge(step, n[0])

                    dve.wait_ge(loaded, 64)
                    after(dve.tensor_copy(posf[:, :], posi[:, :]))
                    after(dve.tensor_scalar(wrap[:, :], posf[:, :], 0.0, float(S), ALU.is_lt, ALU.mult))
                    after(dve.tensor_tensor(posf[:, :], posf[:, :], wrap[:, :], ALU.add))
                    after(dve.tensor_scalar(posf[:, :], posf[:, :], 0.0, float(S - 1), ALU.max, ALU.min))
                    dve.tensor_scalar(hot[:, :], posf[:, :], con[0:S, C_IDX:C_IDX + 1], None, ALU.is_equal).then_inc(hot_ready, 1)
                    after(dve.tensor_scalar(tokf[:, :], tok[:, :], 1.0, None, ALU.is_equal))
                    after(dve.tensor_tensor(is_v[:, 0:N - B], tokf[:, 0:N - B], tokf[:, B:N], ALU.mult))
                    after(dve.memset(is_v[:, N - B:N], 0.0))
                    dve.tensor_scalar(is_l[:, :], is_v[:, :], -1.0, 1.0, ALU.mult, ALU.add)
                    after(dve.tensor_reduce(flagf[:, :], is_v[:, :].rearrange("p (g c) -> p g c", g=NG), AX_X, ALU.max))
                    after(dve.tensor_copy(flag[:, :], flagf[:, :]))
                    dve.wait_ge(table, 1)
                    dve.tensor_copy(cosT[:, :], bank[0][:, 0:S]).then_inc(copied, 1)
                    dve.tensor_copy(sinT[:, :], bank[0][:, S:2 * S]).then_inc(copied, 1)
                    dve.wait_ge(copied, 2)

                @block.tensor
                def _(pe):
                    pe.wait_ge(hot_ready, 1)
                    pe.matmul(bank[0][:, 0:S], con[0:S, C_COS:C_COS + P], hot[:, :], start=True, stop=True)
                    pe.matmul(bank[0][:, S:2 * S], con[0:S, C_SIN:C_SIN + P], hot[:, :], start=True, stop=True).then_inc(table, 1)

        end_stage()

        def linear(name, w, pairs, nk, ne, operand, epilogue, prepare=None, first_flag=0, vision_slot=False, groups=2):
            R = ne * nk * P
            with ExitStack() as st:
                raw = [sbuf(st, f"raw{s}", [P, R]) for s in range(2)]
                whi = [sbuf(st, f"whi{s}", [P, R], F32R) for s in range(2)]
                wlo = [sbuf(st, f"wlo{s}", [P, R], F32R) for s in range(2)]
                w_loaded = [sem("w_loaded") for _ in range(2)]
                w_hi = [sem("w_hi") for _ in range(2)]
                w_lo = [sem("w_lo") for _ in range(2)]
                w_lo_v = [sem("w_lo_v") for _ in range(2)]
                cut = R * 3 // 8
                ready = [sem("out_ready") for _ in range(2 * groups)]
                taken = [sem("out_taken") for _ in range(2 * groups)]
                env = dict(st=st, ready=ready, taken=taken, operands=[[[] for _ in range(groups)] for _ in range(ne)], groups=groups)
                prep = prepare(env) if prepare else {}
                epi = epilogue(env)

                with nc.Block() as block:
                    @block.sync
                    def _(sp):
                        with sp.Fori(0, pairs) as p:
                            for s in range(2):
                                sp.wait_ge(w_lo[s], FREE + p)
                                sp.wait_ge(w_lo_v[s], FREE + p)
                                sp.dma_start(raw[s][:, :], w[2 * p + s]).then_inc(w_loaded[s], 16)
                        for s in range(2):
                            sp.wait_ge(w_loaded[s], 16 * pairs)

                    @block.gpsimd
                    def _(pool):
                        def split_low(s, p):
                            pool.wait_ge(w_hi[s], p + 1)
                            pool.tensor_tensor(wlo[s][:, 0:cut], raw[s][:, 0:cut], whi[s][:, 0:cut].bitcast(F32),
                                               ALU.subtract).then_inc(w_lo[s], 1)

                        for s in range(2):
                            split_low(s, 0)
                        if "pool" in prep:
                            prep["pool"](pool)
                        if pairs > 1:
                            with pool.Fori(1, pairs) as p:
                                for s in range(2):
                                    split_low(s, p)
                        if "pool" in epi:
                            epi["pool"](pool)

                    @block.scalar
                    def _(act):
                        def split_high(s, p):
                            act.wait_ge(w_loaded[s], 16 * (p + 1))
                            act.activation(whi[s][:, :], raw[s][:, :], ACT.Copy).then_inc(w_hi[s], 1)

                        weights = iter([lambda: split_high(0, 0), lambda: split_high(1, 0)])
                        if "act_first" in prep:
                            prep["act_first"](act, weights)
                        for split in weights:
                            split()
                        if "act" in prep:
                            prep["act"](act)

                        def body(p, last):
                            for s in range(2):
                                act.wait_ge(ready[groups * s + groups - 1], p + 1)
                                if not last:
                                    split_high(s, p + 1)
                                for g in range(groups):
                                    epi["act"](act, p, s, g)

                        if pairs > 1:
                            with act.Fori(0, pairs - 1) as p:
                                body(p, False)
                        body(pairs - 1, True)

                    @block.vector
                    def _(dve):
                        def split_low(s, p):
                            dve.wait_ge(w_hi[s], p + 1)
                            dve.tensor_tensor(wlo[s][:, cut:R], raw[s][:, cut:R], whi[s][:, cut:R].bitcast(F32),
                                              ALU.subtract).then_inc(w_lo_v[s], 1)

                        weights = iter([lambda: split_low(0, 0), lambda: split_low(1, 0)])

                        def body(p, last):
                            for s in range(2):
                                if not last:
                                    split_low(s, p + 1)
                                for g in range(groups):
                                    epi["dve"](dve, p, s, g)

                        for free in (*w_lo, *w_lo_v, *taken, *env.get("open", ())):
                            dve.sem_inc(free, FREE)
                        if "dve" in prep:
                            prep["dve"](dve, weights)
                        for split in weights:
                            split()
                        if pairs > 1:
                            with dve.Fori(0, pairs - 1) as p:
                                body(p, False)
                        body(pairs - 1, True)

                    @block.tensor
                    def _(pe):
                        has_v = []
                        if ne == 2 or vision_slot:
                            for g in range(2):
                                has_v.append(pe.value_load(flag[0:1, first_flag + g:first_flag + g + 1], min_val=0, max_val=1))
                        if "pe" in prep:
                            prep["pe"](pe)

                        def products(acc, s, e, g, kts, start, stop):
                            last = None
                            for kt in kts:
                                c = (e * nk + kt) * P
                                cols = slice(g * G, g * G + G)
                                hi, lo = operand[e]
                                terms = ((whi, hi), (wlo, hi), (whi, lo))
                                for n, (wt, x) in enumerate(terms):
                                    last = pe.matmul(acc, wt[s][:, c:c + P], x[:, kt, cols], start=start and kt == kts[0] and n == 0,
                                                     stop=stop and kt == kts[-1] and n == 2, skip_group_check=True)
                            return last

                        with pe.Fori(0, pairs) as p:
                            for s in range(2):
                                pe.wait_ge(w_lo[s], FREE + p + 1)
                                pe.wait_ge(w_lo_v[s], FREE + p + 1)
                                for g in range(groups):
                                    if s == 0:
                                        for operands, count in env["operands"][0][g]:
                                            pe.wait_ge(operands, count)
                                    i = groups * s + g
                                    pe.wait_ge(taken[i], FREE + p)
                                    acc = bank[i][:, 0:G]
                                    if vision_slot and s == 1:
                                        with pe.If(has_v[g] != 0):
                                            products(acc, s, 0, g, range(nk), True, True).then_inc(ready[i], 1)
                                        with pe.Else():
                                            pe.matmul(acc, con[:, C_ZERO:C_ZERO + P], con[:, 0:G], start=True, stop=True,
                                                      skip_group_check=True).then_inc(ready[i], 1)
                                        continue
                                    products(acc, s, 0, g, range(nk - 1), True, False)
                                    if ne == 2:
                                        with pe.If(has_v[g] != 0):
                                            if s == 0:
                                                for operands, count in env["operands"][1][g]:
                                                    pe.wait_ge(operands, count)
                                            products(acc, s, 1, g, range(nk), False, False)
                                    products(acc, s, 0, g, range(nk - 1, nk), False, True).then_inc(ready[i], 1)

            end_stage()

        def splitter(source, operand, nk, first, norm=None, batch_major=False, masked=True, more=None, groups=2):
            ne = 2 if masked else 1

            def columns(kt, g):
                c0 = first + g * G
                if batch_major:
                    return source[:, kt, :, c0 // B:c0 // B + GP].rearrange("p b s -> p s b")
                if kt >= KT:
                    return more[:, kt - KT, c0:c0 + G]
                return source[:, kt, c0:c0 + G]

            def shaped(ap):
                return ap.rearrange("p (s b) -> p s b", b=B) if batch_major else ap

            def prepare(env):
                st = env["st"]
                steps = [(g, kt, e) for e in range(ne) for g in range(groups) for kt in range(nk)]
                D = 3
                tmp = [sbuf(st, f"tmp{i}", [P, G]) for i in range(D)]
                made, high = sem("made"), sem("high")
                low_p, low_d = sem("low_by_pool"), sem("low_by_vector")

                def by_vector(n):
                    return n % 3 == 1

                def low_of(n):
                    mine = [m for m in range(n + 1) if by_vector(m) == by_vector(n)]
                    return (low_d if by_vector(n) else low_p), len(mine)

                for e in range(ne):
                    for g in range(groups):
                        last = (e * groups + g + 1) * nk - 1
                        env["operands"][e][g].append(low_of(last))
                        other = [m for m in range(last) if by_vector(m) != by_vector(last)]
                        if other:
                            env["operands"][e][g].append(low_of(other[-1]))
                if norm is not None:
                    sq = [sbuf(st, f"sq{i}", [P, G]) for i in range(2)]
                    rms = [sbuf(st, f"rms{i}", [P, G]) for i in range(groups)]
                    rs = [sbuf(st, f"rs{i}", [P, G]) for i in range(groups)] if masked else None
                    squared, summed, root, inverse, scaled = (sem(x) for x in ("squared", "summed", "root", "inverse", "scaled"))

                def pe(eng):
                    if norm is None:
                        return
                    for g in range(groups):
                        for kt in range(nk):
                            eng.wait_ge(squared, g * nk + kt + 1)
                            eng.matmul(bank[4 + g][:, 0:G], ones, sq[kt % 2][:, :], start=kt == 0, stop=kt == nk - 1).then_inc(summed, 1)

                def act_first(eng, weights):
                    if norm is None:
                        return
                    for g in range(groups):
                        for kt in range(nk):
                            n = g * nk + kt
                            if n >= 2:
                                eng.wait_ge(summed, n - 1)
                            eng.activation(sq[kt % 2][:, :], columns(kt, g), ACT.Square).then_inc(squared, 1)
                        for split in weights:
                            split()
                            break
                        eng.wait_ge(summed, (g + 1) * nk)
                        eng.activation(rms[g][:, :], bank[4 + g][:, 0:G], ACT.Sqrt, bias=con[:, C_EPS:C_EPS + 1],
                                       scale=1.0 / H).then_inc(root, 1)

                def act(eng):
                    for n, (g, kt, e) in enumerate(steps):
                        eng.wait_ge(made, n + 1)
                        eng.activation(operand[e][0][:, kt, g * G:g * G + G], tmp[n % D][:, :], ACT.Copy).then_inc(high, 1)

                def subtract_high(eng, n, low):
                    g, kt, e = steps[n]
                    hi, lo = operand[e]
                    cols = slice(g * G, g * G + G)
                    eng.wait_ge(high, n + 1)
                    eng.tensor_tensor(lo[:, kt, cols], tmp[n % D][:, :], hi[:, kt, cols].bitcast(F32), ALU.subtract).then_inc(low, 1)

                def dve(eng, weights):
                    if norm is not None:
                        next(weights)()
                    pending = []

                    def flush():
                        for n in pending:
                            subtract_high(eng, n, low_d)
                        pending.clear()

                    for n, (g, kt, e) in enumerate(steps):
                        if kt == 0:
                            flush()
                        if n == D:
                            for split in weights:
                                split()
                        if norm is not None and kt == 0 and e == 0:
                            eng.wait_ge(root, g + 1)
                            eng.reciprocal(rms[g][:, :], rms[g][:, :]).then_inc(inverse, 1)
                            eng.wait_ge(inverse, g + 1)
                        if norm is not None and masked and kt == 0:
                            cols = slice(first + g * G, first + g * G + G)
                            eng.tensor_tensor((rms if e else rs)[g][:, :], rms[g][:, :], (is_v if e else is_l)[:, cols],
                                              ALU.mult).then_inc(scaled, 1)
                            eng.wait_ge(scaled, e * groups + g + 1)
                        if n >= D:
                            eng.wait_ge(*low_of(n - D))
                        if norm is not None:
                            ins = eng.scalar_tensor_tensor(out=tmp[n % D][:, :], in0=columns(kt, g), scalar=wcol[:, norm + kt:norm + kt + 1],
                                                           in1=(rs if masked and not e else rms)[g][:, :], op0=ALU.mult, op1=ALU.mult)
                        elif masked:
                            mask = (is_l, is_v)[e][:, first + g * G:first + g * G + G]
                            ins = eng.tensor_tensor(shaped(tmp[n % D][:, :]), columns(kt, g), shaped(mask), ALU.mult)
                        else:
                            ins = eng.tensor_copy(shaped(tmp[n % D][:, :]), columns(kt, g))
                        ins.then_inc(made, 1)
                        flush()
                        if by_vector(n):
                            pending.append(n)
                    flush()

                def pool(eng):
                    for n in range(len(steps)):
                        if not by_vector(n):
                            subtract_high(eng, n, low_p)

                return dict(pe=pe, act_first=act_first, act=act, dve=dve, pool=pool)

            return prepare

        def store_batch_major(target, first):
            def epilogue(env):
                def emit(eng, mine, copy):
                    def f(eng, p, s, g):
                        if s != mine:
                            return
                        i = env["groups"] * s + g
                        p0 = (first + g * G) // B
                        eng.wait_ge(env["ready"][i], p + 1)
                        copy(eng, target[:, 2 * p + s, :, p0:p0 + GP], bank[i][:, 0:G].rearrange("p (s b) -> p b s", b=B)).then_inc(env["taken"][i], 1)
                    return f
                return dict(act=emit(None, 0, lambda e, o, i: e.activation(o, i, ACT.Copy)),
                            dve=emit(None, 1, lambda e, o, i: e.tensor_copy(o, i)))
            return epilogue

        def store_split(target, first, scale):
            def epilogue(env):
                high = [sem("stored_high") for _ in range(2 * env["groups"])]

                def places(p, s, g):
                    p0 = (first + g * G) // B
                    return (bank[env["groups"] * s + g][:, 0:G].rearrange("p (s b) -> p b s", b=B),
                            *(target[:, 2 * p + s, part, :, p0:p0 + GP] for part in range(2)))

                def act(eng, p, s, g):
                    i = env["groups"] * s + g
                    source, hi, _ = places(p, s, g)
                    eng.wait_ge(env["ready"][i], p + 1)
                    eng.activation(hi, source, ACT.Copy, scale=scale).then_inc(high[i], 1)

                def dve(eng, p, s, g):
                    i = env["groups"] * s + g
                    source, hi, lo = places(p, s, g)
                    eng.wait_ge(high[i], p + 1)
                    eng.scalar_tensor_tensor(out=lo, in0=source, scalar=scale, in1=hi.bitcast(F32), op0=ALU.mult,
                                             op1=ALU.subtract).then_inc(env["taken"][i], 1)
                return dict(act=act, dve=dve)
            return epilogue

        def add_to_residual(first):
            def epilogue(env):
                def dve(eng, p, s, g):
                    i = env["groups"] * s + g
                    c0 = first + g * G
                    eng.wait_ge(env["ready"][i], p + 1)
                    h = hT[:, 2 * p + s, c0:c0 + G]
                    eng.tensor_tensor(h, h, bank[i][:, 0:G], ALU.add).then_inc(env["taken"][i], 1)
                return dict(act=lambda *a: None, dve=dve)
            return epilogue

        def add_masked(first):
            def epilogue(env):
                part = [sbuf(env["st"], f"part{g}", [P, G]) for g in range(2)]
                added = sem("added")

                def dve(eng, p, s, g):
                    i = env["groups"] * s + g
                    cols = slice(first + g * G, first + g * G + G)
                    eng.wait_ge(env["ready"][i], p + 1)
                    eng.tensor_tensor(part[g][:, :], bank[i][:, 0:G], (is_l, is_v)[s][:, cols], ALU.mult).then_inc(env["taken"][i], 1)
                    eng.wait_ge(env["taken"][i], FREE + p + 1)
                    h = hT[:, p, cols]
                    eng.tensor_tensor(h, h, part[g][:, :], ALU.add).then_inc(added, 1)
                    eng.wait_ge(added, 4 * p + 2 * s + g + 1)
                return dict(act=lambda *a: None, dve=dve)
            return epilogue

        def pair_of_splits(st, name, nk, groups=2):
            return tuple(sbuf(st, f"{name}_{part}", [P, nk, groups * G], F32R) for part in ("hi", "lo"))

        with ExitStack() as st:
            qkv = sbuf(st, "qkv", [P, 12, B, S])
            for half in range(2):
                with ExitStack() as s2:
                    xl, xv = pair_of_splits(s2, "xl", KT), pair_of_splits(s2, "xv", KT)
                    linear("qkv", d["w_qkv"], 6, KT, 2, (xl, xv), store_batch_major(qkv, half * 2 * G),
                           splitter(hT, (xl, xv), KT, half * 2 * G, norm=W_IN), first_flag=2 * half)
            rotate(nc, sem, sbuf, qkv, cosT, sinT)
            end_stage()
            self_attention(nc, sem, sbuf, d, qkv, bank, con, ident)
            end_stage()
            for half in range(2):
                with ExitStack() as s2:
                    al, av = pair_of_splits(s2, "al", KT), pair_of_splits(s2, "av", KT)
                    linear("dense", d["w_dense"], 2, KT, 2, (al, av), add_to_residual(half * 2 * G),
                           splitter(qkv, (al, av), KT, half * 2 * G, batch_major=True), first_flag=2 * half)

        with ExitStack() as st:
            cctx = sbuf(st, "cctx", [P, 2, B, S])
            with ExitStack() as s1:
                q_parts = sbuf(s1, "q_parts", [P, 2, 2, B, S], F32R)
                with ExitStack() as s2:
                    x = pair_of_splits(s2, "x", KT, NG)
                    linear("cq", d["w_cq"], 1, KT, 1, (x,), store_split(q_parts, 0, 1.0),
                           splitter(hT, (x,), KT, 0, norm=W_CROSS, masked=False, groups=NG), groups=NG)
                cross_attention(nc, sem, sbuf, d, q_parts, cctx, bank, con, ident)
                end_stage()
            with ExitStack() as s1:
                x = pair_of_splits(s1, "x", 2, NG)
                linear("cdense", d["w_cd"], 2, 2, 1, (x,), add_to_residual(0),
                       splitter(cctx, (x,), 2, 0, batch_major=True, masked=False, groups=NG), groups=NG)

        for half in range(2):
            with ExitStack() as st:
                act_hi = sbuf(st, "act_hi", [P, IT, 2 * G], F32R)
                act_lo = sbuf(st, "act_lo", [P, IT, 2 * G], F32R)

                def gate_times_up(env):
                    silu = [sbuf(env["st"], f"silu{g}", [P, G]) for g in range(2)]
                    prod = [sbuf(env["st"], f"prod{g}", [P, G]) for g in range(2)]
                    prod_ready = [sem("prod_ready") for _ in range(2)]
                    prod_high = [sem("prod_high") for _ in range(2)]
                    prod_low = [sem("prod_low") for _ in range(2)]
                    ready, taken = env["ready"], env["taken"]
                    env["open"] = prod_ready

                    def act(eng, p, s, g):
                        if s == 0:
                            eng.wait_ge(ready[g], p + 1)
                            eng.wait_ge(prod_ready[g], FREE + p)
                            eng.activation(silu[g][:, :], bank[g][:, 0:G], ACT.Silu).then_inc(taken[g], 1)
                        else:
                            eng.wait_ge(prod_ready[g], FREE + p + 1)
                            eng.activation(act_hi[:, p, g * G:g * G + G], prod[g][:, :], ACT.Copy).then_inc(prod_high[g], 1)

                    def dve(eng, p, s, g):
                        if s == 0:
                            return
                        eng.wait_ge(ready[2 + g], p + 1)
                        eng.wait_ge(taken[g], FREE + p + 1)
                        eng.tensor_tensor(prod[g][:, :], silu[g][:, :], bank[2 + g][:, 0:G], ALU.mult).then_inc(prod_ready[g], 1)
                        eng.wait_ge(prod_high[g], p + 1)
                        cols = slice(g * G, g * G + G)
                        eng.tensor_tensor(act_lo[:, p, cols], prod[g][:, :], act_hi[:, p, cols].bitcast(F32), ALU.subtract).then_inc(taken[2 + g], 1)

                    return dict(act=act, dve=dve)

                with ExitStack() as s2:
                    xl, xv = pair_of_splits(s2, "xl", KT), pair_of_splits(s2, "xv", KT)
                    linear("gate_up", d["w_gu"], IT, KT, 2, (xl, xv), gate_times_up,
                           splitter(hT, (xl, xv), KT, half * 2 * G, norm=W_ATTN), first_flag=2 * half)
                linear("down", d["w_down"], 4, IT, 1, ((act_hi, act_lo),), add_masked(half * 2 * G), first_flag=2 * half,
                       vision_slot=True)

        fusion(nc, sem, end_stage, sbuf, d, linear, splitter, store_split, pair_of_splits, bank, hT, con, wcol, ident, ones, out)


def wait_apart(eng, passed, sem, value):
    eng.wait_ge(sem, value)
    eng.sem_inc(passed, 1)


def rotate(nc, sem, sbuf, qkv, cosT, sinT):
    with ExitStack() as st:
        swap = [sbuf(st, f"swap{i}", [P, B, S]) for i in range(2)]
        part = [sbuf(st, f"part{i}", [P, B, S]) for i in range(2)]
        swapped, sined, cosed, pool_cosed, done = (sem(x) for x in ("swapped", "sined", "cosed", "pool_cosed", "done"))
        mask = [(i + HD // 2) % HD for i in range(HD)]
        cos = cosT[:, :].unsqueeze(1).to_broadcast([P, B, S])
        sin = sinT[:, :].unsqueeze(1).to_broadcast([P, B, S])
        by_pool = (2, 5)

        def count(t, pool):
            return sum((i in by_pool) == pool for i in range(t + 1))

        with nc.Block() as block:
            @block.vector
            def _(dve):
                def add(t):
                    dve.wait_ge(sined, t + 1)
                    if t in by_pool:
                        dve.wait_ge(pool_cosed, count(t, True))
                    else:
                        dve.wait_ge(cosed, count(t, False))
                    dve.tensor_tensor(qkv[:, t], swap[t % 2][:, :, :], part[t % 2][:, :, :], ALU.add).then_inc(done, 1)

                for t in range(8):
                    if t >= 2:
                        dve.wait_ge(done, t - 1)
                    dve.stream_shuffle(swap[t % 2][:, :, :], qkv[:, t], mask).then_inc(swapped, 1)
                    if t not in by_pool:
                        dve.tensor_tensor(part[t % 2][:, :, :], qkv[:, t], cos, ALU.mult).then_inc(cosed, 1)
                    if t >= 1:
                        add(t - 1)
                add(7)

            @block.gpsimd
            def _(pool):
                for t in range(8):
                    if t in by_pool:
                        pool.wait_ge(done, t - 1)
                        pool.tensor_tensor(part[t % 2][:, :, :], qkv[:, t], cos, ALU.mult).then_inc(pool_cosed, 1)
                    pool.wait_ge(swapped, t + 1)
                    pool.tensor_tensor(swap[t % 2][:, :, :], swap[t % 2][:, :, :], sin, ALU.mult).then_inc(sined, 1)


def self_attention(nc, sem, sbuf, d, qkv, bank, con, ident):
    T = NH // 4
    with ExitStack() as st:
        def two(name, shape, dt=F32):
            return [sbuf(st, f"{name}{i}", shape, dt) for i in range(2)]

        causal_f = sbuf(st, "causal_f", [S, 4 * S])
        causal = sbuf(st, "causal", [S, 4 * S], BF16)
        ident_b = sbuf(st, "ident_b", [S, S], BF16)
        q_masked = two("q_masked", [P, 4, S])
        v_in = sbuf(st, "v_in", [P, T, S])
        v = two("v", [S, H])
        neg_max, probs, probs_t = two("neg_max", [S, 4]), two("probs", [S, 4, S]), two("probs_t", [S, 4 * S])
        den, rden = two("den", [S, NH]), two("rden", [S, NH])
        rows = sbuf(st, "rows", [S, NH, HD])
        sc, pt, ob, vb, xb = bank[0:2], bank[2:4], bank[4:6], bank[6], bank[7]
        (c_loaded, c_ready, v_in_ready, v_turned, v_ready, q_ready, scored, maxed, exped, turned, copied, weighted, inverted, normed,
         rows_turned, stored, passed) = (
            sem(x) for x in ("c_loaded", "c_ready", "v_in_ready", "v_turned", "v_ready", "q_ready", "scored", "maxed", "exped", "turned",
                             "copied", "weighted", "inverted", "normed", "rows_turned", "stored", "passed"))

        def before(b, t, lag):
            return (b, 0, t - lag) if t >= lag else (b - 1, 1, t - lag + T)

        with nc.Block() as block:
            @block.sync
            def _(sp):
                sp.dma_start(causal_f[:, :], d["causal"]).then_inc(c_loaded, 16)

            @block.gpsimd
            def _(pool):
                with pool.Fori(0, B) as b:
                    wait_apart(pool, passed, v_turned, FREE + b)
                    pool.tensor_copy(v_in[:, :, :], qkv[:, 8:12, b, :]).then_inc(v_in_ready, 1)
                    for t in range(T):
                        wait_apart(pool, passed, scored, 1 + T * b + t)
                        pool.tensor_tensor(q_masked[t % 2][:, :, :], qkv[:, t, b, :].unsqueeze(1).to_broadcast([P, 4, S]),
                                           con[:, C_M4:C_M4 + 4].unsqueeze(2).to_broadcast([P, 4, S]), ALU.mult).then_inc(q_ready, 1)

            @block.tensor
            def _(pe):
                def turn_v(b):
                    pe.wait_ge(v_in_ready, b + 1)
                    pe.wait_ge(v_ready, FREE + b)
                    for t in range(T):
                        ins = pe.transpose(vb[0:S, t * P:t * P + P], v_in[:, t, :], ident)
                    ins.then_inc(v_turned, 1)

                def score(b, t):
                    pe.wait_ge(q_ready, T * b + t + 1)
                    pe.wait_ge(exped, 1 + T * b + t)
                    pe.matmul(sc[t % 2][0:S, 0:4 * S], ident_b[:, :], causal[:, :], start=True, stop=False, skip_group_check=True)
                    for j in range(4):
                        ins = pe.matmul(sc[t % 2][0:S, j * S:j * S + S], q_masked[t % 2][:, j, :], qkv[:, 4 + t, b, :],
                                        start=False, stop=j == 3, skip_group_check=True)
                    ins.then_inc(scored, 1)

                def turn(b, t):
                    pe.wait_ge(exped, TWO + T * b + t + 1)
                    pe.wait_ge(copied, 1 + T * b + t)
                    for j in range(4):
                        ins = pe.transpose(pt[t % 2][0:S, j * S:j * S + S], probs[t % 2][:, j, :], ident[0:S, 0:S])
                    ins.then_inc(turned, 1)

                def weigh(b, r, t):
                    pe.wait_ge(copied, TWO + T * b + t + 1)
                    if t == 0:
                        pe.wait_ge(v_ready, FREE + b + 1)
                        pe.wait_ge(normed, 1 + b)
                    for j in range(4):
                        h = 4 * t + j
                        ins = pe.matmul(ob[r][0:S, h * HD:h * HD + HD], probs_t[t % 2][:, j * S:j * S + S], v[r][:, h * HD:h * HD + HD],
                                        start=True, stop=True)
                    ins.then_inc(weighted, 1)

                def turn_rows(b):
                    pe.wait_ge(normed, TWO + b + 1)
                    pe.wait_ge(stored, FREE + b)
                    for t in range(T):
                        ins = pe.transpose(xb[:, t * S:t * S + S], rows[:, 4 * t:4 * t + 4, :].rearrange("p h e -> p (h e)"), ident[0:S, 0:S])
                    ins.then_inc(rows_turned, 1)

                def batch(b, r, first):
                    for t in range(T):
                        if t == 0:
                            turn_v(b)
                        score(b, t)
                        for lag, step in ((2, "turn"), (3, "weigh")):
                            bb, back, tt = before(b, t, lag)
                            if first and back:
                                continue
                            if step == "turn":
                                turn(bb, tt)
                            else:
                                weigh(bb, r ^ back, tt)
                        if t == 3 and not first:
                            turn_rows(b - 1)

                pe.wait_ge(c_ready, 2)
                batch(0, 0, True)
                batch(1, 1, False)
                with pe.Fori(1, B // 2) as c:
                    for r in range(2):
                        batch(2 * c + r, r, False)
                turn(B - 1, 2)
                weigh(B - 1, 1, 1)
                turn(B - 1, 3)
                weigh(B - 1, 1, 2)
                weigh(B - 1, 1, 3)
                turn_rows(B - 1)

            @block.scalar
            def _(act):
                with act.Fori(0, B // 2) as c:
                    for r in range(2):
                        b = 2 * c + r
                        for t in range(T):
                            act.wait_ge(maxed, T * b + t + 1)
                            act.wait_ge(turned, 1 + T * b + t)
                            if t == 0:
                                act.wait_ge(normed, 1 + b)
                            for j in range(4):
                                ins = act.activation(probs[t % 2][:, j, :], sc[t % 2][0:S, j * S:j * S + S], ACT.Exp,
                                                     bias=neg_max[t % 2][:, j:j + 1], accum_out=den[r][:, 4 * t + j:4 * t + j + 1])
                            ins.then_inc(exped, 1)
                            if t == 1:
                                act.wait_ge(v_turned, FREE + b + 1)
                                act.activation(v[r][:, :], vb[0:S, 0:H], ACT.Copy).then_inc(v_ready, 1)

            @block.vector
            def _(dve):
                def row_max(b, t):
                    dve.wait_ge(scored, TWO + T * b + t + 1)
                    dve.wait_ge(exped, 1 + T * b + t)
                    dve.tensor_reduce(neg_max[t % 2][:, :], sc[t % 2][0:S, 0:4 * S].rearrange("p (j k) -> p j k", j=4), AX_X, ALU.max,
                                      negate=True).then_inc(maxed, 1)

                def copy_turned(b, t):
                    dve.wait_ge(turned, TWO + T * b + t + 1)
                    dve.wait_ge(weighted, 1 + T * b + t)
                    dve.tensor_copy(probs_t[t % 2][:, :], pt[t % 2][0:S, 0:4 * S]).then_inc(copied, 1)

                def normalise(b, r):
                    dve.wait_ge(weighted, TWO + T * (b + 1))
                    dve.wait_ge(rows_turned, FREE + b)
                    dve.reciprocal(rden[r][:, :], den[r][:, :]).then_inc(inverted, 1)
                    dve.wait_ge(inverted, b + 1)
                    dve.tensor_tensor(rows[:, :, :], ob[r][0:S, 0:H].rearrange("p (h e) -> p h e", h=NH),
                                      rden[r][:, :].unsqueeze(2).to_broadcast([S, NH, HD]), ALU.mult).then_inc(normed, 1)

                def store(b):
                    dve.wait_ge(rows_turned, FREE + b + 1)
                    dve.tensor_copy(qkv[:, 0:T, b, :], xb[:, 0:4 * S].rearrange("p (t s) -> p t s", t=T)).then_inc(stored, 1)

                def batch(b, r, first):
                    for t in range(T):
                        row_max(b, t)
                        bb, back, tt = before(b, t, 2)
                        if not first or not back:
                            copy_turned(bb, tt)
                        if t == 2 and not first:
                            normalise(b - 1, 1 - r)
                        if t == 3 and not first:
                            store(b - 1)

                for free in (v_turned, v_ready, stored, rows_turned):
                    dve.sem_inc(free, FREE)
                for free in (scored, exped, turned, copied, weighted, normed):
                    dve.sem_inc(free, TWO)
                dve.wait_ge(c_loaded, 16)
                dve.tensor_copy(causal[:, :], causal_f[:, :]).then_inc(c_ready, 1)
                dve.tensor_copy(ident_b[:, :], ident[0:S, 0:S]).then_inc(c_ready, 1)
                batch(0, 0, True)
                batch(1, 1, False)
                with dve.Fori(1, B // 2) as c:
                    for r in range(2):
                        batch(2 * c + r, r, False)
                copy_turned(B - 1, 2)
                copy_turned(B - 1, 3)
                normalise(B - 1, 1)
                store(B - 1)


def cross_attention(nc, sem, sbuf, d, q_parts, cctx, bank, con, ident):
    MP = M + 1
    TURN, WEIGH = 3, 4
    with ExitStack() as st:
        def many(n, name, shape, dt=F32):
            return [sbuf(st, f"{name}{i}", shape, dt) for i in range(n)]

        w_kv = sbuf(st, "w_kv", [P, 2, 2 * CC])
        w_hi = sbuf(st, "w_hi", [P, 2, 2 * CC], F32R)
        w_lo = sbuf(st, "w_lo", [P, 2, 2 * CC], F32R)
        ctx_raw = sbuf(st, "ctx_raw", [P, 2, MP])
        ctx_hi = sbuf(st, "ctx_hi", [P, 2, MP], F32R)
        ctx_lo = sbuf(st, "ctx_lo", [P, 2, MP], F32R)
        ck_hi, ck_lo = many(2, "ck_hi", [P, 2, MP], F32R), many(2, "ck_lo", [P, 2, MP], F32R)
        cv = many(2, "cv", [MK, MT, CC])
        q = many(4, "q", [P, 2, S], F32R)
        neg_max, probs = many(4, "neg_max", [S, 1]), many(4, "probs", [S, M])
        probs_t = many(2, "probs_t", [MK, MT * S])
        den, rden = many(2, "den", [S, NH]), many(2, "rden", [S, NH])
        rows = sbuf(st, "rows", [S, NH, CHD])
        sc, pt, ob, xb = bank[0:4], bank[4:6], bank[6], bank[7]
        XT = MT * S
        (w_loaded, w_high, w_ready, ctx_loaded, ctx_high, ctx_ready, x_ready, ck_high, x_taken, inverted, normed, rows_turned,
         stored, q_ready, scored, maxed, exped, turned, weighted, passed) = (
            sem(x) for x in ("w_loaded", "w_high", "w_ready", "ctx_loaded", "ctx_high", "ctx_ready", "x_ready", "ck_high",
                             "x_taken", "inverted", "normed", "rows_turned", "stored", "q_ready", "scored", "maxed", "exped", "turned",
                             "weighted", "passed"))
        copied = [sem("copied_even"), sem("copied_odd")]

        def before(h, lag):
            return (h - lag) % NH, int(h < lag)

        with nc.Block() as block:
            @block.sync
            def _(sp):
                sp.dma_start(w_kv[:, :, :], d["w_ckv"]).then_inc(w_loaded, 16)
                with sp.Fori(0, B + 2) as b:
                    sp.wait_ge(ctx_ready, FREE + b)
                    sp.dma_start(ctx_raw[:, :, :], d["ctx_t"][b]).then_inc(ctx_loaded, 16)
                sp.wait_ge(ctx_loaded, 16 * (B + 2))

            @block.gpsimd
            def _(pool):
                def split_context(b):
                    wait_apart(pool, passed, ctx_high, b + 1)
                    pool.tensor_tensor(ctx_lo[:, :, :], ctx_raw[:, :, :], ctx_hi[:, :, :].bitcast(F32), ALU.subtract).then_inc(ctx_ready, 1)

                pool.wait_ge(w_high, 1)
                pool.tensor_tensor(w_lo[:, :, :], w_kv[:, :, :], w_hi[:, :, :].bitcast(F32), ALU.subtract).then_inc(w_ready, 1)
                split_context(0)
                split_context(1)
                with pool.Fori(0, B) as b:
                    for h in range(NH):
                        wait_apart(pool, passed, scored, 1 + NH * b + h)
                        pool.tensor_tensor(q[h % 4][:, :, :], q_parts[:, h // 8, :, b, :].bitcast(F32),
                                           con[:, C_M8 + h % 8:C_M8 + h % 8 + 1].unsqueeze(2).to_broadcast([P, 2, S]),
                                           ALU.mult).then_inc(q_ready, 1)
                    split_context(b + 2)

            @block.tensor
            def _(pe):
                def make_kv(b, r, halves=range(2)):
                    terms = ((w_hi, ctx_hi), (w_lo, ctx_hi), (w_hi, ctx_lo))
                    for kt in halves:
                        if kt == 0:
                            if r == 0:
                                pe.wait_ge(ctx_ready, FREE + b + 1)
                            pe.wait_ge(x_taken, FREE + 5 * b + r)
                        for n, (w, c) in enumerate(terms):
                            start, stop = kt == 0 and n == 0, kt == 1 and n == 2
                            if r < 2:
                                ins = pe.matmul(xb[:, 0:MP], w[:, kt, r * P:r * P + P], c[:, kt, :], start=start, stop=stop)
                            else:
                                m0 = (r - 2) * (MK - 1)
                                ins = pe.matmul(xb[0:MK, 0:CC], c[:, kt, m0:m0 + MK], w[:, kt, CC:2 * CC], start=start, stop=stop)
                        if kt == 1:
                            ins.then_inc(x_ready, 1)

                def score(b, par_b, h):
                    if h == 0:
                        pe.wait_ge(x_taken, FREE + 5 * b + 2)
                    pe.wait_ge(q_ready, NH * b + h + 1)
                    pe.wait_ge(exped, 1 + NH * b + h)
                    for k, (part, c) in enumerate(((0, ck_hi), (1, ck_hi), (0, ck_lo))):
                        ins = pe.matmul(sc[h % 4][0:S, 0:MP], q[h % 4][:, part, :], c[par_b][:, h // 8, :], start=k == 0, stop=k == 2)
                    ins.then_inc(scored, 1)

                def turn(b, h):
                    pe.wait_ge(exped, 4 + NH * b + h + 1)
                    pe.wait_ge(copied[h % 2], FREE + 8 * b + h // 2)
                    if h == 12:
                        pe.wait_ge(stored, FREE + b)
                    for kt in range(MT):
                        m0 = kt * (MK - 1)
                        ins = pe.transpose(pt[h % 2][0:MK, kt * S:kt * S + S], probs[h % 4][:, m0:m0 + MK], ident[0:S, 0:S])
                    ins.then_inc(turned, 1)

                def weigh(b, par_b, h):
                    pe.wait_ge(copied[h % 2], FREE + 8 * b + h // 2 + 1)
                    if h == 0:
                        pe.wait_ge(x_taken, FREE + 5 * b + 5)
                        pe.wait_ge(normed, 1 + b + 1)
                    for kt in range(MT):
                        c0 = h * CHD
                        ins = pe.matmul(ob[0:S, c0:c0 + CHD], probs_t[h % 2][:, kt * S:kt * S + S], cv[par_b][:, kt, h * CHD:h * CHD + CHD],
                                        start=kt == 0, stop=kt == MT - 1)
                    ins.then_inc(weighted, 1)

                def turn_rows(b, rows_after=0):
                    pe.wait_ge(normed, TWO + b + 1)
                    pe.wait_ge(copied[0], FREE + 8 * b + 8 + rows_after)
                    for t in range(2):
                        ins = pe.transpose(pt[0][:, XT + t * S:XT + t * S + S], rows[:, 8 * t:8 * t + 8, :].rearrange("p h e -> p (h e)"),
                                           ident[0:S, 0:S])
                    ins.then_inc(rows_turned, 1)

                def batch(b, par_b, first):
                    for h in range(NH):
                        score(b, par_b, h)
                        if h == 13 and not first:
                            turn_rows(b - 1, 5)
                        hh, back = before(h, TURN)
                        if not (first and back):
                            turn(b - back, hh)
                        hh, back = before(h, WEIGH)
                        if not (first and back):
                            weigh(b - back, par_b ^ back, hh)
                        if 2 <= h < 12:
                            make_kv(b + 1, (h - 2) // 2, (h % 2,))

                pe.wait_ge(w_ready, 1)
                for r in range(5):
                    make_kv(0, r)
                batch(0, 0, True)
                batch(1, 1, False)
                with pe.Fori(1, B // 2) as c:
                    for par_b in range(2):
                        batch(2 * c + par_b, par_b, False)
                for h in range(NH, NH + WEIGH):
                    if h - TURN < NH:
                        turn(B - 1, h - TURN)
                    weigh(B - 1, 1, h - WEIGH)
                turn_rows(B - 1)

            @block.scalar
            def _(act):
                def split_context(b):
                    act.wait_ge(ctx_loaded, 16 * (b + 1))
                    if not isinstance(b, int) or b > 0:
                        act.wait_ge(x_ready, 5 * b)
                        act.wait_ge(ctx_ready, FREE + b)
                    act.activation(ctx_hi[:, :, :], ctx_raw[:, :, :], ACT.Copy).then_inc(ctx_high, 1)

                def take_keys(b, par_b, r):
                    act.wait_ge(x_ready, 5 * b + r + 1)
                    act.activation(ck_hi[par_b][:, r, :], xb[:, 0:MP], ACT.Copy).then_inc(ck_high, 1)

                def copy_turned(b, h):
                    act.wait_ge(turned, 4 + NH * b + h + 1)
                    act.wait_ge(weighted, 1 + NH * b + h)
                    act.activation(probs_t[1][:, :], pt[1][0:MK, 0:MT * S], ACT.Copy).then_inc(copied[1], 1)

                def exp(b, par_b, h):
                    act.wait_ge(maxed, NH * b + h + 1)
                    act.wait_ge(turned, 1 + NH * b + h)
                    if h == 0:
                        act.wait_ge(normed, 1 + b)
                    act.activation(probs[h % 4][:, :], sc[h % 4][0:S, 0:M], ACT.Exp, bias=neg_max[h % 4][:, :],
                                   accum_out=den[par_b][:, h:h + 1]).then_inc(exped, 1)

                def batch(b, par_b, first):
                    for h in range(NH):
                        hh, back = before(h, TURN)
                        if hh % 2 and not (first and back):
                            copy_turned(b - back, hh)
                        exp(b, par_b, h)
                        if h in (3, 5):
                            take_keys(b + 1, 1 - par_b, (h - 3) // 2)
                        if h == 12:
                            split_context(b + 2)

                act.wait_ge(w_loaded, 16)
                act.activation(w_hi[:, :, :], w_kv[:, :, :], ACT.Copy).then_inc(w_high, 1)
                split_context(0)
                for r in range(2):
                    take_keys(0, 0, r)
                split_context(1)
                batch(0, 0, True)
                batch(1, 1, False)
                with act.Fori(1, B // 2) as c:
                    for par_b in range(2):
                        batch(2 * c + par_b, par_b, False)
                for h in range(NH - TURN, NH):
                    if h % 2:
                        copy_turned(B - 1, h)

            @block.vector
            def _(dve):
                def take_kv(b, par_b, r):
                    dve.wait_ge(x_ready, 5 * b + r + 1)
                    if r < 2:
                        dve.wait_ge(ck_high, 2 * b + r + 1)
                        ins = dve.tensor_tensor(ck_lo[par_b][:, r, :], xb[:, 0:MP], ck_hi[par_b][:, r, :].bitcast(F32), ALU.subtract)
                    else:
                        ins = dve.tensor_scalar(cv[par_b][:, r - 2, :], xb[0:MK, 0:CC], con[0:MK, C_ROW + r - 2:C_ROW + r - 1], None, ALU.mult)
                    ins.then_inc(x_taken, 1)

                def row_max(b, h):
                    dve.wait_ge(scored, 4 + NH * b + h + 1)
                    dve.wait_ge(exped, 1 + NH * b + h)
                    dve.tensor_reduce(neg_max[h % 4][:, :], sc[h % 4][0:S, 0:M], AX_X, ALU.max, negate=True).then_inc(maxed, 1)

                def copy_turned(b, h):
                    dve.wait_ge(turned, 4 + NH * b + h + 1)
                    dve.wait_ge(weighted, 1 + NH * b + h)
                    dve.tensor_copy(probs_t[0][:, :], pt[0][0:MK, 0:MT * S]).then_inc(copied[0], 1)

                def normalise(b, par_b):
                    dve.wait_ge(weighted, 2 + NH * (b + 1))
                    dve.wait_ge(rows_turned, FREE + b)
                    dve.reciprocal(rden[par_b][:, :], den[par_b][:, :]).then_inc(inverted, 1)
                    dve.wait_ge(inverted, b + 1)
                    dve.tensor_tensor(rows[:, :, :], ob[0:S, 0:CC].rearrange("p (h e) -> p h e", h=NH),
                                      rden[par_b][:, :].unsqueeze(2).to_broadcast([S, NH, CHD]), ALU.mult).then_inc(normed, 1)

                def store(b):
                    dve.wait_ge(rows_turned, FREE + b + 1)
                    dve.tensor_copy(cctx[:, :, b, :], pt[0][:, XT:XT + 2 * S].rearrange("p (t s) -> p t s", t=2)).then_inc(stored, 1)

                def batch(b, par_b, first):
                    for h in range(NH):
                        row_max(b, h)
                        hh, back = before(h, TURN)
                        if hh % 2 == 0 and not (first and back):
                            copy_turned(b - back, hh)
                        if h == 3 and not first:
                            normalise(b - 1, 1 - par_b)
                        if h in (3, 5, 7, 9, 11):
                            take_kv(b + 1, 1 - par_b, (h - 3) // 2)
                        if h == 13 and not first:
                            store(b - 1)

                for free in (ctx_ready, x_taken, stored, rows_turned, *copied):
                    dve.sem_inc(free, FREE)
                for free in (normed, weighted):
                    dve.sem_inc(free, TWO)
                for free in (scored, exped, turned):
                    dve.sem_inc(free, 4)
                for r in range(5):
                    take_kv(0, 0, r)
                batch(0, 0, True)
                batch(1, 1, False)
                with dve.Fori(1, B // 2) as c:
                    for par_b in range(2):
                        batch(2 * c + par_b, par_b, False)
                for h in range(NH - TURN, NH):
                    if h % 2 == 0:
                        copy_turned(B - 1, h)
                normalise(B - 1, 1)
                store(B - 1)


def memory_attention(nc, sem, sbuf, d, g_parts, am, bank, con, ident):
    MP = M + 1
    with ExitStack() as st:
        def two(name, shape, dt=F32):
            return [sbuf(st, f"{name}{i}", shape, dt) for i in range(2)]

        raw, hi, lo = two("raw", [P, 2, MP]), two("hi", [P, 2, MP], F32R), two("lo", [P, 2, MP], F32R)
        mem = two("mem", [MK, MT, CC])
        g = two("g", [P, 2, 2, S], F32R)
        neg_max, probs, probs_t = two("neg_max", [S, 1]), two("probs", [S, M]), two("probs_t", [MK, MT * S])
        den, rden, rows = two("den", [S, 1]), two("rden", [S, 1]), two("rows", [S, CC])
        sc, pt, ob, xb = bank[0:2], bank[2:4], bank[4:6], bank[6]
        loaded, mem_loaded = [sem("loaded"), sem("loaded")], [sem("mem_loaded"), sem("mem_loaded")]
        high, low, g_ready, scored, maxed, exped, turned, copied, weighted, inverted, normed, rows_turned, stored, passed = (
            sem(x) for x in ("high", "low", "g_ready", "scored", "maxed", "exped", "turned", "copied", "weighted", "inverted", "normed",
                             "rows_turned", "stored", "passed"))
        with nc.Block() as block:
            @block.sync
            def _(sp):
                def load_raw(c, r):
                    sp.wait_ge(low, 1 + 2 * c + r)
                    sp.dma_start(raw[r][:, :, :], d["ctx_t"][2 * c + r]).then_inc(loaded[r], 16)

                def load_mem(c, r):
                    sp.wait_ge(weighted, 1 + 2 * c + r)
                    sp.dma_start(mem[r][:, :, :], d["ctx_rows"][2 * c + r]).then_inc(mem_loaded[r], 16)

                last = B // 2 - 1
                load_raw(0, 0)
                with sp.Fori(0, last) as c:
                    load_raw(c, 1)
                    load_mem(c, 0)
                    load_raw(c + 1, 0)
                    load_mem(c, 1)
                load_raw(last, 1)
                load_mem(last, 0)
                load_mem(last, 1)

            @block.gpsimd
            def _(pool):
                with pool.Fori(0, B // 2) as c:
                    for r in range(2):
                        wait_apart(pool, passed, high, 2 * c + r + 1)
                        pool.tensor_tensor(lo[r][:, :, :], raw[r][:, :, :], hi[r][:, :, :].bitcast(F32), ALU.subtract).then_inc(low, 1)

            @block.scalar
            def _(act):
                def split(c, r):
                    act.wait_ge(loaded[r], 16 * (c + 1))
                    act.wait_ge(scored, 1 + 2 * c + r)
                    act.activation(hi[r][:, :, :], raw[r][:, :, :], ACT.Copy).then_inc(high, 1)

                def exp(c, r):
                    b = 2 * c + r
                    act.wait_ge(maxed, b + 1)
                    act.wait_ge(turned, 1 + b)
                    act.wait_ge(normed, 1 + b)
                    act.activation(probs[r][:, :], sc[r][0:S, 0:M], ACT.Exp, bias=neg_max[r][:, :], accum_out=den[r][:, :]).then_inc(exped, 1)

                last = B // 2 - 1
                split(0, 0)
                split(0, 1)
                with act.Fori(0, last) as c:
                    for r in range(2):
                        exp(c, r)
                        split(c + 1, r)
                exp(last, 0)
                exp(last, 1)

            @block.tensor
            def _(pe):
                def score(c, r):
                    b = 2 * c + r
                    pe.wait_ge(low, TWO + b + 1)
                    pe.wait_ge(g_ready, b + 1)
                    pe.wait_ge(exped, 1 + b)
                    for kt in range(2):
                        for n, (part, m) in enumerate(((0, hi), (1, hi), (0, lo))):
                            ins = pe.matmul(sc[r][0:S, 0:MP], g[r][:, kt, part, :], m[r][:, kt, :], start=kt == 0 and n == 0, stop=kt == 1 and n == 2)
                    ins.then_inc(scored, 1)

                def turn(c, r):
                    pe.wait_ge(exped, TWO + 2 * c + r + 1)
                    pe.wait_ge(copied, 1 + 2 * c + r)
                    for kt in range(MT):
                        ins = pe.transpose(pt[r][0:MK, kt * S:kt * S + S], probs[r][:, kt * (MK - 1):kt * (MK - 1) + MK], ident[0:S, 0:S])
                    ins.then_inc(turned, 1)

                def weigh(c, r):
                    pe.wait_ge(copied, TWO + 2 * c + r + 1)
                    pe.wait_ge(mem_loaded[r], 16 * (c + 1))
                    pe.wait_ge(normed, 1 + 2 * c + r)
                    for kt in range(MT):
                        ins = pe.matmul(ob[r][0:S, 0:CC], probs_t[r][:, kt * S:kt * S + S], mem[r][:, kt, :], start=kt == 0, stop=kt == MT - 1)
                    ins.then_inc(weighted, 1)

                def turn_rows(c, r):
                    pe.wait_ge(normed, TWO + 2 * c + r + 1)
                    pe.wait_ge(stored, FREE + 2 * c + r)
                    for t in range(2):
                        ins = pe.transpose(xb[:, t * S:t * S + S], rows[r][:, t * P:t * P + P], ident[0:S, 0:S])
                    ins.then_inc(rows_turned, 1)

                last = B // 2 - 1
                score(0, 0)
                score(0, 1)
                turn(0, 0)
                with pe.Fori(1, B // 2) as c:
                    score(c, 0)
                    weigh(c - 1, 0)
                    turn(c - 1, 1)
                    score(c, 1)
                    turn_rows(c - 1, 0)
                    weigh(c - 1, 1)
                    turn(c, 0)
                    turn_rows(c - 1, 1)
                weigh(last, 0)
                turn(last, 1)
                turn_rows(last, 0)
                weigh(last, 1)
                turn_rows(last, 1)

            @block.vector
            def _(dve):
                def fetch(c, r):
                    dve.wait_ge(scored, 1 + 2 * c + r)
                    dve.tensor_copy(g[r][:, :, :, :], g_parts[:, :, :, 2 * c + r, :]).then_inc(g_ready, 1)

                def row_max(c, r):
                    dve.wait_ge(scored, TWO + 2 * c + r + 1)
                    dve.wait_ge(exped, 1 + 2 * c + r)
                    dve.tensor_reduce(neg_max[r][:, :], sc[r][0:S, 0:M], AX_X, ALU.max, negate=True).then_inc(maxed, 1)

                def copy_turned(c, r):
                    dve.wait_ge(turned, TWO + 2 * c + r + 1)
                    dve.wait_ge(weighted, 1 + 2 * c + r)
                    dve.tensor_copy(probs_t[r][:, :], pt[r][0:MK, 0:MT * S]).then_inc(copied, 1)

                def normalise(c, r):
                    b = 2 * c + r
                    dve.wait_ge(weighted, TWO + b + 1)
                    dve.reciprocal(rden[r][:, :], den[r][:, :]).then_inc(inverted, 1)
                    dve.wait_ge(inverted, b + 1)
                    dve.wait_ge(rows_turned, 1 + b)
                    dve.tensor_scalar(rows[r][:, :], ob[r][0:S, 0:CC], rden[r][:, :], None, ALU.mult).then_inc(normed, 1)

                def store(c, r):
                    dve.wait_ge(rows_turned, TWO + 2 * c + r + 1)
                    dve.tensor_copy(am[:, :, 2 * c + r, :], xb[:, 0:2 * S].rearrange("p (t s) -> p t s", t=2)).then_inc(stored, 1)

                dve.sem_inc(stored, FREE)
                for free in (low, scored, exped, turned, copied, weighted, normed, rows_turned):
                    dve.sem_inc(free, TWO)
                last = B // 2 - 1
                fetch(0, 0)
                fetch(0, 1)
                row_max(0, 0)
                row_max(0, 1)
                copy_turned(0, 0)
                with dve.Fori(1, B // 2) as c:
                    fetch(c, 0)
                    row_max(c, 0)
                    normalise(c - 1, 0)
                    copy_turned(c - 1, 1)
                    fetch(c, 1)
                    row_max(c, 1)
                    store(c - 1, 0)
                    normalise(c - 1, 1)
                    copy_turned(c, 0)
                    store(c - 1, 1)
                normalise(last, 0)
                copy_turned(last, 1)
                store(last, 0)
                normalise(last, 1)
                store(last, 1)


def fusion(nc, sem, end_stage, sbuf, d, linear, splitter, store_split, pair_of_splits, bank, hT, con, wcol, ident, ones, out):
    with ExitStack() as st:
        mc = sbuf(st, "mc", [P, KT, N])
        with ExitStack() as s1:
            g_parts = sbuf(s1, "g_parts", [P, 2, 2, B, S], F32R)
            am = sbuf(s1, "am", [P, 2, B, S])
            with ExitStack() as s2:
                x = pair_of_splits(s2, "x", KT, NG)
                linear("mem_query", d["w_mem"], 1, KT, 1, (x,), store_split(g_parts, 0, 1.0 / float(np.sqrt(H))),
                       splitter(hT, (x,), KT, 0, masked=False, groups=NG), groups=NG)
            memory_attention(nc, sem, sbuf, d, g_parts, am, bank, con, ident)
            end_stage()

            def store_context(env):
                def emit(mine, copy):
                    def f(eng, p, s, g):
                        if s != mine:
                            return
                        i = env["groups"] * s + g
                        eng.wait_ge(env["ready"][i], p + 1)
                        copy(eng, mc[:, 2 * p + s, g * G:g * G + G], bank[i][:, 0:G]).then_inc(env["taken"][i], 1)
                    return f
                return dict(act=emit(0, lambda e, o, i: e.activation(o, i, ACT.Copy)), dve=emit(1, lambda e, o, i: e.tensor_copy(o, i)))

            with ExitStack() as s2:
                x = pair_of_splits(s2, "x", 2, NG)
                linear("mem_out", d["w_mem_t"], 2, 2, 1, (x,), store_context,
                       splitter(am, (x,), 2, 0, batch_major=True, masked=False, groups=NG), groups=NG)

        def gate_and_fuse(first):
            def epilogue(env):
                gate = [sbuf(env["st"], f"gate{i}", [P, G]) for i in range(4)]
                gated, fused = [sem("gated") for _ in range(4)], [sem("fused") for _ in range(4)]
                env["open"] = fused

                def act(eng, p, s, g):
                    i = 2 * s + g
                    eng.wait_ge(env["ready"][i], p + 1)
                    eng.wait_ge(fused[i], FREE + p)
                    eng.activation(gate[i][:, :], bank[i][:, 0:G], ACT.Sigmoid, bias=bias[:, 2 * p + s]).then_inc(env["taken"][i], 1)

                def dve(eng, p, s, g):
                    i = 2 * s + g
                    cols = slice(first + g * G, first + g * G + G)
                    eng.wait_ge(env["taken"][i], FREE + p + 1)
                    eng.tensor_tensor(gate[i][:, :], gate[i][:, :], mc[:, 2 * p + s, cols], ALU.mult).then_inc(gated[i], 1)
                    eng.wait_ge(gated[i], p + 1)
                    h = hT[:, 2 * p + s, cols]
                    eng.tensor_tensor(h, h, gate[i][:, :], ALU.add).then_inc(fused[i], 1)

                bias = wcol[:, W_BIAS:W_BIAS + KT].rearrange("p (k o) -> p k o", o=1)
                return dict(act=act, dve=dve)
            return epilogue

        for half in range(2):
            with ExitStack() as s2:
                x = pair_of_splits(s2, "x", 2 * KT)
                linear("gate", d["w_gate"], 2, 2 * KT, 1, (x,), gate_and_fuse(half * 2 * G),
                       splitter(hT, (x,), 2 * KT, half * 2 * G, masked=False, more=mc))

    with ExitStack() as st:
        sq = [sbuf(st, f"sq{i}", [P, G]) for i in range(2)]
        rms = [sbuf(st, f"rms{i}", [P, G]) for i in range(2)]
        y = sbuf(st, "y", [P, KT, N])
        squared, summed, root, inverse, scaled, stored = (sem(x) for x in ("squared", "summed", "root", "inverse", "scaled", "stored"))
        with nc.Block() as block:
            @block.scalar
            def _(act):
                for g in range(NG):
                    for kt in range(KT):
                        n = g * KT + kt
                        if n >= 2:
                            act.wait_ge(summed, n - 1)
                        act.activation(sq[kt % 2][:, :], hT[:, kt, g * G:g * G + G], ACT.Square).then_inc(squared, 1)
                    act.wait_ge(summed, (g + 1) * KT)
                    if g >= 2:
                        act.wait_ge(scaled, (g - 1) * KT)
                    act.activation(rms[g % 2][:, :], bank[g % 2][:, 0:G], ACT.Sqrt, bias=con[:, C_EPS:C_EPS + 1], scale=1.0 / H).then_inc(root, 1)

            @block.tensor
            def _(pe):
                for g in range(NG):
                    if g >= 2:
                        pe.wait_ge(root, g - 1)
                    for kt in range(KT):
                        pe.wait_ge(squared, g * KT + kt + 1)
                        pe.matmul(bank[g % 2][:, 0:G], ones, sq[kt % 2][:, :], start=kt == 0, stop=kt == KT - 1).then_inc(summed, 1)

            @block.vector
            def _(dve):
                for g in range(NG):
                    dve.wait_ge(root, g + 1)
                    dve.reciprocal(rms[g % 2][:, :], rms[g % 2][:, :]).then_inc(inverse, 1)
                    dve.wait_ge(inverse, g + 1)
                    for kt in range(KT):
                        dve.scalar_tensor_tensor(out=y[:, kt, g * G:g * G + G], in0=hT[:, kt, g * G:g * G + G],
                                                 scalar=wcol[:, W_OUT + kt:W_OUT + kt + 1], in1=rms[g % 2][:, :],
                                                 op0=ALU.mult, op1=ALU.mult).then_inc(scaled, 1)

            @block.sync
            def _(sp):
                for g in range(NG):
                    sp.wait_ge(scaled, (g + 1) * KT)
                    sp.dma_start(out[:, :, g * G:g * G + G], y[:, :, g * G:g * G + G]).then_inc(stored, 16)
                sp.wait_ge(stored, 16 * NG)


def kernel(**inputs):
    import concourse.bacc as _bacc
    from concourse.bass_utils import run_bass_kernel_spmd as _run

    a = {k: np.ascontiguousarray(v) for k, v in inputs.items()}

    def tiles(w):
        k, m = w.shape
        return w.reshape(k // P, P, m // P, P).transpose(2, 1, 0, 3)

    def experts(v, l):
        return np.stack([tiles(l), tiles(v)], axis=2)

    def padded(w, axis):
        pad = [(0, 0), (0, 0)]
        pad[axis] = (0, IT * P - w.shape[axis])
        return np.pad(w, pad)

    L0, L1 = "L0_xattn_", "L1_xattn_"
    ctx = a["ctx_1024"]
    ctx_t = np.pad(ctx.reshape(B, M, 2, P).transpose(0, 3, 2, 1), ((0, 2), (0, 0), (0, 0), (0, 1)))
    rows = np.zeros((B, MK, MT, CC), ctx.dtype)
    for kt in range(MT):
        lo = 0 if kt == 0 else 1
        rows[:, lo:, kt] = ctx[:, kt * (MK - 1) + lo:kt * (MK - 1) + MK]
    gu = np.stack([experts(padded(a[L0 + "v_" + n], 1), padded(a[L0 + "l_" + n], 1)) for n in ("gate", "up")], axis=1)
    down = np.stack([tiles(padded(a[L0 + n + "_down"], 0)) for n in ("l", "v")], axis=1)
    ckv = a[L0 + "ckv_w"]
    con, causal = shape_constants()
    vec = [a[L0 + "ln_in_w"], a[L0 + "ln_post_cross_w"], a[L0 + "ln_post_attn_w"], a[L1 + "norm_w"], a[L1 + "b_gate"]]
    arrays = {
        "x": a["x"].transpose(2, 1, 0).reshape(KT, P, N).transpose(1, 0, 2),
        "tok": a["mask_BxS_ik0"].T.reshape(N),
        "pos": a["pos_1xS"].reshape(S),
        "con": con,
        "causal": causal,
        "wcol": np.concatenate([v.reshape(KT, P).T for v in vec], axis=1),
        "w_qkv": experts(a[L0 + "v_qkv"], a[L0 + "l_qkv"]).reshape(12, P, -1),
        "w_dense": experts(a[L0 + "v_dense"], a[L0 + "l_dense"]).reshape(4, P, -1),
        "w_cq": tiles(a[L0 + "cq_w"]).reshape(2, P, -1),
        "w_ckv": ckv.reshape(2, P, 2 * CC).transpose(1, 0, 2),
        "w_cd": tiles(a[L0 + "cdense_w"]).reshape(4, P, -1),
        "w_gu": gu.reshape(2 * IT, P, -1),
        "w_down": down.reshape(8, P, -1),
        "w_mem": tiles(a[L1 + "W_mem"]).reshape(2, P, -1),
        "w_mem_t": tiles(np.ascontiguousarray(a[L1 + "W_mem"].T)).reshape(4, P, -1),
        "w_gate": tiles(np.ascontiguousarray(a[L1 + "W_gate"].T)).reshape(4, P, -1),
        "ctx_t": ctx_t,
        "ctx_rows": rows,
    }
    arrays = {f"in_{k}": np.ascontiguousarray(v) for k, v in arrays.items()}
    nc = _bacc.Bacc("TRN2", target_bir_lowering=False, num_devices=1)
    d = {k[3:]: nc.dram_tensor(k, v.shape, mybir.dt.from_np(v.dtype), kind="ExternalInput").ap() for k, v in arrays.items()}
    out = nc.dram_tensor("out_0", (P, KT, N), F32, kind="ExternalOutput").ap()
    build(nc, d, out)
    got = _run(nc, [arrays], core_ids=[0]).results[0]["out_0"]
    return np.ascontiguousarray(got.transpose(1, 0, 2).reshape(H, S, B).transpose(2, 1, 0))
```
